# Optimizing a Trainium2 kernel written in Bass

```python
import numpy as np
import jax
import jax.numpy as jnp

def _softmax(x, axis=-1):
    return jax.nn.softmax(x, axis=axis)

def _gelu(x):
    return jax.nn.gelu(x, approximate=True)

def _silu(x):
    return jax.nn.silu(x)

def _sigmoid(x):
    return jax.nn.sigmoid(x)

def _layernorm(x, axis=-1, eps=1e-05):
    m = jnp.mean(x, axis=axis, keepdims=True)
    v = jnp.var(x, axis=axis, keepdims=True)
    return (x - m) / jnp.sqrt(v + eps)

def _scatter_add(tgt, idx, src, axis=0):
    return tgt.at[idx].add(src)

def _segment_sum(src, seg, n):
    return jax.ops.segment_sum(src, seg, n)
kernel_name = 'mk_gnn_ffn_d2_gnn_r8_9b8a14'

def setup_inputs(seed: int=0):
    np.random.seed(seed)
    _w = jnp.asarray

    def _rec_inputs():
        import jax
        import jax.numpy as jnp
        _gk = jax.random.key(seed)
        x = -6.415e-05 + 1 * jax.random.normal(jax.random.fold_in(_gk, 1), (1250, 512), jnp.float32)
        src = jax.random.randint(jax.random.fold_in(_gk, 2), (40000,), 0, 1250, jnp.int32)
        dst = jnp.minimum((1250 * jax.random.uniform(jax.random.fold_in(_gk, 3), (40000,)) ** 2.0).astype(jnp.int32), 9999)
        _o = jnp.argsort(dst, stable=True)
        src = src[_o]
        dst = dst[_o]
        return (x, src, dst)
    x, src, dst = _rec_inputs()

    def _L0_gnn_setup():
        import jax, jax.numpy as jnp
        import numpy as np
        N_NODES = 2500
        N_EDGES = 40000
        D = 512
        L = 3
        key = jax.random.key(seed)
        ks = jax.random.split(key, 6)
        x = jax.random.normal(ks[0], (N_NODES, D), dtype=jnp.float32)
        Ws_self = jax.random.normal(ks[1], (L, D, D), dtype=jnp.float32) * 0.05
        Ws_neigh = jax.random.normal(ks[2], (L, D, D), dtype=jnp.float32) * 0.05
        bs = jax.random.normal(ks[3], (L, D), dtype=jnp.float32) * 0.05
        src = jax.random.randint(ks[4], (N_EDGES,), 0, N_NODES, dtype=jnp.int64)
        dst = jax.random.randint(ks[5], (N_EDGES,), 0, N_NODES, dtype=jnp.int64)
        return {'x': x, 'Ws_self': Ws_self, 'Ws_neigh': Ws_neigh, 'bs': bs, 'src': src, 'dst': dst}
    _L0_gnn_all = _L0_gnn_setup()
    _L0_gnn_in = {k: v for k, v in _L0_gnn_all.items() if k in ('Ws_self', 'Ws_neigh', 'bs')}
    del _L0_gnn_all

    def _L0_ffn_setup():
        import jax, jax.numpy as jnp
        import numpy as np
        D_MODEL = 512
        D_FF = 512
        N_EXPERTS = 16
        TOP_K = 3
        BATCH, SEQ = (1, 256)

        def _swiglu(combined):
            gate, up = jnp.split(combined, 2, axis=-1)
            return jax.nn.silu(gate) * up
        key = jax.random.key(seed)
        ks = jax.random.split(key, 6)
        x = jax.random.normal(ks[0], (BATCH, SEQ, D_MODEL), dtype=jnp.float32)
        gate_w = 0.01 * jax.random.normal(ks[1], (N_EXPERTS, D_MODEL), dtype=jnp.float32)
        expert_bias = jnp.zeros((N_EXPERTS,), dtype=jnp.float32)
        shared_gate_up = 0.02 * jax.random.normal(ks[2], (2 * D_FF, D_MODEL), dtype=jnp.float32)
        shared_down = 0.02 * jax.random.normal(ks[3], (D_MODEL, D_FF), dtype=jnp.float32)
        expert_gate_up = 0.02 * jax.random.normal(ks[4], (N_EXPERTS, 2 * D_FF, D_MODEL), dtype=jnp.float32)
        expert_down = 0.02 * jax.random.normal(ks[5], (N_EXPERTS, D_MODEL, D_FF), dtype=jnp.float32)
        return {'x': x, 'gate_w': gate_w, 'expert_bias': expert_bias, 'shared_gate_up': shared_gate_up, 'shared_down': shared_down, 'expert_gate_up': expert_gate_up, 'expert_down': expert_down}
    _L0_ffn_all = _L0_ffn_setup()
    _L0_ffn_in = {k: v for k, v in _L0_ffn_all.items() if k in ('gate_w', 'expert_bias', 'shared_gate_up', 'shared_down', 'expert_gate_up', 'expert_down')}
    del _L0_ffn_all

    def _L1_gnn_setup():
        import jax, jax.numpy as jnp
        import numpy as np
        B = 32
        MAXN = 256
        HEADS = 8
        DH = 64
        M = 256
        D = 512
        EPS = 1e-05
        KEPS = 1e-06

        def _batchnorm(x, g, b):
            mu = jnp.mean(x, axis=0)
            var = jnp.mean((x - mu) ** 2, axis=0)
            return (x - mu) * jax.lax.rsqrt(var + EPS) * g + b

        def _forward(x, batch, edge_index, norm1_g, norm1_b, norm2_g, norm2_b, W_conv, b_conv, Wq, Wk, Wv, Wo, proj):
            N = x.shape[0]
            E = edge_index.shape[1]
            h = x
            xn = _batchnorm(x, norm1_g, norm1_b)
            msg = xn[edge_index[0]]
            agg = jax.ops.segment_sum(msg, edge_index[1], num_segments=N)
            deg = jax.ops.segment_sum(jnp.ones((E,), x.dtype), edge_index[1], num_segments=N)
            agg = agg / jnp.maximum(deg, 1.0)[:, None]
            conv_out = jax.nn.relu(agg @ W_conv + b_conv)
            counts = jax.ops.segment_sum(jnp.ones((N,), jnp.int32), batch, num_segments=B)
            offsets = jnp.concatenate([jnp.zeros((1,), jnp.int32), jnp.cumsum(counts)[:-1]])
            pos = jnp.arange(N, dtype=jnp.int32) - offsets[batch]
            h_dense = jnp.zeros((B, MAXN, D), x.dtype).at[batch, pos].set(h)
            mask = jnp.zeros((B, MAXN), bool).at[batch, pos].set(True)

            def heads(t, W):
                return (t @ W).reshape(B, MAXN, HEADS, DH).transpose(0, 2, 1, 3)
            q, k, v = (heads(h_dense, Wq), heads(h_dense, Wk), heads(h_dense, Wv))
            scale = DH ** (-0.25)

            def phi(t, is_query):
                t = t * scale
                u = jnp.einsum('bhnd,md->bhnm', t, proj)
                diag = 0.5 * jnp.sum(t * t, axis=-1, keepdims=True)
                if is_query:
                    m_ = jnp.max(u, axis=-1, keepdims=True)
                else:
                    m_ = jnp.max(u, axis=(-2, -1), keepdims=True)
                return jnp.exp(u - diag - jax.lax.stop_gradient(m_)) / np.sqrt(M) + KEPS
            qf = phi(q, True)
            kf = phi(k, False) * mask[:, None, :, None]
            vm = v * mask[:, None, :, None]
            kv = jnp.einsum('bhnm,bhnd->bhmd', kf, vm)
            z = 1.0 / (jnp.einsum('bhnm,bhm->bhn', qf, kf.sum(axis=2)) + KEPS)
            attn = jnp.einsum('bhnm,bhmd->bhnd', qf, kv) * z[..., None]
            attn = attn.transpose(0, 2, 1, 3).reshape(B, MAXN, D) @ Wo
            h_attn = attn[batch, pos]
            return _batchnorm(conv_out + h_attn + h, norm2_g, norm2_b)
        key = jax.random.key(seed)
        ks = jax.random.split(key, 10)
        sizes = 1024 + np.arange(B) * 131 % 1025
        N = int(sizes.sum())
        E = N * 8
        batch = jnp.asarray(np.repeat(np.arange(B), sizes), dtype=jnp.int32)
        edge_index = jax.random.randint(ks[0], (2, E), 0, N, dtype=jnp.int32)
        s = 1.0 / np.sqrt(D)
        return {'x': jax.random.normal(ks[1], (N, D), jnp.float32), 'batch': batch, 'edge_index': edge_index, 'norm1_g': jnp.ones((D,), jnp.float32), 'norm1_b': jnp.zeros((D,), jnp.float32), 'norm2_g': jnp.ones((D,), jnp.float32), 'norm2_b': jnp.zeros((D,), jnp.float32), 'W_conv': jax.random.normal(ks[2], (D, D), jnp.float32) * s, 'b_conv': jnp.zeros((D,), jnp.float32), 'Wq': jax.random.normal(ks[3], (D, D), jnp.float32) * s, 'Wk': jax.random.normal(ks[4], (D, D), jnp.float32) * s, 'Wv': jax.random.normal(ks[5], (D, D), jnp.float32) * s, 'Wo': jax.random.normal(ks[6], (D, D), jnp.float32) * s, 'proj': jax.random.normal(ks[7], (M, DH), jnp.float32)}
    _L1_gnn_all = _L1_gnn_setup()
    _L1_gnn_in = {k: v for k, v in _L1_gnn_all.items() if k in ('norm1_g', 'norm1_b', 'norm2_g', 'norm2_b', 'W_conv', 'b_conv', 'Wq', 'Wk', 'Wv', 'Wo', 'proj')}
    del _L1_gnn_all

    def _L1_ffn_setup():
        import jax, jax.numpy as jnp
        import numpy as np
        K_INPUT, K_PROCESS, K_OUTPUT = (256, 128, 256)

        def _gelu(x):
            return jax.nn.gelu(x, approximate=False)
        key = jax.random.key(seed)
        ks = jax.random.split(key, 6)
        d_model, n_in, n_proc, n_out, d_pv = (512, 256, 1024, 256, 256)
        B, S = (2, 1024)

        def xavier(k, shape):
            std = (2.0 / (shape[0] + shape[1])) ** 0.5
            return jax.random.normal(k, shape, dtype=jnp.float32) * std
        return {'x': jax.random.normal(ks[0], (B, S, d_model), dtype=jnp.float32), 'input_patterns': xavier(ks[1], (n_in, d_model)), 'process_input_weights': xavier(ks[2], (n_proc, n_in)), 'process_values': xavier(ks[3], (n_proc, d_pv)), 'output_input_weights': xavier(ks[4], (n_out, d_pv)), 'output_patterns': xavier(ks[5], (n_out, d_model))}
    _L1_ffn_all = _L1_ffn_setup()
    _L1_ffn_in = {k: v for k, v in _L1_ffn_all.items() if k in ('input_patterns', 'process_input_weights', 'process_values', 'output_input_weights', 'output_patterns')}
    del _L1_ffn_all
    return {'x': x, 'src': src, 'dst': dst, 'L0_gnn_Ws_self': _L0_gnn_in['Ws_self'], 'L0_gnn_Ws_neigh': _L0_gnn_in['Ws_neigh'], 'L0_gnn_bs': _L0_gnn_in['bs'], 'L0_ffn_gate_w': _L0_ffn_in['gate_w'], 'L0_ffn_expert_bias': _L0_ffn_in['expert_bias'], 'L0_ffn_shared_gate_up': _L0_ffn_in['shared_gate_up'], 'L0_ffn_shared_down': _L0_ffn_in['shared_down'], 'L0_ffn_expert_gate_up': _L0_ffn_in['expert_gate_up'], 'L0_ffn_expert_down': _L0_ffn_in['expert_down'], 'L1_gnn_norm1_g': _L1_gnn_in['norm1_g'], 'L1_gnn_norm1_b': _L1_gnn_in['norm1_b'], 'L1_gnn_norm2_g': _L1_gnn_in['norm2_g'], 'L1_gnn_norm2_b': _L1_gnn_in['norm2_b'], 'L1_gnn_W_conv': _L1_gnn_in['W_conv'], 'L1_gnn_b_conv': _L1_gnn_in['b_conv'], 'L1_gnn_Wq': _L1_gnn_in['Wq'], 'L1_gnn_Wk': _L1_gnn_in['Wk'], 'L1_gnn_Wv': _L1_gnn_in['Wv'], 'L1_gnn_Wo': _L1_gnn_in['Wo'], 'L1_gnn_proj': _L1_gnn_in['proj'], 'L1_ffn_input_patterns': _L1_ffn_in['input_patterns'], 'L1_ffn_process_input_weights': _L1_ffn_in['process_input_weights'], 'L1_ffn_process_values': _L1_ffn_in['process_values'], 'L1_ffn_output_input_weights': _L1_ffn_in['output_input_weights'], 'L1_ffn_output_patterns': _L1_ffn_in['output_patterns']}

def reference(x, src, dst, L0_gnn_Ws_self, L0_gnn_Ws_neigh, L0_gnn_bs, L0_ffn_gate_w, L0_ffn_expert_bias, L0_ffn_shared_gate_up, L0_ffn_shared_down, L0_ffn_expert_gate_up, L0_ffn_expert_down, L1_gnn_norm1_g, L1_gnn_norm1_b, L1_gnn_norm2_g, L1_gnn_norm2_b, L1_gnn_W_conv, L1_gnn_b_conv, L1_gnn_Wq, L1_gnn_Wk, L1_gnn_Wv, L1_gnn_Wo, L1_gnn_proj, L1_ffn_input_patterns, L1_ffn_process_input_weights, L1_ffn_process_values, L1_ffn_output_input_weights, L1_ffn_output_patterns):
    import jax
    import jax.numpy as jnp

    def _L0_gnn_ref(x, Ws_self, Ws_neigh, bs, src, dst):
        import jax, jax.numpy as jnp
        import numpy as np
        N_NODES = 2500
        N_EDGES = 40000
        D = 512
        L = 3
        n = x.shape[0]
        deg = jax.ops.segment_sum(jnp.ones_like(dst, dtype=x.dtype), dst, num_segments=n)
        inv_deg = (1.0 / jnp.clip(deg, 1.0))[:, None]
        h = x
        n_layers = Ws_self.shape[0]
        for l in range(n_layers):
            neigh = jax.ops.segment_sum(h[src], dst, num_segments=n) * inv_deg
            h = h @ Ws_self[l] + neigh @ Ws_neigh[l] + bs[l]
            if l != n_layers - 1:
                h = jax.nn.relu(h)
        return h

    def _L0_ffn_ref(x, gate_w, expert_bias, shared_gate_up, shared_down, expert_gate_up, expert_down):
        import jax, jax.numpy as jnp
        import numpy as np
        D_MODEL = 512
        D_FF = 512
        N_EXPERTS = 16
        TOP_K = 3
        BATCH, SEQ = (1, 256)

        def _swiglu(combined):
            gate, up = jnp.split(combined, 2, axis=-1)
            return jax.nn.silu(gate) * up
        B, S, D = x.shape
        xf = x.reshape(-1, D)
        shared_out = _swiglu(xf @ shared_gate_up.T) @ shared_down.T
        logits = xf @ gate_w.T
        affinity = jax.nn.sigmoid(logits)
        routing_scores = affinity + expert_bias
        _, sel = jax.lax.top_k(routing_scores, TOP_K)
        sel_aff = jnp.take_along_axis(affinity, sel, axis=1)
        gating = sel_aff / (sel_aff.sum(axis=-1, keepdims=True) + 1e-09)
        combined = jnp.einsum('td,efd->tef', xf, expert_gate_up)
        hidden = _swiglu(combined)
        expert_out = jnp.einsum('tef,edf->ted', hidden, expert_down)
        sel_out = jnp.take_along_axis(expert_out, sel[:, :, None], axis=1)
        routed_out = jnp.einsum('tk,tkd->td', gating, sel_out)
        out = shared_out + routed_out
        return out.reshape(B, S, D)

    def _L1_gnn_ref(x, batch, edge_index, norm1_g, norm1_b, norm2_g, norm2_b, W_conv, b_conv, Wq, Wk, Wv, Wo, proj):
        import jax, jax.numpy as jnp
        import numpy as np
        B = 32
        MAXN = 256
        HEADS = 8
        DH = 64
        M = 256
        D = 512
        EPS = 1e-05
        KEPS = 1e-06

        def _batchnorm(x, g, b):
            mu = jnp.mean(x, axis=0)
            var = jnp.mean((x - mu) ** 2, axis=0)
            return (x - mu) * jax.lax.rsqrt(var + EPS) * g + b

        def _forward(x, batch, edge_index, norm1_g, norm1_b, norm2_g, norm2_b, W_conv, b_conv, Wq, Wk, Wv, Wo, proj):
            N = x.shape[0]
            E = edge_index.shape[1]
            h = x
            xn = _batchnorm(x, norm1_g, norm1_b)
            msg = xn[edge_index[0]]
            agg = jax.ops.segment_sum(msg, edge_index[1], num_segments=N)
            deg = jax.ops.segment_sum(jnp.ones((E,), x.dtype), edge_index[1], num_segments=N)
            agg = agg / jnp.maximum(deg, 1.0)[:, None]
            conv_out = jax.nn.relu(agg @ W_conv + b_conv)
            counts = jax.ops.segment_sum(jnp.ones((N,), jnp.int32), batch, num_segments=B)
            offsets = jnp.concatenate([jnp.zeros((1,), jnp.int32), jnp.cumsum(counts)[:-1]])
            pos = jnp.arange(N, dtype=jnp.int32) - offsets[batch]
            h_dense = jnp.zeros((B, MAXN, D), x.dtype).at[batch, pos].set(h)
            mask = jnp.zeros((B, MAXN), bool).at[batch, pos].set(True)

            def heads(t, W):
                return (t @ W).reshape(B, MAXN, HEADS, DH).transpose(0, 2, 1, 3)
            q, k, v = (heads(h_dense, Wq), heads(h_dense, Wk), heads(h_dense, Wv))
            scale = DH ** (-0.25)

            def phi(t, is_query):
                t = t * scale
                u = jnp.einsum('bhnd,md->bhnm', t, proj)
                diag = 0.5 * jnp.sum(t * t, axis=-1, keepdims=True)
                if is_query:
                    m_ = jnp.max(u, axis=-1, keepdims=True)
                else:
                    m_ = jnp.max(u, axis=(-2, -1), keepdims=True)
                return jnp.exp(u - diag - jax.lax.stop_gradient(m_)) / np.sqrt(M) + KEPS
            qf = phi(q, True)
            kf = phi(k, False) * mask[:, None, :, None]
            vm = v * mask[:, None, :, None]
            kv = jnp.einsum('bhnm,bhnd->bhmd', kf, vm)
            z = 1.0 / (jnp.einsum('bhnm,bhm->bhn', qf, kf.sum(axis=2)) + KEPS)
            attn = jnp.einsum('bhnm,bhmd->bhnd', qf, kv) * z[..., None]
            attn = attn.transpose(0, 2, 1, 3).reshape(B, MAXN, D) @ Wo
            h_attn = attn[batch, pos]
            return _batchnorm(conv_out + h_attn + h, norm2_g, norm2_b)
        return _forward(x, batch, edge_index, norm1_g, norm1_b, norm2_g, norm2_b, W_conv, b_conv, Wq, Wk, Wv, Wo, proj)

    def _L1_ffn_ref(x, input_patterns, process_input_weights, process_values, output_input_weights, output_patterns):
        import jax, jax.numpy as jnp
        import numpy as np
        K_INPUT, K_PROCESS, K_OUTPUT = (256, 128, 256)

        def _gelu(x):
            return jax.nn.gelu(x, approximate=False)
        B, S, d_model = x.shape
        n_in = input_patterns.shape[0]
        input_acts = _gelu(jnp.einsum('bsd,nd->bsn', x, input_patterns))
        top_in_acts, top_in_idx = jax.lax.top_k(input_acts, K_INPUT)
        bi = jnp.arange(B)[:, None, None]
        si = jnp.arange(S)[None, :, None]
        input_repr = jnp.zeros((B, S, n_in), dtype=x.dtype).at[bi, si, top_in_idx].set(top_in_acts)
        process_acts = _gelu(jnp.einsum('bsn,pn->bsp', input_repr, process_input_weights))
        top_p_acts, top_p_idx = jax.lax.top_k(process_acts, K_PROCESS)
        sel_values = process_values[top_p_idx]
        p_weights = jax.nn.softmax(top_p_acts, axis=-1)
        agg_value = jnp.einsum('bsk,bskd->bsd', p_weights, sel_values)
        output_acts = _gelu(jnp.einsum('bsd,od->bso', agg_value, output_input_weights))
        top_o_acts, top_o_idx = jax.lax.top_k(output_acts, K_OUTPUT)
        sel_patterns = output_patterns[top_o_idx]
        out = jnp.einsum('bsk,bskm->bsm', top_o_acts, sel_patterns)
        return out
    edge_index = jnp.stack([src, dst])
    batch0 = jnp.zeros((1250,), jnp.int32)
    x = x + _L0_gnn_ref(_layernorm(x, axis=-1), L0_gnn_Ws_self, L0_gnn_Ws_neigh, L0_gnn_bs, src, dst)
    x = x + _L0_ffn_ref(_layernorm(x, axis=-1)[None], L0_ffn_gate_w, L0_ffn_expert_bias, L0_ffn_shared_gate_up, L0_ffn_shared_down, L0_ffn_expert_gate_up, L0_ffn_expert_down)[0]
    x = x + _L1_gnn_ref(_layernorm(x, axis=-1), batch0, edge_index, L1_gnn_norm1_g, L1_gnn_norm1_b, L1_gnn_norm2_g, L1_gnn_norm2_b, L1_gnn_W_conv, L1_gnn_b_conv, L1_gnn_Wq, L1_gnn_Wk, L1_gnn_Wv, L1_gnn_Wo, L1_gnn_proj)
    x = x + _L1_ffn_ref(_layernorm(x, axis=-1)[None], L1_ffn_input_patterns, L1_ffn_process_input_weights, L1_ffn_process_values, L1_ffn_output_input_weights, L1_ffn_output_patterns)[0]
    return x

_drawn_inputs = setup_inputs


def setup_inputs(seed=0):
    import zlib

    import numpy as np

    out = dict(_drawn_inputs(seed))
    spreads = {'L0_ffn_expert_bias': (0.0, 0.311),
     'L1_gnn_norm1_g': (1.0, 0.6),
     'L1_gnn_norm1_b': (0.0, 0.323),
     'L1_gnn_norm2_g': (1.0, 0.2),
     'L1_gnn_norm2_b': (0.0, 0.1),
     'L1_gnn_b_conv': (0.0, 0.372)}
    factors = {'L0_ffn_gate_w': 4.175,
     'L1_gnn_Wk': 5.408,
     'L1_ffn_input_patterns': 8.0,
     'L1_ffn_process_input_weights': 8.0,
     'L1_ffn_process_values': 8.0,
     'L1_ffn_output_input_weights': 8.0,
     'L1_ffn_output_patterns': 8.0}
    for name, (base, spread) in spreads.items():
        noise = np.random.default_rng([zlib.crc32(name.encode()), seed]).standard_normal(out[name].shape)
        drawn = base * np.exp(spread * noise) if base else spread * noise
        out[name] = jnp.asarray(drawn.astype(out[name].dtype))
    for name, factor in factors.items():
        out[name] = (out[name] * factor).astype(out[name].dtype)
    return out
```

```python
from contextlib import ExitStack

import concourse.bass as bass
import concourse.mybir as mybir

F32 = mybir.dt.float32
BF16 = mybir.dt.bfloat16
FP16 = mybir.dt.float16
I32 = mybir.dt.int32
U32 = mybir.dt.uint32
ALU = mybir.AluOpType
ACT = mybir.ActivationFunctionType
AX = mybir.AxisListType

N_TOK, D = 1250, 512
TP = 125
NT = N_TOK // TP
KD = D // 128
TOK_CHUNKS = [(0, 418), (418, 416), (834, 416)]
N_EDGES = 40000
ECH = N_EDGES // TP
EPAIR = ECH // 2
N_GNN = 3
LN_EPS, BN_EPS = 1e-5, 1e-5
N_EXP, TOP_K, D_FF = 16, 3, 512
SLOTS = 128
MIN_BLOCKS = -(-N_TOK * TOP_K // SLOTS)
MAX_BLOCKS = (N_TOK * TOP_K + N_EXP * SLOTS) // SLOTS
HEADS, DH, M_FEAT, N_DENSE = 8, 64, 256, 256
K_EPS = 1e-6
N_IN, N_PROC, D_PV, N_OUT, K_PROC = 256, 1024, 256, 256, 128
REPLACED = -3.0e38


class Lane:

    def __init__(self, sem):
        self.sem, self.steps, self.count, self.seen = sem, [], 0, {}

    def wait(self, *tokens):
        for t in tokens:
            if t is None:
                continue
            if isinstance(t, list):
                self.wait(*t)
                continue
            sem, value = t
            if self.seen.get(id(sem), 0) < value:
                self.seen[id(sem)] = value
                self.steps.append(lambda e, sem=sem, value=value: e.wait_ge(sem, value))

    def do(self, fn, *tokens):
        self.wait(*tokens)
        self.count += 1
        self.steps.append(lambda e: fn(e).then_inc(self.sem, 1))
        return (self.sem, self.count)

    def raw(self, fn, *tokens):
        self.wait(*tokens)
        self.steps.append(fn)

    def run(self, eng):
        for s in self.steps:
            s(eng)


class Landing:

    def __init__(self, sem):
        self.sem, self.total = sem, 0

    def dma(self, lane, out, in_, *tokens):
        lane.wait(*tokens)
        self.total += 16
        lane.steps.append(lambda e: e.dma_start(out, in_).then_inc(self.sem, 16))
        return (self.sem, self.total)


def build(nc, a, upto=9):
    ctx = ExitStack()
    with ctx:
        def sb(name, shape, dt=F32):
            return ctx.enter_context(nc.sbuf_tensor("sb_" + name, shape, dt))[:]

        def sem(name):
            return ctx.enter_context(nc.semaphore(name))

        PE, DVE, SC, POOL = (Lane(sem("done_" + n)) for n in ("pe", "dve", "act", "pool"))
        SP = Lane(sem("done_sp"))

        def landing(name):
            return Landing(sem("ld_" + name))

        x_res = sb("x_res", [TP, NT, D])
        a_reg = sb("a_reg", [128, NT * N_TOK])
        adj = a_reg[0:TP, :].rearrange("p (t n) -> p t n", n=N_TOK)
        htok = sb("htok", [TP, NT, D])
        hT = sb("hT", [128, KD, N_TOK])
        z_reg = sb("z_reg", [128, NT * D])
        z = z_reg[0:TP, :].rearrange("p (t n) -> p t n", n=D)
        w_reg = sb("w_reg", [128, 2, 6 * 1024])
        w_conv = sb("w_conv", [128, KD, D])
        blk = sb("blk", [128, 3584])
        ident = sb("ident", [128, 128])
        inv_deg = sb("inv_deg", [TP, NT])
        deg3 = sb("deg3", [TP, NT, 3])
        stats = sb("stats", [TP, NT, 6])
        mv = sb("mv", [TP, NT, 2])
        rstd = sb("rstd", [TP, NT])
        eps = sb("eps", [128, 1])
        ones_row = sb("ones_row", [1, TP])
        bias_rows = blk[0:1, 0:N_GNN * D].rearrange("p (l d) -> p l d", d=D)
        tmp = blk[0:TP, 1536:2560].rearrange("p (l d) -> p l d", d=D)

        psum = ctx.enter_context(nc.psum_tensor("psum", [128, 8, 512], F32))
        bank_free = [None] * 8
        turn = [0]

        def bank(lo=0, hi=8):
            b = lo + turn[0] % (hi - lo)
            turn[0] += 1
            return b

        def group(out, pairs):
            def fn(e):
                for n, (l, r) in enumerate(pairs):
                    ins = e.matmul(out, l, r, start=(n == 0), stop=(n == len(pairs) - 1))
                return ins
            return fn

        def pipeline(n, *stages):
            for t in range(n + len(stages) - 1):
                for s in reversed(range(len(stages))):
                    if 0 <= t - s < n:
                        stages[s](t - s)

        ld_x = landing("x")
        x_dram = a["x"].rearrange("(t p) d -> p t d", p=TP)
        ld_x.dma(SP, x_res[0:112], x_dram[0:112])
        x_in = ld_x.dma(SP, x_res[112:TP], x_dram[112:TP])

        src_i = z_reg[0:TP, 0:ECH].bitcast(I32)
        dst_i = z_reg[0:TP, ECH:2 * ECH].bitcast(I32)
        src_f = z_reg[0:TP, 2 * ECH:3 * ECH]
        dst_f = z_reg[0:TP, 3 * ECH:4 * ECH]
        o = 4 * ECH
        node_iota = z_reg[0:TP, o:o + N_TOK // 2].bitcast(FP16)
        o += N_TOK // 2
        hot_src = [z_reg[0:TP, o + j * 625:o + (j + 1) * 625].bitcast(BF16) for j in range(2)]
        o += 1250
        hot_dst = [z_reg[0:TP, o + j * 63:o + (j + 1) * 63].bitcast(BF16)[:, 0:TP] for j in range(2)]
        o += 126
        a_row = z_reg[0:TP, o:o + N_TOK]
        o += N_TOK
        assert o <= NT * D
        ld_edges = landing("edges")
        ld_edges.dma(SC, src_i, a["src"])
        edges_in = ld_edges.dma(SC, dst_i, a["dst"])

        ld_w0 = landing("w0")
        w_gnn = w_reg.rearrange("p s n -> p (s n)").rearrange("p (m k n) -> p m k n", m=6, k=KD)
        ld_w0.dma(SP, bias_rows[:], a["L0_gnn_bs"])
        w0_in = ld_w0.dma(SP, w_reg.rearrange("p s n -> p (s n)"), a["w_gnn"])
        ld_wc = landing("wc")
        wc_in = ld_wc.dma(SP, w_conv.rearrange("p k n -> p (k n)"), a["L1_gnn_W_conv"])

        sel = sb("sel", [TP, NT, NT], BF16)
        zeros = sb("zeros", [1, 512], BF16)
        ramps = blk[0:NT, 2560:2880].rearrange("p (a c) -> p a c", a=2)
        t_id0 = POOL.do(lambda e: e.memset(ident, 0.0))
        t_id = POOL.do(lambda e: e.affine_select(out=ident, in_=ident, compare_op=ALU.not_equal, fill=1.0,
                                                 base=0, pattern=[[-1, 128]], channel_multiplier=1), t_id0)
        POOL.do(lambda e: e.iota(node_iota, [[1, N_TOK]], base=0, channel_multiplier=0,
                                 allow_small_or_imprecise_dtypes=True))
        POOL.do(lambda e: e.iota(ramps[:, 0, :], [[1, EPAIR]], base=1, channel_multiplier=0,
                                 allow_small_or_imprecise_dtypes=True))
        t_iota = POOL.do(lambda e: e.iota(ramps[:, 1, :], [[-1, EPAIR]], base=EPAIR, channel_multiplier=0,
                                          allow_small_or_imprecise_dtypes=True))
        t_c0 = DVE.do(lambda e: e.memset(sel, 0.0))
        sel_flat = sel.rearrange("p a b -> p (a b)")
        DVE.do(lambda e: e.memset(sel_flat[:, 0:NT * NT:NT + 1], 1.0), t_c0)
        DVE.do(lambda e: e.memset(sel_flat[:, NT:NT * NT:NT + 1], -1.0))
        DVE.do(lambda e: e.memset(zeros, 0.0))
        DVE.do(lambda e: e.memset(ones_row, 1.0))
        t_const = DVE.do(lambda e: e.memset(eps, LN_EPS))

        DVE.do(lambda e: e.tensor_copy(src_f, src_i), edges_in)
        t_dst = DVE.do(lambda e: e.tensor_copy(dst_f, dst_i))
        ge = htok[:, 0:4, :].rearrange("p a b -> p (a b)").bitcast(BF16)[:, 0:NT * ECH].rearrange(
            "p (b c) -> p b c", c=ECH)
        for b in range(NT):
            t_ge = DVE.do(lambda e, b=b: e.tensor_scalar(ge[:, b, :], dst_f, float(TP * b), None, ALU.is_ge), t_dst)
        t_cnt = PE.do(group(psum[0:NT, 6, 0:ECH], [(sel[:, b, :], ge[:, b, :]) for b in range(NT)]), t_ge, t_const)
        has = blk[0:NT, 2880:3200].rearrange("p (c a) -> p c a", a=2)
        span = blk[0:NT, 3200:3520].rearrange("p (a c) -> p a c", a=2)
        reach = sb("reach", [NT, 2])
        span_i = sb("span_i", [NT, 2], I32)
        t = DVE.do(lambda e: e.tensor_copy(has.rearrange("p c two -> p (c two)"), psum[0:NT, 6, 0:ECH]), t_cnt)
        bank_free[6] = t
        t = DVE.do(lambda e: e.tensor_tensor(has[:, :, 0], has[:, :, 0], has[:, :, 1], ALU.add), t)
        t = DVE.do(lambda e: e.tensor_scalar(has[:, :, 0], has[:, :, 0], 1.0, None, ALU.min), t)
        DVE.do(lambda e: e.tensor_tensor(span[:, 0, :], has[:, :, 0], ramps[:, 0, :], ALU.mult), t, t_iota)
        t = DVE.do(lambda e: e.tensor_tensor(span[:, 1, :], has[:, :, 0], ramps[:, 1, :], ALU.mult))
        t = DVE.do(lambda e: e.tensor_reduce(reach, span, AX.X, ALU.max), t)
        t = DVE.do(lambda e: e.tensor_scalar(span[:, 1, 0:1], reach[:, 1:2], -1.0, float(EPAIR), ALU.mult, ALU.add), t)
        t = DVE.do(lambda e: e.tensor_scalar(span[:, 1, 0:1], span[:, 1, 0:1], float(EPAIR - 1), None, ALU.min), t)
        DVE.do(lambda e: e.tensor_copy(span_i[:, 0:1], span[:, 1, 0:1]), t)
        t = DVE.do(lambda e: e.tensor_tensor(span[:, 0, 0:1], reach[:, 0:1], span[:, 1, 0:1], ALU.subtract), t)
        t_span = DVE.do(lambda e: e.tensor_scalar(span_i[:, 1:2], span[:, 0, 0:1], 1.0, None, ALU.max), t)

        def layer_norm(dst, src, ready):
            for i in range(NT):
                t = DVE.do(lambda e, i=i: e.bn_stats(stats[:, i, :], src[:, i, :]), ready[i])
            for i in range(NT):
                t2 = DVE.do(lambda e, i=i: e.bn_aggr(mv[:, i, :], stats[:, i, :]), t)
            t = SC.do(lambda e: e.activation(rstd, mv[:, :, 1], ACT.Sqrt, bias=eps[0:TP, :]), t2, t_const)
            t = DVE.do(lambda e: e.reciprocal(rstd, rstd), t)
            return [DVE.do(lambda e, i=i: e.tensor_scalar(dst[:, i, :], src[:, i, :], mv[:, i, 0:1],
                                                          rstd[:, i:i + 1], ALU.subtract, ALU.mult), t)
                    for i in range(NT)]

        def to_features(src, ready, free=None, relu=False, banks=(0, 8), engines=None):
            out = []
            for i in range(NT):
                out.append(turn_tile(src, i, ready[i], free, relu, banks))
            return out

        def turn_tile(src, i, ready, free, relu, banks=(0, 8), eng=None):
            b = bank(*banks)

            def fn(e):
                for k in range(KD):
                    ins = e.transpose(psum[:, b, k * TP:(k + 1) * TP], src[:, i, k * 128:(k + 1) * 128],
                                      ident[0:TP, 0:TP])
                return ins
            t = PE.do(fn, ready, bank_free[b], t_id)
            view = psum[:, b, 0:KD * TP].rearrange("p (k n) -> p k n", k=KD)
            dst = hT[:, :, i * TP:(i + 1) * TP]
            if relu:
                t = SC.do(lambda e: e.activation(dst, view, ACT.Relu), t, free)
            else:
                t = SC.do(lambda e: e.copy(dst, view), t, free)
            bank_free[b] = t
            return t

        s_hot, s_used = sem("hot_ready"), sem("hot_used")

        def build_bucket_dve(e, b, state):
            first = e.value_load(span_i[b:b + 1, 0:1], min_val=0, max_val=EPAIR - 1)
            number = e.value_load(span_i[b:b + 1, 1:2], min_val=1, max_val=EPAIR)
            before = state.get("turns", 0)
            with e.Fori(0, number) as i:
                pair = e.bass.s_assert_within(
                    first + i, 0, EPAIR - 1,
                    skip_runtime_bounds_check_because="first + number <= EPAIR by their computation")
                for j in range(2):
                    chunk = pair * 2 + j
                    e.wait_ge(s_used, (before + i) * 2 + (j + 1))
                    e.tensor_scalar(hot_dst[j], node_iota[:, b * TP:(b + 1) * TP],
                                    dst_f[:, bass.ds(chunk, 1)], None, ALU.is_equal)
                    e.tensor_scalar(hot_src[j], node_iota, src_f[:, bass.ds(chunk, 1)], None,
                                    ALU.is_equal).then_inc(s_hot, 1)
            state["turns"] = e.snap(before + number)

        def build_bucket_pe(e, b, state, pb):
            number = e.value_load(span_i[b:b + 1, 1:2], min_val=1, max_val=EPAIR)
            before = state.get("turns", 0)
            if b == 0:
                e.sem_inc(s_used, 2)
            for n, (o, w) in enumerate(TOK_CHUNKS):
                e.matmul(psum[0:TP, pb + n, 0:w], zeros[0:1, 0:TP], zeros[0:1, 0:w], start=True, stop=False,
                         skip_group_check=True)
            with e.Fori(0, number) as i:
                for j in range(2):
                    e.wait_ge(s_hot, (before + i) * 2 + (j + 1))
                    for n, (o, w) in enumerate(TOK_CHUNKS):
                        ins = e.matmul(psum[0:TP, pb + n, 0:w], hot_dst[j], hot_src[j][:, o:o + w],
                                       start=False, stop=False, skip_group_check=True)
                    ins.then_inc(s_used, 1)
            state["turns"] = e.snap(before + number)
            for n, (o, w) in enumerate(TOK_CHUNKS):
                ins = e.matmul(psum[0:TP, pb + n, 0:w], zeros[0:1, 0:TP], zeros[0:1, 0:w], start=False, stop=True,
                               skip_group_check=True)
            return ins

        ln_ready = layer_norm(htok, x_res, [[x_in, t_cnt]] * NT)
        dve_state, pe_state = {}, {}
        row_free = [None]
        adj_done = []

        def bucket_sum(b):
            pb = 3 * (b % 2)
            DVE.raw(lambda e: build_bucket_dve(e, b, dve_state), t_span, t_iota)
            t = PE.do(lambda e: build_bucket_pe(e, b, pe_state, pb), t_span, t_const,
                      [bank_free[pb + n] for n in range(3)])
            SC.wait(row_free[0])
            for n, (o, w) in enumerate(TOK_CHUNKS):
                t2 = SC.do(lambda e, n=n, o=o, w=w: e.activation(a_row[:, o:o + w], psum[0:TP, pb + n, 0:w], ACT.Copy,
                                                                accum_out=deg3[:, b, n:n + 1]), t)
            for n in range(3):
                bank_free[pb + n] = t2
            rows[b] = t2

        rows = {}

        def bucket_turn(b):
            for g, s0 in enumerate(range(0, NT, 4)):
                ns = min(4, NT - s0)
                q = 6 + turn[0] % 2
                turn[0] += 1

                def fn(e, s0=s0, ns=ns, q=q):
                    for s in range(ns):
                        ins = e.transpose(psum[0:TP, q, s * TP:(s + 1) * TP],
                                          a_row[:, (s0 + s) * TP:(s0 + s + 1) * TP], ident[0:TP, 0:TP])
                    return ins
                t = PE.do(fn, rows[b], bank_free[q], t_id)
                row_free[0] = t
                bank_free[q] = SC.do(lambda e, s0=s0, ns=ns, q=q: e.copy(
                    adj[:, s0:s0 + ns, b * TP:(b + 1) * TP],
                    psum[0:TP, q, 0:ns * TP].rearrange("p (s n) -> p s n", n=TP)), t)
            adj_done.append(bank_free[q])

        turned = to_features(htok, ln_ready)
        pipeline(NT, bucket_sum, bucket_turn)
        t = DVE.do(lambda e: e.tensor_reduce(inv_deg, deg3, AX.X, ALU.add), adj_done[-1])
        t = DVE.do(lambda e: e.tensor_scalar(inv_deg, inv_deg, 1.0, None, ALU.max), t)
        t_inv = DVE.do(lambda e: e.reciprocal(inv_deg, inv_deg), t)

        def z_tiles(w, ready, free):
            out = []
            for i in range(NT):
                b = bank()
                t = PE.do(group(psum[0:TP, b, :], [(hT[:, k, i * TP:(i + 1) * TP], w[:, k, :]) for k in range(KD)]),
                          ready[i], bank_free[b])
                cp = SC.do if i % 2 else DVE.do
                f = (lambda e, i=i, b=b: e.copy(z[:, i, :], psum[0:TP, b, :])) if i % 2 else \
                    (lambda e, i=i, b=b: e.tensor_copy(z[:, i, :], psum[0:TP, b, :]))
                bank_free[b] = cp(f, t, free)
                out.append(bank_free[b])
            return out

        def neigh_pairs(i):
            return [(adj[:, s, i * TP:(i + 1) * TP], z[:, s, :]) for s in range(NT)]

        h_ready, z_free, self_free = turned, adj_done[-1], [None, None]
        PE.wait(w0_in)
        for l in range(N_GNN):
            w_self, w_neigh = w_gnn[:, 2 * l], w_gnn[:, 2 * l + 1]
            z_ready = z_tiles(w_neigh, h_ready, z_free)
            last = l == N_GNN - 1
            new = {}

            def sums(i):
                bs, bn = bank(), bank()
                t_s = PE.do(group(psum[0:TP, bs, :], [(hT[:, k, i * TP:(i + 1) * TP], w_self[:, k, :])
                                                      for k in range(KD)] + [(ones_row, bias_rows[:, l, :])]),
                            bank_free[bs])
                t_n = PE.do(group(psum[0:TP, bn, :], neigh_pairs(i)), z_ready, bank_free[bn])
                t = SC.do(lambda e: e.copy(tmp[:, i % 2, :], psum[0:TP, bs, :]), t_s, self_free[i % 2])
                bank_free[bs] = t
                t = DVE.do(lambda e: e.scalar_tensor_tensor(htok[:, i, :], psum[0:TP, bn, :], inv_deg[:, i:i + 1],
                                                            tmp[:, i % 2, :], ALU.mult, ALU.add), t, t_n, t_inv)
                bank_free[bn] = self_free[i % 2] = t
                if last:
                    t = DVE.do(lambda e: e.tensor_tensor(x_res[:, i, :], x_res[:, i, :], htok[:, i, :], ALU.add), t)
                new[i] = t

            def turns(i):
                new[i] = turn_tile(htok, i, new[i], None, True)

            if last:
                pipeline(NT, sums)
            else:
                pipeline(NT, sums, turns)
            h_ready = [new[i] for i in range(NT)]
            z_free = (PE.sem, PE.count)
        x_ready = h_ready
        t_l0 = (PE.sem, PE.count)

        if upto >= 2:
            def expert_views(slot):
                w = w_reg[:, slot, :]
                return (w[:, 0:4096].rearrange("p (k n) -> p k n", k=KD),
                        w[:, 4096:6144].rearrange("p (k n) -> p k n", k=KD))
            ld_slot = [landing("slot0"), landing("slot1")]
            shared_in = ld_slot[1].dma(SP, w_reg[:, 1, :], a["w_shared"], t_l0)
            slot_in = {0: ld_slot[0].dma(SP, w_reg[:, 0, :], a["w_expert"][0], t_l0)}

            gate_w = sb("gate_w", [128, KD, N_EXP])
            bias16 = blk[0:TP, 0:16]
            ld_r = landing("router")
            ld_r.dma(SC, gate_w.rearrange("p k n -> p (k n)"), a["L0_ffn_gate_w"])
            router_in = ld_r.dma(SC, bias16, a["L0_ffn_expert_bias"].partition_broadcast(TP), t_l0)

            ln_ready = layer_norm(htok, x_res, x_ready)
            turned = to_features(htok, ln_ready)

            rows_dram = nc.dram_tensor("rows", [N_TOK, D], F32).ap()
            list_dram = nc.dram_tensor("slot_tokens", [MAX_BLOCKS * SLOTS, 1], I32).ap()
            outs_dram = nc.dram_tensor("slot_outs", [MAX_BLOCKS * SLOTS, D], F32).ap()
            ld_rows = landing("rows")
            r_view = rows_dram.rearrange("(t p) d -> p t d", p=TP)
            ld_rows.dma(SC, r_view[0:112], htok[0:112], ln_ready)
            rows_out = ld_rows.dma(SC, r_view[112:TP], htok[112:TP])
            rt = blk[0:TP, 16:16 + 2400]
            zero_list = blk[:, 2600:2600 + MAX_BLOCKS].bitcast(I32)
            t = DVE.do(lambda e: e.memset(zero_list, 0), t_l0)
            ld_list = landing("list")
            list_zero = ld_list.dma(SC, list_dram.rearrange("(p c) o -> p (c o)", p=128), zero_list, t)

            zero_rows = blk[:, 2660:3172]
            t = DVE.do(lambda e: e.memset(zero_rows, 0.0), t_l0)
            ld_fill = landing("fill")
            spare = MAX_BLOCKS - MIN_BLOCKS
            outs_filled = ld_fill.dma(SC, outs_dram[MIN_BLOCKS * SLOTS:, :].rearrange("(b p) d -> p b d", p=SLOTS),
                                      zero_rows.unsqueeze(1).to_broadcast([128, spare, D]), t)

            def small(n, w=N_EXP * NT):
                return rt[:, n * w:(n + 1) * w]

            def by_tile(v):
                return v.rearrange("p (t n) -> p t n", t=NT)
            aff, score, hot, prod = (by_tile(small(n)) for n in (0, 1, 2, 3))
            ones_hot = [by_tile(small(4 + k)) for k in range(TOP_K)]
            exp_iota, rank = by_tile(small(7)), by_tile(small(8))
            top8 = small(9)[:, 0:8 * NT].rearrange("p (t n) -> p t n", t=NT)
            top8_i = small(10)[:, 0:8 * NT].bitcast(U32).rearrange("p (t n) -> p t n", t=NT)
            top8_f = small(11)[:, 0:8 * NT].rearrange("p (t n) -> p t n", t=NT)
            sel_aff = small(12)[:, 0:TOP_K * NT].rearrange("p (t n) -> p t n", t=NT)
            gating = sb("gating", [TP, NT, TOP_K])
            slot_f = small(13)[:, 0:TOP_K * NT].rearrange("p (t n) -> p t n", t=NT)
            slot_i = sb("slot_i", [TP, TOP_K, NT], I32)
            tok_id = sb("tok_id", [TP, NT], I32)
            picked = sb("picked", [TP, NT, N_EXP], BF16)
            before = sb("before", [TP, TP], BF16)
            ones_b = sb("ones_b", [TP, 128], BF16)
            n_blk_i = sb("n_blk_i", [128, N_EXP + 1], I32)
            n_blk_f = sb("n_blk_f", [128, N_EXP])
            base_f = sb("base_f", [128, N_EXP])
            one16 = sb("one16", [128, N_EXP])

            POOL.do(lambda e: e.iota(exp_iota, [[0, NT], [1, N_EXP]], base=0, channel_multiplier=0,
                                     allow_small_or_imprecise_dtypes=True), t_l0)
            t_tok = POOL.do(lambda e: e.iota(tok_id, [[TP, NT]], base=0, channel_multiplier=1))
            t = POOL.do(lambda e: e.memset(before, 1.0))
            t_lt = POOL.do(lambda e: e.affine_select(out=before, in_=before, compare_op=ALU.is_gt, fill=0.0, base=0,
                                                     pattern=[[1, TP]], channel_multiplier=-1), t)
            DVE.do(lambda e: e.memset(one16, 1.0))
            t_ones = DVE.do(lambda e: e.memset(ones_b, 1.0))

            lb = bank()

            def logits(e):
                for i in range(NT):
                    for k in range(KD):
                        ins = e.matmul(psum[0:TP, lb, i * N_EXP:(i + 1) * N_EXP], hT[:, k, i * TP:(i + 1) * TP],
                                       gate_w[:, k, :], start=(k == 0), stop=(k == KD - 1))
                return ins
            t = PE.do(logits, turned, router_in, bank_free[lb])
            t = SC.do(lambda e: e.activation(aff, psum[0:TP, lb, 0:NT * N_EXP].rearrange("p (t n) -> p t n", t=NT),
                                             ACT.Sigmoid), t, t_l0)
            bank_free[lb] = t
            t = DVE.do(lambda e: e.tensor_tensor(score, aff, bias16.unsqueeze(1).to_broadcast([TP, NT, N_EXP]),
                                                 ALU.add), t, router_in)
            for i in range(NT):
                t2 = DVE.do(lambda e, i=i: e.max(top8[:, i, :], score[:, i, :]), t)
            for i in range(NT):
                t = DVE.do(lambda e, i=i: e.max_index(top8_i[:, i, :], top8[:, i, :], score[:, i, :]), t2)
            t_top = DVE.do(lambda e: e.tensor_copy(top8_f, top8_i), t)
            for k in range(TOP_K):
                t = DVE.do(lambda e, k=k: e.tensor_tensor(
                    ones_hot[k], exp_iota, top8_f[:, :, k:k + 1].to_broadcast([TP, NT, N_EXP]), ALU.is_equal),
                    t_top, t_tok)
                t2 = DVE.do(lambda e, k=k: e.tensor_tensor(prod, ones_hot[k], aff, ALU.mult), t)
                t2 = DVE.do(lambda e, k=k: e.tensor_reduce(sel_aff[:, :, k], prod, AX.X, ALU.add), t2)
            denom = small(12)[:, 40:40 + NT]
            t2 = DVE.do(lambda e: e.tensor_reduce(denom, sel_aff, AX.X, ALU.add), t2)
            t2 = DVE.do(lambda e: e.tensor_scalar(denom, denom, 1e-9, None, ALU.add), t2)
            t2 = DVE.do(lambda e: e.reciprocal(denom, denom), t2)
            t_gate = DVE.do(lambda e: e.tensor_tensor(
                gating, sel_aff, denom.unsqueeze(2).to_broadcast([TP, NT, TOP_K]), ALU.mult), t2)
            t = DVE.do(lambda e: e.tensor_tensor(hot, ones_hot[0], ones_hot[1], ALU.add), t)
            t = DVE.do(lambda e: e.tensor_tensor(picked, hot, ones_hot[2], ALU.add), t)

            rb = bank()

            def ranks(e):
                for i in range(NT):
                    for j in range(i + 1):
                        e.matmul(psum[0:TP, rb, i * N_EXP:(i + 1) * N_EXP], before if j == i else ones_b[:, 0:TP],
                                 picked[:, j, :], start=(j == 0), stop=(j == i))
                for j in range(NT):
                    ins = e.matmul(psum[:, rb, 256:256 + N_EXP], ones_b, picked[:, j, :],
                                   start=(j == 0), stop=(j == NT - 1))
                return ins
            t_rank = PE.do(ranks, t, t_lt, t_ones, bank_free[rb])
            t = DVE.do(lambda e: e.tensor_scalar(n_blk_i[:, 0:N_EXP], psum[:, rb, 256:256 + N_EXP],
                                                 float(SLOTS - 1), float(SLOTS), ALU.add, ALU.max), t_rank)
            t = DVE.do(lambda e: e.tensor_single_scalar(n_blk_i[:, 0:N_EXP], n_blk_i[:, 0:N_EXP],
                                                        SLOTS.bit_length() - 1, ALU.arith_shift_right), t)
            t = DVE.do(lambda e: e.tensor_copy(n_blk_f, n_blk_i[:, 0:N_EXP]), t)
            t = DVE.do(lambda e: e.tensor_tensor_scan(base_f, one16, n_blk_f, 0.0, ALU.mult, ALU.add), t)
            t_nblk = DVE.do(lambda e: e.tensor_copy(n_blk_i[:, N_EXP:N_EXP + 1], base_f[:, N_EXP - 1:N_EXP]), t)
            t = DVE.do(lambda e: e.tensor_tensor(base_f, base_f, n_blk_f, ALU.subtract), t_nblk)
            t = DVE.do(lambda e: e.tensor_scalar(base_f, base_f, float(SLOTS), None, ALU.mult), t)
            t = DVE.do(lambda e: e.tensor_tensor(
                rank, psum[0:TP, rb, 0:NT * N_EXP].rearrange("p (t n) -> p t n", t=NT),
                base_f[0:TP].unsqueeze(1).to_broadcast([TP, NT, N_EXP]), ALU.add), t)
            bank_free[rb] = t
            for k in range(TOP_K):
                t = DVE.do(lambda e, k=k: e.tensor_tensor(prod, ones_hot[k], rank, ALU.mult), t)
                t = DVE.do(lambda e, k=k: e.tensor_reduce(slot_f[:, :, k], prod, AX.X, ALU.add), t)
                t = DVE.do(lambda e, k=k: e.tensor_copy(slot_i[:, k, :], slot_f[:, :, k]), t)
            t_slot = t

            ld_scatter = landing("scatter")
            for i in range(NT):
                for k in range(TOP_K):
                    POOL.wait(t_slot, t_tok, list_zero)
                    ld_scatter.total += 16
                    POOL.steps.append(lambda e, i=i, k=k: e.indirect_dma_start(
                        list_dram, bass.IndirectOffsetOnAxis(ap=slot_i[:, k, i:i + 1], axis=0),
                        tok_id[:, i:i + 1], None).then_inc(ld_scatter.sem, 16))
            list_out = (ld_scatter.sem, ld_scatter.total)

            w_gu, w_dn = expert_views(1)
            hid_s = z_reg[:, 0:KD * N_TOK].rearrange("p (k n) -> p k n", k=KD)
            sil = sb("sil", [128, 2, 418])
            sil_free = [None, None]
            hid_ready = []
            steps = [(c, f) for c in range(len(TOK_CHUNKS)) for f in range(KD)]

            def shared_up(n):
                c, f = steps[n]
                o, w = TOK_CHUNKS[c]
                bg, bu = bank(), bank()
                t_g = PE.do(group(psum[:, bg, 0:w], [(w_gu[:, k, f * 128:(f + 1) * 128], hT[:, k, o:o + w])
                                                     for k in range(KD)]), turned, shared_in, bank_free[bg])
                t_u = PE.do(group(psum[:, bu, 0:w], [(w_gu[:, k, D_FF + f * 128:D_FF + (f + 1) * 128],
                                                      hT[:, k, o:o + w]) for k in range(KD)]), bank_free[bu])
                t = SC.do(lambda e: e.activation(sil[:, n % 2, 0:w], psum[:, bg, 0:w], ACT.Silu), t_g, sil_free[n % 2])
                bank_free[bg] = t
                t = DVE.do(lambda e: e.tensor_tensor(hid_s[:, f, o:o + w], sil[:, n % 2, 0:w], psum[:, bu, 0:w],
                                                     ALU.mult), t, t_u)
                bank_free[bu] = sil_free[n % 2] = t
                hid_ready.append(t)
            for n in range(len(steps)):
                shared_up(n)
            x_ready = []
            for i in range(NT):
                b = bank()
                t = PE.do(group(psum[0:TP, b, :], [(hid_s[:, k, i * TP:(i + 1) * TP], w_dn[:, k, :])
                                                   for k in range(KD)]), hid_ready[-1], bank_free[b])
                bank_free[b] = DVE.do(lambda e, i=i, b=b: e.tensor_tensor(
                    x_res[:, i, :], x_res[:, i, :], psum[0:TP, b, :], ALU.add), t)
                x_ready.append(bank_free[b])
            t_shared = (PE.sem, PE.count)

            xg = blk[:, 0:512]
            xgT = blk[:, 512:1024].rearrange("p (k n) -> p k n", k=KD)
            hid = blk[:, 1024:1536]
            hidT = blk[:, 1536:2048].rearrange("p (k n) -> p k n", k=KD)
            silg = blk[:, 2048:2560].rearrange("p (h n) -> p h n", h=2)
            y_blk = blk[:, 2560:3072]
            idx = blk[:, 3072:3073].bitcast(I32)
            s_idx, s_row, s_out = sem("idx_in"), sem("rows_in"), sem("block_out")
            s_xt, s_xe, s_gu, s_hid, s_ht, s_he, s_dn, s_y = (sem(n) for n in (
                "x_turned", "x_copied", "gate_up", "hidden", "hid_turned", "hid_copied", "down", "y_ready"))
            HF = D_FF // 2

            def row_of(e, g):
                return e.bass.s_assert_within(
                    g, 0, MAX_BLOCKS - 1,
                    skip_runtime_bounds_check_because="the experts' blocks are at most MAX_BLOCKS in all") * SLOTS

            def loops(e, body, before_expert=None, after_expert=None):
                done = 0
                for x in range(N_EXP):
                    if before_expert:
                        before_expert(e, x)
                    number = e.value_load(n_blk_i[0:1, x:x + 1], min_val=1, max_val=10)
                    with e.Fori(0, number) as i:
                        body(e, x, done + i)
                    done = e.snap(done + number)
                    if after_expert:
                        after_expert(e, x)
                return done

            s_pass = sem("gather_may_go")

            def pool_blocks(e):
                total = e.value_load(n_blk_i[0:1, N_EXP:N_EXP + 1], min_val=N_EXP, max_val=MAX_BLOCKS)
                with e.Fori(0, total) as g:
                    e.wait_ge(s_xt, g + 1)
                    e.dma_start(idx, list_dram[bass.ds(row_of(e, g), SLOTS), :]).then_inc(s_idx, 16)
                    e.wait_ge(s_idx, g * 16 + 16)
                    e.sem_inc(s_pass, 1)
                    e.indirect_dma_start(xg, None, rows_dram,
                                         bass.IndirectOffsetOnAxis(ap=idx, axis=0)).then_inc(s_row, 16)
            POOL.raw(pool_blocks, t_nblk, list_out, rows_out, t_rank, t_shared, outs_filled, list_zero)

            def pe_block(e, x, g):
                w_gu, w_dn = expert_views(x % 2)
                e.wait_ge(s_row, g * 16 + 16)
                for k in range(KD):
                    ins = e.transpose(psum[:, 0, k * 128:(k + 1) * 128], xg[:, k * 128:(k + 1) * 128], ident)
                ins.then_inc(s_xt, 1)
                e.wait_ge(s_xe, g + 1)
                e.wait_ge(s_hid, g * 2 + 2)
                for h in range(2):
                    for part in range(2):
                        for k in range(KD):
                            c = part * D_FF + h * HF
                            ins = e.matmul(psum[:, 1 + h, part * HF:(part + 1) * HF], xgT[:, k, :],
                                           w_gu[:, k, c:c + HF], start=(k == 0), stop=(k == KD - 1))
                    ins.then_inc(s_gu, 1)
                for h in range(2):
                    e.wait_ge(s_hid, g * 2 + h + 3)
                    if h == 0:
                        e.wait_ge(s_he, g * 2 + 2)
                    for k in range(2):
                        ins = e.transpose(psum[:, 3 + h, k * 128:(k + 1) * 128],
                                          hid[:, h * HF + k * 128:h * HF + (k + 1) * 128], ident)
                    ins.then_inc(s_ht, 1)
                e.wait_ge(s_y, g + 1)
                for k in range(KD):
                    if k % 2 == 0:
                        e.wait_ge(s_he, g * 2 + k // 2 + 3)
                    ins = e.matmul(psum[:, 5, :], hidT[:, k, :], w_dn[:, k, :], start=(k == 0), stop=(k == KD - 1))
                ins.then_inc(s_dn, 1)

            def act_block(e, x, g):
                e.wait_ge(s_xt, g + 2)
                e.copy(xgT.rearrange("p k n -> p (k n)"), psum[:, 0, :]).then_inc(s_xe, 1)
                for h in range(2):
                    e.wait_ge(s_gu, g * 2 + h + 1)
                    e.activation(silg[:, h, :], psum[:, 1 + h, 0:HF], ACT.Silu).then_inc(s_sil, 1)
                e.wait_ge(s_dn, g + 1)
                e.wait_ge(s_out, g * 16 + 16)
                e.copy(y_blk, psum[:, 5, :]).then_inc(s_y, 1)
            s_sil = sem("silu")

            def dve_block(e, x, g):
                for h in range(2):
                    e.wait_ge(s_sil, g * 2 + h + 1)
                    e.tensor_tensor(hid[:, h * HF:(h + 1) * HF], silg[:, h, :], psum[:, 1 + h, HF:2 * HF],
                                    ALU.mult).then_inc(s_hid, 1)
                for h in range(2):
                    e.wait_ge(s_ht, g * 2 + h + 1)
                    e.tensor_copy(hidT[:, 2 * h:2 * h + 2, :].rearrange("p k n -> p (k n)"),
                                  psum[:, 3 + h, 0:256]).then_inc(s_he, 1)

            def sp_block(e, x, g):
                e.wait_ge(s_y, g + 2)
                e.dma_start(outs_dram[bass.ds(row_of(e, g), SLOTS), :], y_blk).then_inc(s_out, 16)

            PE.wait(bank_free, t_nblk)
            s_exp = sem("expert_done")

            def weights_ready(e, x):
                e.wait_ge(ld_slot[x % 2].sem, slot_need[x])

            slot_need = {0: 16}
            for x in range(1, N_EXP):
                slot_need[x] = slot_need.get(x - 2, 16) + 16 if x > 1 else 32

            def load_next(e, x):
                if x + 1 < N_EXP:
                    if x >= 1:
                        e.wait_ge(s_exp, x)
                    e.dma_start(w_reg[:, (x + 1) % 2, :], a["w_expert"][x + 1]).then_inc(
                        ld_slot[(x + 1) % 2].sem, 16)

            def pe_all(e):
                done = 0
                for x in range(N_EXP):
                    weights_ready(e, x)
                    number = e.value_load(n_blk_i[0:1, x:x + 1], min_val=1, max_val=10)
                    with e.Fori(0, number) as i:
                        pe_block(e, x, done + i)
                    done = e.snap(done + number)
                    ins = e.matmul(psum[0:1, 6, 0:2], ident[:, 0:1], ident[:, 0:2], start=True, stop=True)
                    ins.then_inc(s_exp, 1)
                return e.matmul(psum[0:1, 6, 0:2], ident[:, 0:1], ident[:, 0:2], start=True, stop=True)
            t_pe_moe = PE.do(pe_all)
            SC.raw(lambda e: loops(e, act_block), t_nblk, t_shared, bank_free, outs_filled)
            DVE.raw(lambda e: loops(e, dve_block), t_nblk, t_shared, bank_free)
            SP.wait(t_nblk, t_shared, outs_filled)

            def sp_all(e):
                for s, n in ((s_xt, 1), (s_hid, 2), (s_he, 2), (s_y, 1), (s_out, 16)):
                    e.sem_inc(s, n)
                g = loops(e, sp_block, load_next)
                e.wait_ge(s_out, g * 16 + 16)
                return e.sem_inc(stored, 1)
            stored = sem("blocks_stored")
            SP.raw(sp_all)
            for ld, x in ((ld_slot[0], N_EXP - 2), (ld_slot[1], N_EXP - 1)):
                ld.total = slot_need[x]
            t_stored = (stored, 1)

            ring = z_reg[0:TP, :].rearrange("p (r n) -> p r n", n=D)
            RING = NT
            ld_take = [landing(f"take{r}") for r in range(RING)]
            ring_free = [t_shared] * RING
            for i in range(NT):
                for k in range(TOP_K):
                    r = (i * TOP_K + k) % RING
                    POOL.wait(t_stored, ring_free[r])
                    ld_take[r].total += 16
                    POOL.steps.append(lambda e, i=i, k=k, r=r: e.indirect_dma_start(
                        ring[:, r, :], None, outs_dram,
                        bass.IndirectOffsetOnAxis(ap=slot_i[:, k, i:i + 1], axis=0)).then_inc(ld_take[r].sem, 16))
                    x_ready[i] = ring_free[r] = DVE.do(lambda e, i=i, k=k, r=r: e.scalar_tensor_tensor(
                        x_res[:, i, :], ring[:, r, :], gating[:, i, k:k + 1], x_res[:, i, :], ALU.mult, ALU.add),
                        (ld_take[r].sem, ld_take[r].total), x_ready[i], t_gate)
            bank_free[:] = [t_pe_moe] * 8

        if upto >= 3:
            ld_a, ld_b, ld_c = landing("qkv"), landing("slot_b"), landing("norms")
            experts_over = t_pe_moe
            qkv_in = ld_a.dma(SP, w_reg[:, 0, :], a["w_qkv"], (s_exp, N_EXP - 1))
            wb_in = ld_b.dma(SP, w_reg[:, 1, :], a["w_last"], experts_over)
            w_q, w_k, w_v = (w_reg[:, 0, n * 2048:(n + 1) * 2048].rearrange("p (k n) -> p k n", k=KD) for n in range(3))
            w_o = w_reg[:, 1, 0:2048].rearrange("p (k n) -> p k n", k=KD)
            rows3 = blk[0:TP, 0:1536].rearrange("p (m d) -> p m d", d=D)
            attn = blk[:, 1536:2560].rearrange("p (t d) -> p t d", d=D)
            projT = blk[:, 2560:2816]
            kv = blk[:, 2816:3076].rearrange("p (r m d) -> p r m d", r=2, m=2)
            mean_w = blk[0:TP, 3076:3201]
            half = blk[:, 3201:3202]
            s3 = blk[:, 3202:3500]
            blk_over = [x_ready[-1], t_stored, (POOL.sem, POOL.count), t_pe_moe]
            for n, name in enumerate(("L1_gnn_b_conv", "L1_gnn_norm2_g", "L1_gnn_norm2_b")):
                ld_c.dma(SP, rows3[:, n, :], a[name].partition_broadcast(TP), blk_over)
            n1 = sb("n1", [128, 2, KD])
            ld_c.dma(SP, n1[:, 0, :], a["L1_gnn_norm1_g"])
            ld_c.dma(SP, n1[:, 1, :], a["L1_gnn_norm1_b"])
            for h in range(2):
                norms_in = ld_c.dma(SP, projT[h * 64:h * 64 + 64, :], a["projT"])
            DVE.do(lambda e: e.memset(mean_w, 1.0 / N_TOK), blk_over)
            t_half = DVE.do(lambda e: e.memset(half, 0.5))

            ln_ready = layer_norm(htok, x_res, x_ready)
            turned = to_features(htok, ln_ready)

            qk = [z_reg[:, n * 1024:(n + 1) * 1024].rearrange("p (f n) -> p f n", f=KD) for n in range(2)]
            qf = z_reg[:, 2048:3072].rearrange("p (r t m) -> p r t m", r=2, t=2)
            kf = z_reg[:, 3072:4096].rearrange("p (r t m) -> p r t m", r=2, t=2)
            qfT = z_reg[:, 4096:4608].rearrange("p (m n) -> p m n", m=2)
            v_ext = w_reg[:, 0, 0:1040].rearrange("p (t h d) -> p t h d", t=2, h=HEADS)
            attnT = w_reg[:, 0, 2048:4048].rearrange("p (k n) -> p k n", k=KD)
            sq = [w_reg[:, 0, 4096 + n * 1024:5120 + n * 1024].rearrange("p (f n) -> p f n", f=KD) for n in range(2)]
            h_attn = w_reg[0:TP, 0, 0:2048].rearrange("p (t d) -> p t d", d=D)
            scale = DH ** -0.25
            t_qk = []
            for n, w in enumerate((w_q, w_k)):
                for f2 in range(2):
                    b = bank()

                    def fn(e, w=w, f2=f2, b=b):
                        for f in range(2):
                            for k in range(KD):
                                c = (f2 * 2 + f) * 128
                                ins = e.matmul(psum[:, b, f * 256:(f + 1) * 256], w[:, k, c:c + 128], hT[:, k, 0:N_DENSE],
                                               start=(k == 0), stop=(k == KD - 1))
                        return ins
                    t = PE.do(fn, turned[2], qkv_in, bank_free[b])
                    bank_free[b] = SC.do(lambda e, n=n, f2=f2, b=b: e.mul(
                        qk[n][:, 2 * f2:2 * f2 + 2, :].rearrange("p f n -> p (f n)"), psum[:, b, :], scale), t,
                        x_ready[-1])
                    t_qk.append(bank_free[b])
            t_v = []
            for s in range(2):
                b = bank()
                t = PE.do(group(psum[:, b, :], [(hT[:, k, s * 128:(s + 1) * 128], w_v[:, k, :]) for k in range(KD)]),
                          bank_free[b])
                t_v.append((s, b, t))
            t_qkv = t
            for s, b, t in t_v:
                bank_free[b] = DVE.do(lambda e, s=s, b=b: e.tensor_copy(
                    v_ext[:, s, :, 0:DH], psum[:, b, :].rearrange("p (h d) -> p h d", h=HEADS)), t, t_qkv)
            t_vx = DVE.do(lambda e: e.memset(v_ext[:, :, :, DH:DH + 1], 1.0), t_qkv)
            t_sq = [SC.do(lambda e, n=n: e.square(sq[n], qk[n]), t_qk, t_qkv) for n in range(2)]
            diag = s3[:, 0:32].rearrange("p (q t h) -> p q t h", q=2, t=2)
            db = [bank(), bank()]

            def diags(e):
                for odd in range(2):
                    rows = slice(64 * odd, 64 * odd + 64)
                    for n in range(2):
                        for s in range(2):
                            for f in range(KD):
                                c = (n * 2 + s) * KD + f
                                ins = e.matmul(psum[:, db[odd], c:c + 1], sq[n][rows, f, s * 128:(s + 1) * 128],
                                               half[rows, :], start=True, stop=True)
                return ins
            t = PE.do(diags, t_sq, t_half, bank_free[db[0]], bank_free[db[1]])
            for odd in range(2):
                t_diag = bank_free[db[odd]] = DVE.do(lambda e, odd=odd: e.tensor_copy(
                    diag[:, :, :, odd:HEADS:2].rearrange("p q t h -> p (q t) h"),
                    psum[:, db[odd], 0:4 * KD].rearrange("p (q h) -> p q h", h=KD)), t, blk_over)

            def features(n, h, b):
                rows = slice(64 * (h % 2), 64 * (h % 2) + 64)

                def fn(e):
                    for s in range(2):
                        ins = e.matmul(psum[:, b, s * 256:(s + 1) * 256], qk[n][rows, h // 2, s * 128:(s + 1) * 128],
                                       projT[rows, :], start=True, stop=True)
                    return ins
                return PE.do(fn, t_qk, norms_in, bank_free[b])

            k_max = s3[:, 32:40]
            for h in range(HEADS):
                b = bank()
                t = features(1, h, b)
                t_km = bank_free[b] = DVE.do(lambda e, h=h, b=b: e.reduce_max(k_max[:, h:h + 1], psum[:, b, :], AX.X),
                                             t, blk_over)
            b = bank()
            t = PE.do(lambda e, b=b: e.transpose(psum[0:HEADS, b, 0:128], k_max, ident), t_km, bank_free[b])
            k_max8, k_diag = s3[0:HEADS, 40:41], s3[0:HEADS, 41:49]
            t = bank_free[b] = DVE.do(lambda e, b=b: e.reduce_max(k_max8, psum[0:HEADS, b, 0:128], AX.X), t)
            t = DVE.do(lambda e: e.tensor_scalar(k_diag, ident[0:HEADS, 0:HEADS], k_max8, None, ALU.mult), t)
            ones8 = s3[0:HEADS, 49:177]
            t2 = DVE.do(lambda e: e.memset(ones8, 1.0), blk_over)
            b = bank()
            t = PE.do(lambda e, b=b: e.matmul(psum[:, b, 0:HEADS], ones8, k_diag, start=True, stop=True), t, t2,
                      bank_free[b])
            k_bias = s3[:, 180:196].rearrange("p (t h) -> p t h", t=2)
            for s in range(2):
                t_kb = DVE.do(lambda e, s=s, b=b: e.scalar_tensor_tensor(
                    k_bias[:, s, :], diag[:, 1, s, :], -1.0, psum[:, b, 0:HEADS], ALU.mult, ALU.subtract), t, t_diag)
            bank_free[b] = t_kb
            q_max = s3[:, 196:212].rearrange("p (t h) -> p t h", t=2)
            q_bias = s3[:, 212:228].rearrange("p (t h) -> p t h", t=2)
            rden = s3[:, 228:244].rearrange("p (t h) -> p t h", t=2)
            inv_root_m = M_FEAT ** -0.5
            head = [{} for _ in range(HEADS)]
            attn_done = []

            def head_features(h):
                r, me = h % 2, head[h]
                bk, bq = bank(), bank()
                t_k, t_q = features(1, h, bk), features(0, h, bq)
                for s in range(2):
                    t = SC.do(lambda e, s=s: e.activation(kf[:, r, s, :], psum[:, bk, s * 256:(s + 1) * 256], ACT.Exp,
                                                          bias=k_bias[:, s, h:h + 1]), t_k, t_kb,
                              head[h - 2].get("kv") if h >= 2 else None)
                bank_free[bk] = t
                me["kf"] = DVE.do(lambda e: e.tensor_scalar(kf[:, r], kf[:, r], inv_root_m, K_EPS, ALU.mult, ALU.add), t)
                t = DVE.do(lambda e: e.tensor_reduce(q_max[:, :, h], psum[:, bq, :].rearrange("p (t m) -> p t m", t=2),
                                                     AX.X, ALU.max), t_q)
                t = DVE.do(lambda e: e.scalar_tensor_tensor(q_bias[:, :, h], diag[:, 0, :, h], -1.0, q_max[:, :, h],
                                                            ALU.mult, ALU.subtract), t, t_diag)
                for s in range(2):
                    t2 = SC.do(lambda e, s=s: e.activation(qf[:, r, s, :], psum[:, bq, s * 256:(s + 1) * 256], ACT.Exp,
                                                           bias=q_bias[:, s, h:h + 1]), t,
                               head[h - 2].get("turned") if h >= 2 else None)
                bank_free[bq] = t2
                me["qf"] = DVE.do(lambda e: e.tensor_scalar(qf[:, r], qf[:, r], inv_root_m, K_EPS, ALU.mult, ALU.add), t2)

            def head_products(h):
                r, me = h % 2, head[h]
                b = bank()

                def fn_kv(e):
                    for m in range(2):
                        for s in range(2):
                            ins = e.matmul(psum[:, b, m * 65:(m + 1) * 65], kf[:, r, s, m * 128:(m + 1) * 128],
                                           v_ext[:, s, h, :], start=(s == 0), stop=(s == 1))
                    return ins
                me["kv"] = PE.do(fn_kv, me["kf"], t_vx, bank_free[b])
                t_kv = bank_free[b] = DVE.do(lambda e: e.tensor_copy(
                    kv[:, r].rearrange("p m d -> p (m d)"), psum[:, b, 0:130]), me["kv"],
                    head[h - 2].get("out") if h >= 2 else None)
                bt = bank()

                def fn_t(e):
                    for m in range(2):
                        for s in range(2):
                            ins = e.transpose(psum[:, bt, m * 256 + s * 128:m * 256 + (s + 1) * 128],
                                              qf[:, r, s, m * 128:(m + 1) * 128], ident)
                    return ins
                me["turned"] = PE.do(fn_t, me["qf"], bank_free[bt])
                t_q = bank_free[bt] = SC.do(lambda e: e.copy(qfT.rearrange("p m n -> p (m n)"), psum[:, bt, :]),
                                            me["turned"], head[h - 1].get("out") if h >= 1 else None)
                bo = bank()

                def fn_o(e):
                    for s in range(2):
                        for m in range(2):
                            ins = e.matmul(psum[:, bo, s * 65:(s + 1) * 65], qfT[:, m, s * 128:(s + 1) * 128],
                                           kv[:, r, m, :], start=(m == 0), stop=(m == 1))
                    return ins
                me["out"] = PE.do(fn_o, t_q, t_kv, bank_free[bo])
                out = psum[:, bo, 0:130].rearrange("p (t d) -> p t d", t=2)
                t = DVE.do(lambda e: e.tensor_scalar(rden[:, :, h], out[:, :, DH], K_EPS, None, ALU.add), me["out"])
                t = DVE.do(lambda e: e.reciprocal(rden[:, :, h], rden[:, :, h]), t)
                for s in range(2):
                    t2 = DVE.do(lambda e, s=s: e.tensor_scalar(attn[:, s, h * DH:(h + 1) * DH], out[:, s, 0:DH],
                                                               rden[:, s, h:h + 1], None, ALU.mult), t)
                bank_free[bo] = t2
                attn_done.append(t2)
            pipeline(HEADS, head_features, head_products)

            for s in range(2):
                b = bank()

                def fn(e, s=s, b=b):
                    for k in range(KD):
                        ins = e.transpose(psum[:, b, k * 128:(k + 1) * 128], attn[:, s, k * 128:(k + 1) * 128], ident)
                    return ins
                t = PE.do(fn, attn_done[-1], bank_free[b])
                t = bank_free[b] = DVE.do(lambda e, s=s, b=b: e.tensor_copy(
                    attnT[:, :, s * 128:(s + 1) * 128], psum[:, b, :].rearrange("p (k n) -> p k n", k=KD)), t, t_qkv)
            t_at = DVE.do(lambda e: e.tensor_copy(attnT[:, :, N_DENSE:4 * TP],
                                                  attnT[:, :, N_DENSE - 1:N_DENSE].to_broadcast([128, KD, 4 * TP - N_DENSE])), t)
            for i in range(4):
                b = bank()
                t = PE.do(group(psum[0:TP, b, :], [(attnT[:, k, i * TP:(i + 1) * TP], w_o[:, k, :]) for k in range(KD)]),
                          t_at, wb_in, bank_free[b])
                t_ha = bank_free[b] = SC.do(lambda e, i=i, b=b: e.copy(h_attn[:, i, :], psum[0:TP, b, :]), t,
                                            head[HEADS - 1]["out"])

            bst = s3[:, 0:72].rearrange("p (k c s) -> p k c s", k=KD, c=3)
            bmv = s3[:, 72:80].rearrange("p (k s) -> p k s", k=KD)
            bsc, bsh = s3[:, 80:84], s3[:, 84:88]
            for k in range(KD):
                for c, (o, w) in enumerate(TOK_CHUNKS):
                    t = DVE.do(lambda e, k=k, c=c, o=o, w=w: e.bn_stats(bst[:, k, c, :], hT[:, k, o:o + w]), turned,
                               attn_done)
            for k in range(KD):
                t2 = DVE.do(lambda e, k=k: e.bn_aggr(bmv[:, k, :], bst[:, k].rearrange("p c s -> p (c s)")), t)
            t = SC.do(lambda e: e.activation(bsc, bmv[:, :, 1], ACT.Sqrt, bias=eps), t2)
            t = DVE.do(lambda e: e.reciprocal(bsc, bsc), t)
            t = DVE.do(lambda e: e.tensor_tensor(bsc, bsc, n1[:, 0, :], ALU.mult), t, norms_in)
            t = DVE.do(lambda e: e.tensor_tensor(bsh, bmv[:, :, 0], bsc, ALU.mult), t)
            t = DVE.do(lambda e: e.tensor_tensor(bsh, n1[:, 1, :], bsh, ALU.subtract), t)
            for k in range(KD):
                t_xn = DVE.do(lambda e, k=k: e.tensor_scalar(hT[:, k, :], hT[:, k, :], bsc[:, k:k + 1],
                                                             bsh[:, k:k + 1], ALU.mult, ALU.add), t, t_qkv)

            z_ready = z_tiles(w_conv, [[t_xn, wc_in]] * NT, head[HEADS - 1]["out"])
            ctmp = z_t = w_reg[0:TP, 0, 4096:5120].rearrange("p (r d) -> p r d", r=2)
            y_ready, ct_free = [], [None, None]
            for i in range(NT):
                b = bank()
                t = PE.do(group(psum[0:TP, b, :], neigh_pairs(i)), z_ready, bank_free[b])
                t = bank_free[b] = DVE.do(lambda e, i=i, b=b: e.scalar_tensor_tensor(
                    ctmp[:, i % 2, :], psum[0:TP, b, :], inv_deg[:, i:i + 1], rows3[:, 0, :], ALU.mult, ALU.add), t,
                    t_ha, norms_in)
                t = DVE.do(lambda e, i=i: e.scalar_tensor_tensor(
                    ctmp[:, i % 2, :], ctmp[:, i % 2, :], 0.0, h_attn[:, min(i, 3), :], ALU.max, ALU.add), t)
                y_ready.append(DVE.do(lambda e, i=i: e.tensor_tensor(htok[:, i, :], htok[:, i, :], ctmp[:, i % 2, :],
                                                                     ALU.add), t))
            adj_over = (PE.sem, PE.count)

            def token_mean(src, ready):
                b = bank()
                t = None
                for i in range(NT):
                    t = PE.do(lambda e, i=i: e.matmul(psum[0:TP, b, :], mean_w, src(i), start=(i == 0),
                                                      stop=(i == NT - 1)), ready[i], bank_free[b])
                return b, t
            bm, t_mean = token_mean(lambda i: htok[:, i, :], y_ready)
            c_ready, s_ready = [], []
            for i in range(NT):
                c_ready.append(DVE.do(lambda e, i=i: e.tensor_tensor(htok[:, i, :], htok[:, i, :], psum[0:TP, bm, :],
                                                                     ALU.subtract), t_mean))
                s_ready.append(SC.do(lambda e, i=i: e.square(z[:, i, :], htok[:, i, :]), c_ready[i], adj_over))
            bank_free[bm] = c_ready[-1]
            bv, t_var = token_mean(lambda i: z[:, i, :], s_ready)
            sc2 = ctmp[:, 0, :]
            t = bank_free[bv] = SC.do(lambda e: e.activation(sc2, psum[0:TP, bv, :], ACT.Sqrt, bias=eps[0:TP, :]),
                                      t_var, y_ready)
            t = DVE.do(lambda e: e.reciprocal(sc2, sc2), t)
            t_sc = DVE.do(lambda e: e.tensor_tensor(sc2, sc2, rows3[:, 1, :], ALU.mult), t)
            x_ready = []
            for i in range(NT):
                t = POOL.do(lambda e, i=i: e.tensor_tensor(x_res[:, i, :], x_res[:, i, :], rows3[:, 2, :], ALU.add),
                            t_sc)
                t2 = DVE.do(lambda e, i=i: e.tensor_tensor(htok[:, i, :], htok[:, i, :], sc2, ALU.mult), t_sc, s_ready)
                x_ready.append(DVE.do(lambda e, i=i: e.tensor_tensor(x_res[:, i, :], x_res[:, i, :], htok[:, i, :],
                                                                     ALU.add), t, t2))

        if upto >= 4:
            ld_d = landing("values")
            w_pv = w_conv.rearrange("p k n -> p (k n)").rearrange("p (k n) -> p k n", n=D_PV)
            t_zc = (PE.sem, PE.count)
            ld_d.dma(SP, w_conv.rearrange("p k n -> p (k n)"), a["w_values"], t_zc)
            w_oi_flat = a_reg[:, 10720:11232]
            w_oi_r = w_oi_flat.rearrange("p (k n) -> p k n", k=2)
            d_in = ld_d.dma(SP, w_oi_flat, a["w_oi"], adj_over)
            w_pi = w_reg[:, 1, 2048:4096].rearrange("p (k n) -> p k n", k=2)
            w_ip = w_reg[:, 1, 4096:5120].rearrange("p (k n) -> p k n", k=KD)
            w_op = w_reg[:, 1, 5120:6144].rearrange("p (k n) -> p k n", k=2)
            actsT = z_reg[:, 0:2 * N_TOK].rearrange("p (k n) -> p k n", k=2)
            ring3 = a_reg[0:TP, 0:3072].rearrange("p (r n) -> p r n", r=3)
            work = a_reg[0:TP, 3072:5120].rearrange("p (r n) -> p r n", r=2)
            wexp = a_reg[0:TP, 5120:7168].rearrange("p (r n) -> p r n", r=2)
            wT = a_reg[:, 7168:9168].rearrange("p (r k n) -> p r k n", r=2, k=8)
            agg = a_reg[0:TP, 9168:9680].rearrange("p (r n) -> p r n", r=2)
            aggT = a_reg[:, 9680:10180].rearrange("p (r k n) -> p r k n", r=2, k=2)
            outT = a_reg[:, 10180:10680].rearrange("p (r k n) -> p r k n", r=2, k=2)
            best = a_reg[0:TP, 10680:10712].rearrange("p (r n) -> p r n", r=4)
            negm = a_reg[0:TP, 10712:10716]
            wsum = a_reg[0:TP, 10716:10720]

            ln_ready = layer_norm(htok, x_res, x_ready)
            turned = to_features(htok, ln_ready)
            t_ia = []
            for c, (o, w) in enumerate(TOK_CHUNKS):
                for f in range(2):
                    b = bank()
                    t = PE.do(group(psum[:, b, 0:w], [(w_ip[:, k, f * 128:(f + 1) * 128], hT[:, k, o:o + w])
                                                      for k in range(KD)]), turned, wb_in, bank_free[b])
                    bank_free[b] = SC.do(lambda e, o=o, w=w, f=f, b=b: e.activation(
                        actsT[:, f, o:o + w], psum[:, b, 0:w], ACT.Gelu), t, t_var)
                    t_ia.append(bank_free[b])
            it = [{} for _ in range(NT)]

            def process(i):
                me, r = it[i], i % 3
                for half_ in range(2):
                    b = bank()
                    t = PE.do(group(psum[0:TP, b, :], [(actsT[:, k, i * TP:(i + 1) * TP],
                                                        w_pi[:, k, half_ * 512:(half_ + 1) * 512]) for k in range(2)]),
                              t_ia, bank_free[b])
                    bank_free[b] = me["acts"] = SC.do(lambda e, b=b, half_=half_: e.activation(
                        ring3[:, r, half_ * 512:(half_ + 1) * 512], psum[0:TP, b, :], ACT.Gelu), t, adj_over,
                        it[i - 3]["weights"] if i >= 3 else None)

            def choose(i):
                me, r, q = it[i], i % 3, i % 2
                acts, rest = ring3[:, r, :], work[:, q, :]
                src, t = acts, me["acts"]
                for n in range(K_PROC // 8):
                    top = best[:, 2 * q + n % 2, :]
                    t = DVE.do(lambda e, top=top, src=src: e.max(top, src), t)
                    if n == 0:
                        t_neg = DVE.do(lambda e, top=top: e.tensor_scalar(negm[:, q:q + 1], top[:, 0:1], -1.0, None,
                                                                         ALU.mult), t)
                        t_exp = SC.do(lambda e: e.activation(wexp[:, q, :], acts, ACT.Exp, bias=negm[:, q:q + 1]), t_neg,
                                      it[i - 2]["turned"] if i >= 2 else None)
                    t = DVE.do(lambda e, top=top, src=src: e.match_replace(rest, top, src, REPLACED), t)
                    src = rest
                me["weights"] = DVE.do(lambda e: e.scalar_tensor_tensor(
                    wexp[:, q, :], rest, REPLACED, wexp[:, q, :], ALU.is_equal, ALU.mult, accum_out=wsum[:, q:q + 1]),
                    t, t_exp)
                me["sum"] = DVE.do(lambda e: e.reciprocal(wsum[:, 2 + q:3 + q], wsum[:, q:q + 1]), me["weights"],
                                   it[i - 2]["agg"] if i >= 2 else None)

            def values(i):
                me, q = it[i], i % 2
                for g in range(2):
                    b = bank()

                    def fn(e, g=g, b=b):
                        for k in range(4):
                            c = (4 * g + k) * 128
                            ins = e.transpose(psum[:, b, k * TP:(k + 1) * TP], wexp[:, q, c:c + 128], ident[0:TP, 0:TP])
                        return ins
                    me["turned"] = t = PE.do(fn, me["weights"], bank_free[b])
                    t_w = bank_free[b] = SC.do(lambda e, g=g, b=b: e.copy(
                        wT[:, q, 4 * g:4 * g + 4, :], psum[:, b, 0:4 * TP].rearrange("p (k n) -> p k n", k=4)), t,
                        it[i - 2]["aggp"] if i >= 2 else None)
                b = bank()
                me["aggp"] = PE.do(group(psum[0:TP, b, 0:D_PV], [(wT[:, q, k, :], w_pv[:, k, :]) for k in range(8)]),
                                   t_w, d_in, bank_free[b])
                me["agg"] = bank_free[b] = SC.do(lambda e, b=b: e.activation(
                    agg[:, q, :], psum[0:TP, b, 0:D_PV], ACT.Copy, scale=wsum[:, 2 + q:3 + q]), me["aggp"], me["sum"])
                b = bank()

                def fn_t(e, b=b):
                    for k in range(2):
                        ins = e.transpose(psum[:, b, k * TP:(k + 1) * TP], agg[:, q, k * 128:(k + 1) * 128],
                                          ident[0:TP, 0:TP])
                    return ins
                t = PE.do(fn_t, me["agg"], bank_free[b])
                t = bank_free[b] = SC.do(lambda e, b=b: e.copy(
                    aggT[:, q], psum[:, b, 0:2 * TP].rearrange("p (k n) -> p k n", k=2)), t)
                b = bank()

                def fn_o(e, b=b):
                    for f in range(2):
                        for k in range(2):
                            ins = e.matmul(psum[:, b, f * TP:(f + 1) * TP], w_oi_r[:, k, f * 128:(f + 1) * 128],
                                           aggT[:, q, k, :], start=(k == 0), stop=(k == 1))
                    return ins
                t = PE.do(fn_o, t, bank_free[b])
                t = bank_free[b] = SC.do(lambda e, b=b: e.activation(
                    outT[:, q], psum[:, b, 0:2 * TP].rearrange("p (k n) -> p k n", k=2), ACT.Gelu), t)
                b = me["bank"] = bank()
                me["out"] = PE.do(group(psum[0:TP, b, :], [(outT[:, q, k, :], w_op[:, k, :]) for k in range(2)]), t,
                                  bank_free[b])
                bank_free[b] = me["out"]

            ld_out = landing("out")
            o_dram = a["out"].rearrange("(t p) d -> t p d", p=TP)

            def finish(i):
                b = it[i]["bank"]
                t = bank_free[b] = DVE.do(lambda e: e.tensor_tensor(x_res[:, i, :], x_res[:, i, :], psum[0:TP, b, :],
                                                                    ALU.add), it[i]["out"])
                ld_out.dma(SP, o_dram[i], x_res[:, i, :], t)
            pipeline(NT, process, choose, values, finish)
            SP.wait((ld_out.sem, ld_out.total))
        else:
            ld_out = landing("out")
            o_dram = a["out"].rearrange("(t p) d -> p t d", p=TP)
            SP.wait(x_ready)
            ld_out.dma(SP, o_dram[0:112], x_res[0:112])
            SP.wait(ld_out.dma(SP, o_dram[112:TP], x_res[112:TP]))

        block = ctx.enter_context(nc.Block())
        block.sync(SP.run)
        block.gpsimd(POOL.run)
        block.scalar(SC.run)
        block.vector(DVE.run)
        block.tensor(PE.run)


def by_blocks(w):
    import numpy as np
    k = w.shape[0] // 128
    return np.ascontiguousarray(w.reshape(k, 128, -1).transpose(1, 0, 2)).reshape(128, -1)


def host_arrays(inputs):
    import numpy as np
    g = {k: np.asarray(v) for k, v in inputs.items()}
    out = {"x": g["x"], "L0_gnn_bs": g["L0_gnn_bs"].reshape(1, N_GNN, D)}
    for n in ("src", "dst"):
        out[n] = np.ascontiguousarray(g[n].reshape(ECH, TP).T)
    out["w_gnn"] = np.concatenate([by_blocks(g[n][l]) for l in range(N_GNN)
                                   for n in ("L0_gnn_Ws_self", "L0_gnn_Ws_neigh")], axis=1)
    out["w_shared"] = np.concatenate([by_blocks(g["L0_ffn_shared_gate_up"].T), by_blocks(g["L0_ffn_shared_down"].T)],
                                     axis=1)
    out["w_expert"] = np.stack([np.concatenate([by_blocks(gu.T), by_blocks(dn.T)], axis=1)
                                for gu, dn in zip(g["L0_ffn_expert_gate_up"], g["L0_ffn_expert_down"])])
    out["L0_ffn_gate_w"] = by_blocks(g["L0_ffn_gate_w"].T)
    out["L0_ffn_expert_bias"] = g["L0_ffn_expert_bias"]
    out["w_qkv"] = np.concatenate([by_blocks(g[n]) for n in ("L1_gnn_Wq", "L1_gnn_Wk", "L1_gnn_Wv")], axis=1)
    out["w_last"] = np.concatenate([by_blocks(w) for w in (
        g["L1_gnn_Wo"], g["L1_ffn_process_input_weights"].T, g["L1_ffn_input_patterns"].T,
        g["L1_ffn_output_patterns"])], axis=1)
    out["w_values"] = by_blocks(g["L1_ffn_process_values"])
    out["w_oi"] = by_blocks(g["L1_ffn_output_input_weights"].T)
    out["projT"] = np.ascontiguousarray(g["L1_gnn_proj"].T)
    for n in ("L1_gnn_norm1_g", "L1_gnn_norm1_b"):
        out[n] = np.ascontiguousarray(g[n].reshape(KD, 128).T)
    for n in ("L1_gnn_b_conv", "L1_gnn_norm2_g", "L1_gnn_norm2_b"):
        out[n] = g[n]
    out["L1_gnn_W_conv"] = by_blocks(g["L1_gnn_W_conv"])
    return out


def kernel(**inputs):
    import numpy as np
    import concourse.bacc as bacc
    from concourse.bass_utils import run_bass_kernel_spmd

    nc = bacc.Bacc("TRN2", target_bir_lowering=False, num_devices=1)
    arrays = host_arrays(inputs)
    aps = {n: nc.dram_tensor(n, list(v.shape), mybir.dt.from_np(v.dtype), kind="ExternalInput").ap()
           for n, v in arrays.items()}
    aps["out"] = nc.dram_tensor("out", [N_TOK, D], F32, kind="ExternalOutput").ap()
    build(nc, aps)
    r = run_bass_kernel_spmd(nc, [arrays], core_ids=[0])
    return np.asarray(r.results[0]["out"])
```

```python
from contextlib import ExitStack

import concourse.bass as bass
import concourse.mybir as mybir

F32 = mybir.dt.float32
BF16 = mybir.dt.bfloat16
FP16 = mybir.dt.float16
I32 = mybir.dt.int32
U32 = mybir.dt.uint32
ALU = mybir.AluOpType
ACT = mybir.ActivationFunctionType
AX = mybir.AxisListType

N_TOK, D = 1250, 512
TP = 125
NT = N_TOK // TP
KD = D // 128
TOK_CHUNKS = [(0, 418), (418, 416), (834, 416)]
N_EDGES = 40000
ECH = N_EDGES // TP
RUN = 4
RUNS = ECH // RUN
assert RUNS * RUN == ECH
N_GNN = 3
LN_EPS, BN_EPS = 1e-5, 1e-5
N_EXP, TOP_K, D_FF = 16, 3, 512
SLOTS = 128
MIN_BLOCKS = -(-N_TOK * TOP_K // SLOTS)
MAX_BLOCKS = (N_TOK * TOP_K + N_EXP * SLOTS) // SLOTS
HEADS, DH, M_FEAT, N_DENSE = 8, 64, 256, 256
K_EPS = 1e-6
N_IN, N_PROC, D_PV, N_OUT, K_PROC = 256, 1024, 256, 256, 128
REPLACED = -3.0e38


class Lane:

    def __init__(self, sem):
        self.sem, self.steps, self.count, self.seen = sem, [], 0, {}

    def wait(self, *tokens):
        for t in tokens:
            if t is None:
                continue
            if isinstance(t, list):
                self.wait(*t)
                continue
            sem, value = t
            if self.seen.get(id(sem), 0) < value:
                self.seen[id(sem)] = value
                self.steps.append(lambda e, sem=sem, value=value: e.wait_ge(sem, value))

    def do(self, fn, *tokens):
        self.wait(*tokens)
        self.count += 1
        self.steps.append(lambda e: fn(e).then_inc(self.sem, 1))
        return (self.sem, self.count)

    def raw(self, fn, *tokens):
        self.wait(*tokens)
        self.steps.append(fn)

    def split(self, fn, *tokens):
        self.wait(*tokens)
        self.count += 1
        self.steps.append(fn)
        return (self.sem, self.count)

    def run(self, eng):
        for s in self.steps:
            s(eng)


class Landing:

    def __init__(self, sem):
        self.sem, self.total = sem, 0

    def dma(self, lane, out, in_, *tokens):
        lane.wait(*tokens)
        self.total += 16
        lane.steps.append(lambda e: e.dma_start(out, in_).then_inc(self.sem, 16))
        return (self.sem, self.total)


def build(nc, a, upto=9):
    ctx = ExitStack()
    with ctx:
        def sb(name, shape, dt=F32):
            return ctx.enter_context(nc.sbuf_tensor("sb_" + name, shape, dt))[:]

        def sem(name):
            return ctx.enter_context(nc.semaphore(name))

        PE, DVE, SC, POOL = (Lane(sem("done_" + n)) for n in ("pe", "dve", "act", "pool"))
        SP = Lane(sem("done_sp"))

        def landing(name):
            return Landing(sem("ld_" + name))

        x_res = sb("x_res", [TP, NT, D])
        PITCH = TP + TP % 2
        a_reg = sb("a_reg", [128, NT * NT * PITCH])
        half_a = NT * NT * PITCH // 2
        adj = [part.bitcast(BF16).rearrange("p (s t n) -> p s t n", s=NT, t=NT)
               for part in (a_reg[0:TP, 0:half_a], a_reg[0:TP, half_a:])]
        htok = sb("htok", [TP, NT, D])
        hT = sb("hT", [128, KD, N_TOK])
        z_reg = sb("z_reg", [128, NT * D])
        z_part = [part.rearrange("p (t n) -> p t n", n=D)
                  for part in (z_reg[0:TP, 0:NT * D // 2].bitcast(BF16), z_reg[0:TP, NT * D // 2:].bitcast(BF16))]
        w_reg = sb("w_reg", [128, 2, 6 * 1024])
        w_conv = sb("w_conv", [128, KD, D])
        blk = sb("blk", [128, 3584])
        ident = sb("ident", [128, 128])
        inv_deg = sb("inv_deg", [TP, NT])
        deg3 = sb("deg3", [TP, NT, 3])
        stats = sb("stats", [TP, NT, 6])
        mv = sb("mv", [TP, NT, 2])
        rstd = sb("rstd", [TP, NT])
        eps = sb("eps", [128, 1])
        ones_row = sb("ones_row", [1, TP])
        bias_rows = blk[0:1, 0:N_GNN * D].rearrange("p (l d) -> p l d", d=D)
        tmp = blk[0:TP, 1536:2560].rearrange("p (l d) -> p l d", d=D)

        psum = ctx.enter_context(nc.psum_tensor("psum", [128, 8, 512], F32))
        bank_free = [None] * 8
        turn = [0]

        def bank(lo=0, hi=8):
            b = lo + turn[0] % (hi - lo)
            turn[0] += 1
            return b

        def group(out, pairs):
            def fn(e):
                for n, (l, r) in enumerate(pairs):
                    ins = e.matmul(out, l, r, start=(n == 0), stop=(n == len(pairs) - 1))
                return ins
            return fn

        def pipeline(n, *stages):
            for t in range(n + len(stages) - 1):
                for s in reversed(range(len(stages))):
                    if 0 <= t - s < n:
                        stages[s](t - s)

        ld_x = landing("x")
        x_dram = a["x"].rearrange("(t p) d -> p t d", p=TP)
        ld_x.dma(SP, x_res[0:112], x_dram[0:112])
        x_in = ld_x.dma(SP, x_res[112:TP], x_dram[112:TP])

        src_i = z_reg[0:TP, 0:ECH].bitcast(I32)
        dst_i = z_reg[0:TP, ECH:2 * ECH].bitcast(I32)
        src_f = z_reg[0:TP, 2 * ECH:3 * ECH]
        dst_f = z_reg[0:TP, 3 * ECH:4 * ECH]
        o = 4 * ECH
        node_iota = z_reg[0:TP, o:o + N_TOK // 2].bitcast(FP16)
        o += N_TOK // 2
        hot_src = [z_reg[0:TP, o + j * 625:o + (j + 1) * 625].bitcast(BF16) for j in range(RUN)]
        o += RUN * 625
        hot_dst = [z_reg[0:TP, o + j * 63:o + (j + 1) * 63].bitcast(BF16)[:, 0:TP] for j in range(RUN)]
        o += RUN * 63
        assert o <= NT * D
        spare = htok.rearrange("p t n -> p (t n)")
        w_row = NT * PITCH // 2
        *parts4, lo_junk = (
            spare[:, j * w_row:(j + 1) * w_row].bitcast(BF16).rearrange("p (t n) -> p t n", n=PITCH)[:, :, 0:TP]
            for j in range(5))
        a_parts = [parts4[0:2], parts4[2:4]]
        a_row = spare[:, 5 * w_row:5 * w_row + N_TOK]
        a_row_t = a_row.rearrange("p (t n) -> p t n", n=TP)
        ld_edges = landing("edges")
        ld_edges.dma(SC, src_i, a["src"])
        edges_in = ld_edges.dma(SC, dst_i, a["dst"])

        ld_w0 = landing("w0")
        w_gnn = w_reg.rearrange("p s n -> p (s n)").rearrange("p (m k n) -> p m k n", m=6, k=KD)
        ld_w0.dma(SP, bias_rows[:], a["L0_gnn_bs"])
        w0_in = ld_w0.dma(SP, w_reg.rearrange("p s n -> p (s n)"), a["w_gnn"])
        ld_wc = landing("wc")
        wc_in = ld_wc.dma(SP, w_conv.rearrange("p k n -> p (k n)"), a["L1_gnn_W_conv"])

        sel = sb("sel", [TP, NT, NT], BF16)
        zeros = sb("zeros", [1, 512], BF16)
        ramps = blk[0:NT, 2560:2560 + 2 * RUNS].rearrange("p (a c) -> p a c", a=2)
        t_id0 = POOL.do(lambda e: e.memset(ident, 0.0))
        t_id = POOL.do(lambda e: e.affine_select(out=ident, in_=ident, compare_op=ALU.not_equal, fill=1.0,
                                                 base=0, pattern=[[-1, 128]], channel_multiplier=1), t_id0)
        POOL.do(lambda e: e.iota(node_iota, [[1, N_TOK]], base=0, channel_multiplier=0,
                                 allow_small_or_imprecise_dtypes=True))
        POOL.do(lambda e: e.iota(ramps[:, 0, :], [[1, RUNS]], base=1, channel_multiplier=0,
                                 allow_small_or_imprecise_dtypes=True))
        t_iota = POOL.do(lambda e: e.iota(ramps[:, 1, :], [[-1, RUNS]], base=RUNS, channel_multiplier=0,
                                          allow_small_or_imprecise_dtypes=True))
        ident_b = sb("ident_b", [TP, TP], BF16)
        lo_sum = sb("lo_sum", [TP, NT])
        lo_flag = sb("lo_flag", [1, 1], I32)
        ones_tp = sb("ones_tp", [TP, 1])
        DVE.do(lambda e: e.tensor_copy(ident_b, ident[0:TP, 0:TP]), t_id)
        DVE.do(lambda e: e.memset(ones_tp, 1.0))
        t_c0 = DVE.do(lambda e: e.memset(sel, 0.0))
        sel_flat = sel.rearrange("p a b -> p (a b)")
        DVE.do(lambda e: e.memset(sel_flat[:, 0:NT * NT:NT + 1], 1.0), t_c0)
        DVE.do(lambda e: e.memset(sel_flat[:, NT:NT * NT:NT + 1], -1.0))
        DVE.do(lambda e: e.memset(zeros, 0.0))
        DVE.do(lambda e: e.memset(ones_row, 1.0))
        t_const = DVE.do(lambda e: e.memset(eps, LN_EPS))

        DVE.do(lambda e: e.tensor_copy(src_f, src_i), edges_in)
        t_dst = DVE.do(lambda e: e.tensor_copy(dst_f, dst_i))
        ge = htok[:, 0:4, :].rearrange("p a b -> p (a b)").bitcast(BF16)[:, 0:NT * ECH].rearrange(
            "p (b c) -> p b c", c=ECH)
        for b in range(NT):
            t_ge = DVE.do(lambda e, b=b: e.tensor_scalar(ge[:, b, :], dst_f, float(TP * b), None, ALU.is_ge), t_dst)
        t_cnt = PE.do(group(psum[0:NT, 6, 0:ECH], [(sel[:, b, :], ge[:, b, :]) for b in range(NT)]), t_ge, t_const)
        has = blk[0:NT, 2880:3200].rearrange("p (c a) -> p c a", a=RUN)
        span = blk[0:NT, 3200:3200 + 2 * RUNS].rearrange("p (a c) -> p a c", a=2)
        reach = sb("reach", [NT, 2])
        span_i = sb("span_i", [NT, 2], I32)
        t = DVE.do(lambda e: e.tensor_copy(has.rearrange("p c a -> p (c a)"), psum[0:NT, 6, 0:ECH]), t_cnt)
        bank_free[6] = t
        for j in range(1, RUN):
            t = DVE.do(lambda e, j=j: e.tensor_tensor(has[:, :, 0], has[:, :, 0], has[:, :, j], ALU.add), t)
        t = DVE.do(lambda e: e.tensor_scalar(has[:, :, 0], has[:, :, 0], 1.0, None, ALU.min), t)
        DVE.do(lambda e: e.tensor_tensor(span[:, 0, :], has[:, :, 0], ramps[:, 0, :], ALU.mult), t, t_iota)
        t = DVE.do(lambda e: e.tensor_tensor(span[:, 1, :], has[:, :, 0], ramps[:, 1, :], ALU.mult))
        t = DVE.do(lambda e: e.tensor_reduce(reach, span, AX.X, ALU.max), t)
        t = DVE.do(lambda e: e.tensor_scalar(span[:, 1, 0:1], reach[:, 1:2], -1.0, float(RUNS), ALU.mult, ALU.add), t)
        t = DVE.do(lambda e: e.tensor_scalar(span[:, 1, 0:1], span[:, 1, 0:1], float(RUNS - 1), None, ALU.min), t)
        DVE.do(lambda e: e.tensor_copy(span_i[:, 0:1], span[:, 1, 0:1]), t)
        t = DVE.do(lambda e: e.tensor_tensor(span[:, 0, 0:1], reach[:, 0:1], span[:, 1, 0:1], ALU.subtract), t)
        t_span = DVE.do(lambda e: e.tensor_scalar(span_i[:, 1:2], span[:, 0, 0:1], 1.0, None, ALU.max), t)

        def layer_norm(dst, src, ready):
            for i in range(NT):
                t = DVE.do(lambda e, i=i: e.bn_stats(stats[:, i, :], src[:, i, :]), ready[i])
            for i in range(NT):
                t2 = DVE.do(lambda e, i=i: e.bn_aggr(mv[:, i, :], stats[:, i, :]), t)
            t = SC.do(lambda e: e.activation(rstd, mv[:, :, 1], ACT.Sqrt, bias=eps[0:TP, :]), t2, t_const)
            t = DVE.do(lambda e: e.reciprocal(rstd, rstd), t)
            return [DVE.do(lambda e, i=i: e.tensor_scalar(dst[:, i, :], src[:, i, :], mv[:, i, 0:1],
                                                          rstd[:, i:i + 1], ALU.subtract, ALU.mult), t)
                    for i in range(NT)]

        def to_features(src, ready, free=None, relu=False, banks=(0, 8), engines=None):
            out = []
            for i in range(NT):
                out.append(turn_tile(src, i, ready[i], free, relu, banks))
            return out

        def turn_tile(src, i, ready, free, relu, banks=(0, 8), row=None):
            b = bank(*banks)
            row = i if row is None else row

            def fn(e):
                for k in range(KD):
                    ins = e.transpose(psum[:, b, k * TP:(k + 1) * TP], src[:, row, k * 128:(k + 1) * 128],
                                      ident[0:TP, 0:TP])
                return ins
            t = PE.do(fn, ready, bank_free[b], t_id)
            view = psum[:, b, 0:KD * TP].rearrange("p (k n) -> p k n", k=KD)
            dst = hT[:, :, i * TP:(i + 1) * TP]
            if relu:
                t = SC.do(lambda e: e.activation(dst, view, ACT.Relu), t, free)
            else:
                t = SC.do(lambda e: e.copy(dst, view), t, free)
            bank_free[b] = t
            return t

        s_hot, s_used = sem("hot_ready"), sem("hot_used")

        def build_bucket_dve(e, b, state):
            first = e.value_load(span_i[b:b + 1, 0:1], min_val=0, max_val=RUNS - 1)
            number = e.value_load(span_i[b:b + 1, 1:2], min_val=1, max_val=RUNS)
            before = state.get("turns", 0)
            with e.Fori(0, number) as i:
                run = e.bass.s_assert_within(
                    first + i, 0, RUNS - 1,
                    skip_runtime_bounds_check_because="first + number <= RUNS by their computation")
                for j in range(RUN):
                    chunk = run * RUN + j
                    e.wait_ge(s_used, (before + i) * RUN + (j + 1))
                    e.tensor_scalar(hot_dst[j], node_iota[:, b * TP:(b + 1) * TP],
                                    dst_f[:, bass.ds(chunk, 1)], None, ALU.is_equal)
                    e.tensor_scalar(hot_src[j], node_iota, src_f[:, bass.ds(chunk, 1)], None,
                                    ALU.is_equal).then_inc(s_hot, 1)
            state["turns"] = e.snap(before + number)

        def build_bucket_pe(e, b, state, pb):
            number = e.value_load(span_i[b:b + 1, 1:2], min_val=1, max_val=RUNS)
            before = state.get("turns", 0)
            if b == 0:
                e.sem_inc(s_used, RUN)
            for n, (o, w) in enumerate(TOK_CHUNKS):
                e.matmul(psum[0:TP, pb + n, 0:w], zeros[0:1, 0:TP], zeros[0:1, 0:w], start=True, stop=False,
                         skip_group_check=True)
            with e.Fori(0, number) as i:
                for j in range(RUN):
                    e.wait_ge(s_hot, (before + i) * RUN + (j + 1))
                    for n, (o, w) in enumerate(TOK_CHUNKS):
                        ins = e.matmul(psum[0:TP, pb + n, 0:w], hot_dst[j], hot_src[j][:, o:o + w],
                                       start=False, stop=False, skip_group_check=True)
                    ins.then_inc(s_used, 1)
            state["turns"] = e.snap(before + number)
            for n, (o, w) in enumerate(TOK_CHUNKS):
                ins = e.matmul(psum[0:TP, pb + n, 0:w], zeros[0:1, 0:TP], zeros[0:1, 0:w], start=False, stop=True,
                               skip_group_check=True)
            return ins

        ln_ready = layer_norm(htok, x_res, [[x_in, t_cnt]] * NT)
        dve_state, pe_state = {}, {}
        row_free, parts_free = [None], [None, None]
        adj_done = []

        def bucket_sum(b):
            pb = 3 * (b % 2)
            DVE.raw(lambda e: build_bucket_dve(e, b, dve_state), t_span, t_iota)
            t = PE.do(lambda e: build_bucket_pe(e, b, pe_state, pb), t_span, t_const,
                      [bank_free[pb + n] for n in range(3)])
            summed[b] = t

        def bucket_out(b):
            pb = 3 * (b % 2)
            t = summed[b]
            SC.wait(row_free[0], turned)
            for n, (o, w) in enumerate(TOK_CHUNKS):
                t2 = SC.do(lambda e, n=n, o=o, w=w: e.activation(a_row[:, o:o + w], psum[0:TP, pb + n, 0:w], ACT.Copy,
                                                                accum_out=deg3[:, b, n:n + 1]), t)
            for n in range(3):
                bank_free[pb + n] = t2
            t_hi = SC.do(lambda e: e.copy(a_parts[b % 2][0], a_row_t), t2, parts_free[b % 2])
            row_free[0] = rows[b] = POOL.do(lambda e: e.tensor_tensor(a_parts[b % 2][1], a_row_t, a_parts[b % 2][0], ALU.subtract), t_hi)
            rows[b] = [t_hi, rows[b]]
            SC.do(lambda e: e.activation(lo_junk, a_parts[b % 2][1], ACT.Square, accum_out=lo_sum[:, b:b + 1]), rows[b])

        rows, summed = {}, {}

        def bucket_turn(b):
            for part in range(2):
                for s0 in range(0, NT, 8):
                    ns = min(8, NT - s0)
                    q = 6 + turn[0] % 2
                    turn[0] += 1
                    out = psum[0:TP, q, :].bitcast(BF16)

                    def fn(e, part=part, s0=s0, ns=ns, out=out):
                        for s in range(ns):
                            ins = e.transpose(out[:, s * PITCH:s * PITCH + TP], a_parts[b % 2][part][:, s0 + s, :], ident_b)
                        return ins
                    t = PE.do(fn, rows[b], bank_free[q], t_const)
                    bank_free[q] = SC.do(lambda e, part=part, s0=s0, ns=ns, out=out: e.copy(
                        adj[part][:, s0:s0 + ns, b, 0:TP],
                        out[:, 0:ns * PITCH].rearrange("p (s n) -> p s n", n=PITCH)[:, :, 0:TP]), t)
            parts_free[b % 2] = t
            adj_done.append(bank_free[q])

        turned = to_features(htok, ln_ready)
        pipeline(NT, bucket_sum, bucket_out, bucket_turn)
        t = DVE.do(lambda e: e.tensor_reduce(inv_deg, deg3, AX.X, ALU.add), adj_done[-1])
        t = DVE.do(lambda e: e.tensor_scalar(inv_deg, inv_deg, 1.0, None, ALU.max), t)
        t_inv = DVE.do(lambda e: e.reciprocal(inv_deg, inv_deg), t)
        t = DVE.do(lambda e: e.tensor_reduce(lo_sum[:, 0:1], lo_sum, AX.X, ALU.add), adj_done[-1])
        t = PE.do(lambda e: e.matmul(psum[0:1, 6, 0:1], lo_sum[:, 0:1], ones_tp, start=True, stop=True), t,
                  bank_free[6])
        t_flag = bank_free[6] = DVE.do(lambda e: e.tensor_scalar(lo_flag, psum[0:1, 6, 0:1], 1.0, None, ALU.min), t)
        big = {}

        def load_flag(e):
            big["flag"] = e.value_load(lo_flag[0:1, 0:1], min_val=0, max_val=1)
        PE.raw(load_flag, t_flag)

        def z_tiles(w, ready, free, third, diff):
            out, diff_free = [], [None, None]
            parts = z_part + [third]
            for i in range(NT):
                b = bank()
                t = PE.do(group(psum[0:TP, b, :], [(hT[:, k, i * TP:(i + 1) * TP], w[:, k, :]) for k in range(KD)]),
                          ready[i], bank_free[b])
                d = diff[:, i % 2, :]
                t = SC.do(lambda e, i=i, b=b: e.copy(parts[0][:, i, :], psum[0:TP, b, :]), t, free)
                t = bank_free[b] = DVE.do(lambda e, i=i, b=b, d=d: e.tensor_tensor(
                    d, psum[0:TP, b, :], parts[0][:, i, :], ALU.subtract), t, diff_free[i % 2])
                t = DVE.do(lambda e, i=i, d=d: e.tensor_copy(parts[1][:, i, :], d), t)
                t = diff_free[i % 2] = POOL.do(lambda e, i=i, d=d: e.tensor_tensor(
                    parts[2][:, i, :], d, parts[1][:, i, :], ALU.subtract), t)
                out.append(t)
            return out, parts

        def neighbours(out, parts, i, *tokens):
            def pairs(adj_parts):
                return [(a_part[:, s, i, 0:TP], z_[:, s, :])
                        for a_part in adj_parts for s in range(NT) for z_ in parts]

            def fn(e):
                with e.If(big["flag"] > 0):
                    group(out, pairs(adj))(e).then_inc(PE.sem, 1)
                with e.Else():
                    group(out, pairs(adj[:1]))(e).then_inc(PE.sem, 1)
            return PE.split(fn, *tokens)

        h_ready, z_free, self_free = turned, adj_done[-1], [None, None]
        PE.wait(w0_in)
        htok_third = htok[:, 5:NT, :].rearrange("p t n -> p (t n)").bitcast(BF16).rearrange("p (t n) -> p t n", n=D)
        for l in range(N_GNN):
            w_self, w_neigh = w_gnn[:, 2 * l], w_gnn[:, 2 * l + 1]
            z_ready, parts = z_tiles(w_neigh, h_ready, z_free, htok_third, htok[:, 3:5, :])
            last = l == N_GNN - 1
            new = {}

            def sums(i):
                bs, bn = bank(), bank()
                t_s = PE.do(group(psum[0:TP, bs, :], [(hT[:, k, i * TP:(i + 1) * TP], w_self[:, k, :])
                                                      for k in range(KD)] + [(ones_row, bias_rows[:, l, :])]),
                            bank_free[bs])
                t_n = neighbours(psum[0:TP, bn, :], parts, i, z_ready, bank_free[bn])
                r = i % 3
                t = SC.do(lambda e: e.copy(tmp[:, i % 2, :], psum[0:TP, bs, :]), t_s, self_free[i % 2])
                bank_free[bs] = t
                t = DVE.do(lambda e: e.scalar_tensor_tensor(htok[:, r, :], psum[0:TP, bn, :], inv_deg[:, i:i + 1],
                                                            tmp[:, i % 2, :], ALU.mult, ALU.add), t, t_n, t_inv,
                           new.get(i - 3))
                bank_free[bn] = self_free[i % 2] = t
                if last:
                    t = DVE.do(lambda e: e.tensor_tensor(x_res[:, i, :], x_res[:, i, :], htok[:, r, :], ALU.add), t)
                new[i] = t

            def turns(i):
                new[i] = turn_tile(htok, i, new[i], None, True, row=i % 3)

            if last:
                pipeline(NT, sums)
            else:
                pipeline(NT, sums, turns)
            h_ready = [new[i] for i in range(NT)]
            z_free = (PE.sem, PE.count)
        x_ready = h_ready
        t_l0 = (PE.sem, PE.count)

        if upto >= 2:
            def expert_views(slot):
                w = w_reg[:, slot, :]
                return (w[:, 0:4096].rearrange("p (k n) -> p k n", k=KD),
                        w[:, 4096:6144].rearrange("p (k n) -> p k n", k=KD))
            ld_slot = [landing("slot0"), landing("slot1")]
            shared_in = ld_slot[1].dma(SP, w_reg[:, 1, :], a["w_shared"], t_l0)
            slot_in = {0: ld_slot[0].dma(SP, w_reg[:, 0, :], a["w_expert"][0], t_l0)}

            gate_w = sb("gate_w", [128, KD, N_EXP])
            bias16 = blk[0:TP, 0:16]
            ld_r = landing("router")
            ld_r.dma(SC, gate_w.rearrange("p k n -> p (k n)"), a["L0_ffn_gate_w"])
            router_in = ld_r.dma(SC, bias16, a["L0_ffn_expert_bias"].partition_broadcast(TP), t_l0)

            ln_ready = layer_norm(htok, x_res, x_ready)
            turned = to_features(htok, ln_ready)

            rows_dram = nc.dram_tensor("rows", [N_TOK, D], F32).ap()
            list_dram = nc.dram_tensor("slot_tokens", [MAX_BLOCKS * SLOTS, 1], I32).ap()
            outs_dram = nc.dram_tensor("slot_outs", [MAX_BLOCKS * SLOTS, D], F32).ap()
            ld_rows = landing("rows")
            r_view = rows_dram.rearrange("(t p) d -> p t d", p=TP)
            ld_rows.dma(SC, r_view[0:112], htok[0:112], ln_ready)
            rows_out = ld_rows.dma(SC, r_view[112:TP], htok[112:TP])
            rt = blk[0:TP, 16:16 + 2400]
            zero_list = blk[:, 2600:2600 + MAX_BLOCKS].bitcast(I32)
            t = DVE.do(lambda e: e.memset(zero_list, 0), t_l0)
            ld_list = landing("list")
            list_zero = ld_list.dma(SC, list_dram.rearrange("(p c) o -> p (c o)", p=128), zero_list, t)

            zero_rows = blk[:, 2660:3172]
            t = DVE.do(lambda e: e.memset(zero_rows, 0.0), t_l0)
            ld_fill = landing("fill")
            spare = MAX_BLOCKS - MIN_BLOCKS
            outs_filled = ld_fill.dma(SC, outs_dram[MIN_BLOCKS * SLOTS:, :].rearrange("(b p) d -> p b d", p=SLOTS),
                                      zero_rows.unsqueeze(1).to_broadcast([128, spare, D]), t)

            def small(n, w=N_EXP * NT):
                return rt[:, n * w:(n + 1) * w]

            def by_tile(v):
                return v.rearrange("p (t n) -> p t n", t=NT)
            aff, score, hot, prod = (by_tile(small(n)) for n in (0, 1, 2, 3))
            ones_hot = [by_tile(small(4 + k)) for k in range(TOP_K)]
            exp_iota, rank = by_tile(small(7)), by_tile(small(8))
            top8 = small(9)[:, 0:8 * NT].rearrange("p (t n) -> p t n", t=NT)
            top8_i = small(10)[:, 0:8 * NT].bitcast(U32).rearrange("p (t n) -> p t n", t=NT)
            top8_f = small(11)[:, 0:8 * NT].rearrange("p (t n) -> p t n", t=NT)
            sel_aff = small(12)[:, 0:TOP_K * NT].rearrange("p (t n) -> p t n", t=NT)
            gating = sb("gating", [TP, NT, TOP_K])
            slot_f = small(13)[:, 0:TOP_K * NT].rearrange("p (t n) -> p t n", t=NT)
            slot_i = sb("slot_i", [TP, TOP_K, NT], I32)
            tok_id = sb("tok_id", [TP, NT], I32)
            picked = sb("picked", [TP, NT, N_EXP], BF16)
            before = sb("before", [TP, TP], BF16)
            ones_b = sb("ones_b", [TP, 128], BF16)
            n_blk_i = sb("n_blk_i", [128, N_EXP + 1], I32)
            n_blk_f = sb("n_blk_f", [128, N_EXP])
            base_f = sb("base_f", [128, N_EXP])
            one16 = sb("one16", [128, N_EXP])

            POOL.do(lambda e: e.iota(exp_iota, [[0, NT], [1, N_EXP]], base=0, channel_multiplier=0,
                                     allow_small_or_imprecise_dtypes=True), t_l0)
            t_tok = POOL.do(lambda e: e.iota(tok_id, [[TP, NT]], base=0, channel_multiplier=1))
            t = POOL.do(lambda e: e.memset(before, 1.0))
            t_lt = POOL.do(lambda e: e.affine_select(out=before, in_=before, compare_op=ALU.is_gt, fill=0.0, base=0,
                                                     pattern=[[1, TP]], channel_multiplier=-1), t)
            DVE.do(lambda e: e.memset(one16, 1.0))
            t_ones = DVE.do(lambda e: e.memset(ones_b, 1.0))

            lb = bank()

            def logits(e):
                for i in range(NT):
                    for k in range(KD):
                        ins = e.matmul(psum[0:TP, lb, i * N_EXP:(i + 1) * N_EXP], hT[:, k, i * TP:(i + 1) * TP],
                                       gate_w[:, k, :], start=(k == 0), stop=(k == KD - 1))
                return ins
            t = PE.do(logits, turned, router_in, bank_free[lb])
            t = SC.do(lambda e: e.activation(aff, psum[0:TP, lb, 0:NT * N_EXP].rearrange("p (t n) -> p t n", t=NT),
                                             ACT.Sigmoid), t, t_l0)
            bank_free[lb] = t
            t = DVE.do(lambda e: e.tensor_tensor(score, aff, bias16.unsqueeze(1).to_broadcast([TP, NT, N_EXP]),
                                                 ALU.add), t, router_in)
            for i in range(NT):
                t2 = DVE.do(lambda e, i=i: e.max(top8[:, i, :], score[:, i, :]), t)
            for i in range(NT):
                t = DVE.do(lambda e, i=i: e.max_index(top8_i[:, i, :], top8[:, i, :], score[:, i, :]), t2)
            t_top = DVE.do(lambda e: e.tensor_copy(top8_f, top8_i), t)
            for k in range(TOP_K):
                t = DVE.do(lambda e, k=k: e.tensor_tensor(
                    ones_hot[k], exp_iota, top8_f[:, :, k:k + 1].to_broadcast([TP, NT, N_EXP]), ALU.is_equal),
                    t_top, t_tok)
                t2 = DVE.do(lambda e, k=k: e.tensor_tensor(prod, ones_hot[k], aff, ALU.mult), t)
                t2 = DVE.do(lambda e, k=k: e.tensor_reduce(sel_aff[:, :, k], prod, AX.X, ALU.add), t2)
            denom = small(12)[:, 40:40 + NT]
            t2 = DVE.do(lambda e: e.tensor_reduce(denom, sel_aff, AX.X, ALU.add), t2)
            t2 = DVE.do(lambda e: e.tensor_scalar(denom, denom, 1e-9, None, ALU.add), t2)
            t2 = DVE.do(lambda e: e.reciprocal(denom, denom), t2)
            t_gate = DVE.do(lambda e: e.tensor_tensor(
                gating, sel_aff, denom.unsqueeze(2).to_broadcast([TP, NT, TOP_K]), ALU.mult), t2)
            t = DVE.do(lambda e: e.tensor_tensor(hot, ones_hot[0], ones_hot[1], ALU.add), t)
            t = DVE.do(lambda e: e.tensor_tensor(picked, hot, ones_hot[2], ALU.add), t)

            rb = bank()

            def ranks(e):
                for i in range(NT):
                    for j in range(i + 1):
                        e.matmul(psum[0:TP, rb, i * N_EXP:(i + 1) * N_EXP], before if j == i else ones_b[:, 0:TP],
                                 picked[:, j, :], start=(j == 0), stop=(j == i))
                for j in range(NT):
                    ins = e.matmul(psum[:, rb, 256:256 + N_EXP], ones_b, picked[:, j, :],
                                   start=(j == 0), stop=(j == NT - 1))
                return ins
            t_rank = PE.do(ranks, t, t_lt, t_ones, bank_free[rb])
            t = DVE.do(lambda e: e.tensor_scalar(n_blk_i[:, 0:N_EXP], psum[:, rb, 256:256 + N_EXP],
                                                 float(SLOTS - 1), float(SLOTS), ALU.add, ALU.max), t_rank)
            t = DVE.do(lambda e: e.tensor_single_scalar(n_blk_i[:, 0:N_EXP], n_blk_i[:, 0:N_EXP],
                                                        SLOTS.bit_length() - 1, ALU.arith_shift_right), t)
            t = DVE.do(lambda e: e.tensor_copy(n_blk_f, n_blk_i[:, 0:N_EXP]), t)
            t = DVE.do(lambda e: e.tensor_tensor_scan(base_f, one16, n_blk_f, 0.0, ALU.mult, ALU.add), t)
            t_nblk = DVE.do(lambda e: e.tensor_copy(n_blk_i[:, N_EXP:N_EXP + 1], base_f[:, N_EXP - 1:N_EXP]), t)
            t = DVE.do(lambda e: e.tensor_tensor(base_f, base_f, n_blk_f, ALU.subtract), t_nblk)
            t = DVE.do(lambda e: e.tensor_scalar(base_f, base_f, float(SLOTS), None, ALU.mult), t)
            t = DVE.do(lambda e: e.tensor_tensor(
                rank, psum[0:TP, rb, 0:NT * N_EXP].rearrange("p (t n) -> p t n", t=NT),
                base_f[0:TP].unsqueeze(1).to_broadcast([TP, NT, N_EXP]), ALU.add), t)
            bank_free[rb] = t
            for k in range(TOP_K):
                t = DVE.do(lambda e, k=k: e.tensor_tensor(prod, ones_hot[k], rank, ALU.mult), t)
                t = DVE.do(lambda e, k=k: e.tensor_reduce(slot_f[:, :, k], prod, AX.X, ALU.add), t)
                t = DVE.do(lambda e, k=k: e.tensor_copy(slot_i[:, k, :], slot_f[:, :, k]), t)
            t_slot = t

            ld_scatter = landing("scatter")
            for i in range(NT):
                for k in range(TOP_K):
                    POOL.wait(t_slot, t_tok, list_zero)
                    ld_scatter.total += 16
                    POOL.steps.append(lambda e, i=i, k=k: e.indirect_dma_start(
                        list_dram, bass.IndirectOffsetOnAxis(ap=slot_i[:, k, i:i + 1], axis=0),
                        tok_id[:, i:i + 1], None).then_inc(ld_scatter.sem, 16))
            list_out = (ld_scatter.sem, ld_scatter.total)

            w_gu, w_dn = expert_views(1)
            hid_s = z_reg[:, 0:KD * N_TOK].rearrange("p (k n) -> p k n", k=KD)
            sil = sb("sil", [128, 2, 418])
            sil_free = [None, None]
            hid_ready = []
            steps = [(c, f) for c in range(len(TOK_CHUNKS)) for f in range(KD)]

            def shared_up(n):
                c, f = steps[n]
                o, w = TOK_CHUNKS[c]
                bg, bu = bank(), bank()
                t_g = PE.do(group(psum[:, bg, 0:w], [(w_gu[:, k, f * 128:(f + 1) * 128], hT[:, k, o:o + w])
                                                     for k in range(KD)]), turned, shared_in, bank_free[bg])
                t_u = PE.do(group(psum[:, bu, 0:w], [(w_gu[:, k, D_FF + f * 128:D_FF + (f + 1) * 128],
                                                      hT[:, k, o:o + w]) for k in range(KD)]), bank_free[bu])
                t = SC.do(lambda e: e.activation(sil[:, n % 2, 0:w], psum[:, bg, 0:w], ACT.Silu), t_g, sil_free[n % 2])
                bank_free[bg] = t
                t = DVE.do(lambda e: e.tensor_tensor(hid_s[:, f, o:o + w], sil[:, n % 2, 0:w], psum[:, bu, 0:w],
                                                     ALU.mult), t, t_u)
                bank_free[bu] = sil_free[n % 2] = t
                hid_ready.append(t)
            for n in range(len(steps)):
                shared_up(n)
            x_ready = []
            for i in range(NT):
                b = bank()
                t = PE.do(group(psum[0:TP, b, :], [(hid_s[:, k, i * TP:(i + 1) * TP], w_dn[:, k, :])
                                                   for k in range(KD)]), hid_ready[-1], bank_free[b])
                bank_free[b] = DVE.do(lambda e, i=i, b=b: e.tensor_tensor(
                    x_res[:, i, :], x_res[:, i, :], psum[0:TP, b, :], ALU.add), t)
                x_ready.append(bank_free[b])
            t_shared = (PE.sem, PE.count)

            xg = blk[:, 0:512]
            xgT = blk[:, 512:1024].rearrange("p (k n) -> p k n", k=KD)
            hid = blk[:, 1024:1536]
            hidT = blk[:, 1536:2048].rearrange("p (k n) -> p k n", k=KD)
            silg = blk[:, 2048:2560].rearrange("p (h n) -> p h n", h=2)
            y_blk = blk[:, 2560:3072]
            idx = blk[:, 3072:3073].bitcast(I32)
            s_idx, s_row, s_out = sem("idx_in"), sem("rows_in"), sem("block_out")
            s_xt, s_xe, s_gu, s_hid, s_ht, s_he, s_dn, s_y = (sem(n) for n in (
                "x_turned", "x_copied", "gate_up", "hidden", "hid_turned", "hid_copied", "down", "y_ready"))
            HF = D_FF // 2

            def row_of(e, g):
                return e.bass.s_assert_within(
                    g, 0, MAX_BLOCKS - 1,
                    skip_runtime_bounds_check_because="the experts' blocks are at most MAX_BLOCKS in all") * SLOTS

            def loops(e, body, before_expert=None, after_expert=None):
                done = 0
                for x in range(N_EXP):
                    if before_expert:
                        before_expert(e, x)
                    number = e.value_load(n_blk_i[0:1, x:x + 1], min_val=1, max_val=10)
                    with e.Fori(0, number) as i:
                        body(e, x, done + i)
                    done = e.snap(done + number)
                    if after_expert:
                        after_expert(e, x)
                return done

            s_pass = sem("gather_may_go")

            def pool_blocks(e):
                total = e.value_load(n_blk_i[0:1, N_EXP:N_EXP + 1], min_val=N_EXP, max_val=MAX_BLOCKS)
                with e.Fori(0, total) as g:
                    e.wait_ge(s_xt, g + 1)
                    e.dma_start(idx, list_dram[bass.ds(row_of(e, g), SLOTS), :]).then_inc(s_idx, 16)
                    e.wait_ge(s_idx, g * 16 + 16)
                    e.sem_inc(s_pass, 1)
                    e.indirect_dma_start(xg, None, rows_dram,
                                         bass.IndirectOffsetOnAxis(ap=idx, axis=0)).then_inc(s_row, 16)
            POOL.raw(pool_blocks, t_nblk, list_out, rows_out, t_rank, t_shared, outs_filled, list_zero)

            def pe_block(e, x, g):
                w_gu, w_dn = expert_views(x % 2)
                e.wait_ge(s_row, g * 16 + 16)
                for k in range(KD):
                    ins = e.transpose(psum[:, 0, k * 128:(k + 1) * 128], xg[:, k * 128:(k + 1) * 128], ident)
                ins.then_inc(s_xt, 1)
                e.wait_ge(s_xe, g + 1)
                e.wait_ge(s_hid, g * 2 + 2)
                for h in range(2):
                    for part in range(2):
                        for k in range(KD):
                            c = part * D_FF + h * HF
                            ins = e.matmul(psum[:, 1 + h, part * HF:(part + 1) * HF], xgT[:, k, :],
                                           w_gu[:, k, c:c + HF], start=(k == 0), stop=(k == KD - 1))
                    ins.then_inc(s_gu, 1)
                for h in range(2):
                    e.wait_ge(s_hid, g * 2 + h + 3)
                    if h == 0:
                        e.wait_ge(s_he, g * 2 + 2)
                    for k in range(2):
                        ins = e.transpose(psum[:, 3 + h, k * 128:(k + 1) * 128],
                                          hid[:, h * HF + k * 128:h * HF + (k + 1) * 128], ident)
                    ins.then_inc(s_ht, 1)
                e.wait_ge(s_y, g + 1)
                for k in range(KD):
                    if k % 2 == 0:
                        e.wait_ge(s_he, g * 2 + k // 2 + 3)
                    ins = e.matmul(psum[:, 5, :], hidT[:, k, :], w_dn[:, k, :], start=(k == 0), stop=(k == KD - 1))
                ins.then_inc(s_dn, 1)

            def act_block(e, x, g):
                e.wait_ge(s_xt, g + 2)
                e.copy(xgT.rearrange("p k n -> p (k n)"), psum[:, 0, :]).then_inc(s_xe, 1)
                for h in range(2):
                    e.wait_ge(s_gu, g * 2 + h + 1)
                    e.activation(silg[:, h, :], psum[:, 1 + h, 0:HF], ACT.Silu).then_inc(s_sil, 1)
                e.wait_ge(s_dn, g + 1)
                e.wait_ge(s_out, g * 16 + 16)
                e.copy(y_blk, psum[:, 5, :]).then_inc(s_y, 1)
            s_sil = sem("silu")

            def dve_block(e, x, g):
                for h in range(2):
                    e.wait_ge(s_sil, g * 2 + h + 1)
                    e.tensor_tensor(hid[:, h * HF:(h + 1) * HF], silg[:, h, :], psum[:, 1 + h, HF:2 * HF],
                                    ALU.mult).then_inc(s_hid, 1)
                for h in range(2):
                    e.wait_ge(s_ht, g * 2 + h + 1)
                    e.tensor_copy(hidT[:, 2 * h:2 * h + 2, :].rearrange("p k n -> p (k n)"),
                                  psum[:, 3 + h, 0:256]).then_inc(s_he, 1)

            def sp_block(e, x, g):
                e.wait_ge(s_y, g + 2)
                e.dma_start(outs_dram[bass.ds(row_of(e, g), SLOTS), :], y_blk).then_inc(s_out, 16)

            PE.wait(bank_free, t_nblk)
            s_exp = sem("expert_done")

            def weights_ready(e, x):
                e.wait_ge(ld_slot[x % 2].sem, slot_need[x])

            slot_need = {0: 16}
            for x in range(1, N_EXP):
                slot_need[x] = slot_need.get(x - 2, 16) + 16 if x > 1 else 32

            def load_next(e, x):
                if x + 1 < N_EXP:
                    if x >= 1:
                        e.wait_ge(s_exp, x)
                    e.dma_start(w_reg[:, (x + 1) % 2, :], a["w_expert"][x + 1]).then_inc(
                        ld_slot[(x + 1) % 2].sem, 16)

            def pe_all(e):
                done = 0
                for x in range(N_EXP):
                    weights_ready(e, x)
                    number = e.value_load(n_blk_i[0:1, x:x + 1], min_val=1, max_val=10)
                    with e.Fori(0, number) as i:
                        pe_block(e, x, done + i)
                    done = e.snap(done + number)
                    ins = e.matmul(psum[0:1, 6, 0:2], ident[:, 0:1], ident[:, 0:2], start=True, stop=True)
                    ins.then_inc(s_exp, 1)
                return e.matmul(psum[0:1, 6, 0:2], ident[:, 0:1], ident[:, 0:2], start=True, stop=True)
            t_pe_moe = PE.do(pe_all)
            SC.raw(lambda e: loops(e, act_block), t_nblk, t_shared, bank_free, outs_filled)
            DVE.raw(lambda e: loops(e, dve_block), t_nblk, t_shared, bank_free)
            SP.wait(t_nblk, t_shared, outs_filled)

            def sp_all(e):
                for s, n in ((s_xt, 1), (s_hid, 2), (s_he, 2), (s_y, 1), (s_out, 16)):
                    e.sem_inc(s, n)
                g = loops(e, sp_block, load_next)
                e.wait_ge(s_out, g * 16 + 16)
                return e.sem_inc(stored, 1)
            stored = sem("blocks_stored")
            SP.raw(sp_all)
            for ld, x in ((ld_slot[0], N_EXP - 2), (ld_slot[1], N_EXP - 1)):
                ld.total = slot_need[x]
            t_stored = (stored, 1)

            ring = z_reg[0:TP, :].rearrange("p (r n) -> p r n", n=D)
            RING = NT
            ld_take = [landing(f"take{r}") for r in range(RING)]
            ring_free = [t_shared] * RING
            for i in range(NT):
                for k in range(TOP_K):
                    r = (i * TOP_K + k) % RING
                    POOL.wait(t_stored, ring_free[r])
                    ld_take[r].total += 16
                    POOL.steps.append(lambda e, i=i, k=k, r=r: e.indirect_dma_start(
                        ring[:, r, :], None, outs_dram,
                        bass.IndirectOffsetOnAxis(ap=slot_i[:, k, i:i + 1], axis=0)).then_inc(ld_take[r].sem, 16))
                    x_ready[i] = ring_free[r] = DVE.do(lambda e, i=i, k=k, r=r: e.scalar_tensor_tensor(
                        x_res[:, i, :], ring[:, r, :], gating[:, i, k:k + 1], x_res[:, i, :], ALU.mult, ALU.add),
                        (ld_take[r].sem, ld_take[r].total), x_ready[i], t_gate)
            bank_free[:] = [t_pe_moe] * 8

        if upto >= 3:
            ld_a, ld_b, ld_c = landing("qkv"), landing("slot_b"), landing("norms")
            experts_over = t_pe_moe
            qkv_in = ld_a.dma(SP, w_reg[:, 0, :], a["w_qkv"], (s_exp, N_EXP - 1))
            wb_in = ld_b.dma(SP, w_reg[:, 1, :], a["w_last"], experts_over)
            w_q, w_k, w_v = (w_reg[:, 0, n * 2048:(n + 1) * 2048].rearrange("p (k n) -> p k n", k=KD) for n in range(3))
            w_o = w_reg[:, 1, 0:2048].rearrange("p (k n) -> p k n", k=KD)
            rows3 = blk[0:TP, 0:1536].rearrange("p (m d) -> p m d", d=D)
            attn = blk[:, 1536:2560].rearrange("p (t d) -> p t d", d=D)
            projT = blk[:, 2560:2816]
            kv = blk[:, 2816:3076].rearrange("p (r m d) -> p r m d", r=2, m=2)
            mean_w = blk[0:TP, 3076:3201]
            half = blk[:, 3201:3202]
            s3 = blk[:, 3202:3500]
            blk_over = [x_ready[-1], t_stored, (POOL.sem, POOL.count), t_pe_moe]
            for n, name in enumerate(("L1_gnn_b_conv", "L1_gnn_norm2_g", "L1_gnn_norm2_b")):
                ld_c.dma(SP, rows3[:, n, :], a[name].partition_broadcast(TP), blk_over)
            n1 = sb("n1", [128, 2, KD])
            ld_c.dma(SP, n1[:, 0, :], a["L1_gnn_norm1_g"])
            ld_c.dma(SP, n1[:, 1, :], a["L1_gnn_norm1_b"])
            for h in range(2):
                norms_in = ld_c.dma(SP, projT[h * 64:h * 64 + 64, :], a["projT"])
            DVE.do(lambda e: e.memset(mean_w, 1.0 / N_TOK), blk_over)
            t_half = DVE.do(lambda e: e.memset(half, 0.5))

            ln_ready = layer_norm(htok, x_res, x_ready)
            turned = to_features(htok, ln_ready)

            qk = [z_reg[:, n * 1024:(n + 1) * 1024].rearrange("p (f n) -> p f n", f=KD) for n in range(2)]
            qf = z_reg[:, 2048:3072].rearrange("p (r t m) -> p r t m", r=2, t=2)
            kf = z_reg[:, 3072:4096].rearrange("p (r t m) -> p r t m", r=2, t=2)
            qfT = z_reg[:, 4096:4608].rearrange("p (m n) -> p m n", m=2)
            v_ext = w_reg[:, 0, 0:1040].rearrange("p (t h d) -> p t h d", t=2, h=HEADS)
            attnT = w_reg[:, 0, 2048:4048].rearrange("p (k n) -> p k n", k=KD)
            sq = [w_reg[:, 0, 4096 + n * 1024:5120 + n * 1024].rearrange("p (f n) -> p f n", f=KD) for n in range(2)]
            h_attn = w_reg[0:TP, 0, 0:2048].rearrange("p (t d) -> p t d", d=D)
            scale = DH ** -0.25
            t_qk = []
            for n, w in enumerate((w_q, w_k)):
                for f2 in range(2):
                    b = bank()

                    def fn(e, w=w, f2=f2, b=b):
                        for f in range(2):
                            for k in range(KD):
                                c = (f2 * 2 + f) * 128
                                ins = e.matmul(psum[:, b, f * 256:(f + 1) * 256], w[:, k, c:c + 128], hT[:, k, 0:N_DENSE],
                                               start=(k == 0), stop=(k == KD - 1))
                        return ins
                    t = PE.do(fn, turned[2], qkv_in, bank_free[b])
                    bank_free[b] = SC.do(lambda e, n=n, f2=f2, b=b: e.mul(
                        qk[n][:, 2 * f2:2 * f2 + 2, :].rearrange("p f n -> p (f n)"), psum[:, b, :], scale), t,
                        x_ready[-1])
                    t_qk.append(bank_free[b])
            t_v = []
            for s in range(2):
                b = bank()
                t = PE.do(group(psum[:, b, :], [(hT[:, k, s * 128:(s + 1) * 128], w_v[:, k, :]) for k in range(KD)]),
                          bank_free[b])
                t_v.append((s, b, t))
            t_qkv = t
            for s, b, t in t_v:
                bank_free[b] = DVE.do(lambda e, s=s, b=b: e.tensor_copy(
                    v_ext[:, s, :, 0:DH], psum[:, b, :].rearrange("p (h d) -> p h d", h=HEADS)), t, t_qkv)
            t_vx = DVE.do(lambda e: e.memset(v_ext[:, :, :, DH:DH + 1], 1.0), t_qkv)
            t_sq = [SC.do(lambda e, n=n: e.square(sq[n], qk[n]), t_qk, t_qkv) for n in range(2)]
            diag = s3[:, 0:32].rearrange("p (q t h) -> p q t h", q=2, t=2)
            db = [bank(), bank()]

            def diags(e):
                for odd in range(2):
                    rows = slice(64 * odd, 64 * odd + 64)
                    for n in range(2):
                        for s in range(2):
                            for f in range(KD):
                                c = (n * 2 + s) * KD + f
                                ins = e.matmul(psum[:, db[odd], c:c + 1], sq[n][rows, f, s * 128:(s + 1) * 128],
                                               half[rows, :], start=True, stop=True)
                return ins
            t = PE.do(diags, t_sq, t_half, bank_free[db[0]], bank_free[db[1]])
            for odd in range(2):
                t_diag = bank_free[db[odd]] = DVE.do(lambda e, odd=odd: e.tensor_copy(
                    diag[:, :, :, odd:HEADS:2].rearrange("p q t h -> p (q t) h"),
                    psum[:, db[odd], 0:4 * KD].rearrange("p (q h) -> p q h", h=KD)), t, blk_over)

            def features(n, h, b):
                rows = slice(64 * (h % 2), 64 * (h % 2) + 64)

                def fn(e):
                    for s in range(2):
                        ins = e.matmul(psum[:, b, s * 256:(s + 1) * 256], qk[n][rows, h // 2, s * 128:(s + 1) * 128],
                                       projT[rows, :], start=True, stop=True)
                    return ins
                return PE.do(fn, t_qk, norms_in, bank_free[b])

            k_max = s3[:, 32:40]
            for h in range(HEADS):
                b = bank()
                t = features(1, h, b)
                t_km = bank_free[b] = DVE.do(lambda e, h=h, b=b: e.reduce_max(k_max[:, h:h + 1], psum[:, b, :], AX.X),
                                             t, blk_over)
            b = bank()
            t = PE.do(lambda e, b=b: e.transpose(psum[0:HEADS, b, 0:128], k_max, ident), t_km, bank_free[b])
            k_max8, k_diag = s3[0:HEADS, 40:41], s3[0:HEADS, 41:49]
            t = bank_free[b] = DVE.do(lambda e, b=b: e.reduce_max(k_max8, psum[0:HEADS, b, 0:128], AX.X), t)
            t = DVE.do(lambda e: e.tensor_scalar(k_diag, ident[0:HEADS, 0:HEADS], k_max8, None, ALU.mult), t)
            ones8 = s3[0:HEADS, 49:177]
            t2 = DVE.do(lambda e: e.memset(ones8, 1.0), blk_over)
            b = bank()
            t = PE.do(lambda e, b=b: e.matmul(psum[:, b, 0:HEADS], ones8, k_diag, start=True, stop=True), t, t2,
                      bank_free[b])
            k_bias = s3[:, 180:196].rearrange("p (t h) -> p t h", t=2)
            for s in range(2):
                t_kb = DVE.do(lambda e, s=s, b=b: e.scalar_tensor_tensor(
                    k_bias[:, s, :], diag[:, 1, s, :], -1.0, psum[:, b, 0:HEADS], ALU.mult, ALU.subtract), t, t_diag)
            bank_free[b] = t_kb
            q_max = s3[:, 196:212].rearrange("p (t h) -> p t h", t=2)
            q_bias = s3[:, 212:228].rearrange("p (t h) -> p t h", t=2)
            rden = s3[:, 228:244].rearrange("p (t h) -> p t h", t=2)
            inv_root_m = M_FEAT ** -0.5
            head = [{} for _ in range(HEADS)]
            attn_done = []

            def head_features(h):
                r, me = h % 2, head[h]
                bk, bq = bank(), bank()
                t_k, t_q = features(1, h, bk), features(0, h, bq)
                for s in range(2):
                    t = SC.do(lambda e, s=s: e.activation(kf[:, r, s, :], psum[:, bk, s * 256:(s + 1) * 256], ACT.Exp,
                                                          bias=k_bias[:, s, h:h + 1]), t_k, t_kb,
                              head[h - 2].get("kv") if h >= 2 else None)
                bank_free[bk] = t
                me["kf"] = DVE.do(lambda e: e.tensor_scalar(kf[:, r], kf[:, r], inv_root_m, K_EPS, ALU.mult, ALU.add), t)
                t = DVE.do(lambda e: e.tensor_reduce(q_max[:, :, h], psum[:, bq, :].rearrange("p (t m) -> p t m", t=2),
                                                     AX.X, ALU.max), t_q)
                t = DVE.do(lambda e: e.scalar_tensor_tensor(q_bias[:, :, h], diag[:, 0, :, h], -1.0, q_max[:, :, h],
                                                            ALU.mult, ALU.subtract), t, t_diag)
                for s in range(2):
                    t2 = SC.do(lambda e, s=s: e.activation(qf[:, r, s, :], psum[:, bq, s * 256:(s + 1) * 256], ACT.Exp,
                                                           bias=q_bias[:, s, h:h + 1]), t,
                               head[h - 2].get("turned") if h >= 2 else None)
                bank_free[bq] = t2
                me["qf"] = DVE.do(lambda e: e.tensor_scalar(qf[:, r], qf[:, r], inv_root_m, K_EPS, ALU.mult, ALU.add), t2)

            def head_products(h):
                r, me = h % 2, head[h]
                b = bank()

                def fn_kv(e):
                    for m in range(2):
                        for s in range(2):
                            ins = e.matmul(psum[:, b, m * 65:(m + 1) * 65], kf[:, r, s, m * 128:(m + 1) * 128],
                                           v_ext[:, s, h, :], start=(s == 0), stop=(s == 1))
                    return ins
                me["kv"] = PE.do(fn_kv, me["kf"], t_vx, bank_free[b])
                t_kv = bank_free[b] = DVE.do(lambda e: e.tensor_copy(
                    kv[:, r].rearrange("p m d -> p (m d)"), psum[:, b, 0:130]), me["kv"],
                    head[h - 2].get("out") if h >= 2 else None)
                bt = bank()

                def fn_t(e):
                    for m in range(2):
                        for s in range(2):
                            ins = e.transpose(psum[:, bt, m * 256 + s * 128:m * 256 + (s + 1) * 128],
                                              qf[:, r, s, m * 128:(m + 1) * 128], ident)
                    return ins
                me["turned"] = PE.do(fn_t, me["qf"], bank_free[bt])
                t_q = bank_free[bt] = SC.do(lambda e: e.copy(qfT.rearrange("p m n -> p (m n)"), psum[:, bt, :]),
                                            me["turned"], head[h - 1].get("out") if h >= 1 else None)
                bo = bank()

                def fn_o(e):
                    for s in range(2):
                        for m in range(2):
                            ins = e.matmul(psum[:, bo, s * 65:(s + 1) * 65], qfT[:, m, s * 128:(s + 1) * 128],
                                           kv[:, r, m, :], start=(m == 0), stop=(m == 1))
                    return ins
                me["out"] = PE.do(fn_o, t_q, t_kv, bank_free[bo])
                out = psum[:, bo, 0:130].rearrange("p (t d) -> p t d", t=2)
                t = DVE.do(lambda e: e.tensor_scalar(rden[:, :, h], out[:, :, DH], K_EPS, None, ALU.add), me["out"])
                t = DVE.do(lambda e: e.reciprocal(rden[:, :, h], rden[:, :, h]), t)
                for s in range(2):
                    t2 = DVE.do(lambda e, s=s: e.tensor_scalar(attn[:, s, h * DH:(h + 1) * DH], out[:, s, 0:DH],
                                                               rden[:, s, h:h + 1], None, ALU.mult), t)
                bank_free[bo] = t2
                attn_done.append(t2)
            pipeline(HEADS, head_features, head_products)

            for s in range(2):
                b = bank()

                def fn(e, s=s, b=b):
                    for k in range(KD):
                        ins = e.transpose(psum[:, b, k * 128:(k + 1) * 128], attn[:, s, k * 128:(k + 1) * 128], ident)
                    return ins
                t = PE.do(fn, attn_done[-1], bank_free[b])
                t = bank_free[b] = DVE.do(lambda e, s=s, b=b: e.tensor_copy(
                    attnT[:, :, s * 128:(s + 1) * 128], psum[:, b, :].rearrange("p (k n) -> p k n", k=KD)), t, t_qkv)
            t_at = DVE.do(lambda e: e.tensor_copy(attnT[:, :, N_DENSE:4 * TP],
                                                  attnT[:, :, N_DENSE - 1:N_DENSE].to_broadcast([128, KD, 4 * TP - N_DENSE])), t)
            for i in range(4):
                b = bank()
                t = PE.do(group(psum[0:TP, b, :], [(attnT[:, k, i * TP:(i + 1) * TP], w_o[:, k, :]) for k in range(KD)]),
                          t_at, wb_in, bank_free[b])
                t_wo = t
                t_ha = bank_free[b] = SC.do(lambda e, i=i, b=b: e.copy(h_attn[:, i, :], psum[0:TP, b, :]), t,
                                            head[HEADS - 1]["out"])

            bst = s3[:, 0:72].rearrange("p (k c s) -> p k c s", k=KD, c=3)
            bmv = s3[:, 72:80].rearrange("p (k s) -> p k s", k=KD)
            bsc, bsh = s3[:, 80:84], s3[:, 84:88]
            for k in range(KD):
                for c, (o, w) in enumerate(TOK_CHUNKS):
                    t = DVE.do(lambda e, k=k, c=c, o=o, w=w: e.bn_stats(bst[:, k, c, :], hT[:, k, o:o + w]), turned,
                               attn_done)
            for k in range(KD):
                t2 = DVE.do(lambda e, k=k: e.bn_aggr(bmv[:, k, :], bst[:, k].rearrange("p c s -> p (c s)")), t)
            t = SC.do(lambda e: e.activation(bsc, bmv[:, :, 1], ACT.Sqrt, bias=eps), t2)
            t = DVE.do(lambda e: e.reciprocal(bsc, bsc), t)
            t = DVE.do(lambda e: e.tensor_tensor(bsc, bsc, n1[:, 0, :], ALU.mult), t, norms_in)
            t = DVE.do(lambda e: e.tensor_tensor(bsh, bmv[:, :, 0], bsc, ALU.mult), t)
            t = DVE.do(lambda e: e.tensor_tensor(bsh, n1[:, 1, :], bsh, ALU.subtract), t)
            for k in range(KD):
                t_xn = DVE.do(lambda e, k=k: e.tensor_scalar(hT[:, k, :], hT[:, k, :], bsc[:, k:k + 1],
                                                             bsh[:, k:k + 1], ALU.mult, ALU.add), t, t_qkv)

            ctmp = w_reg[0:TP, 0, 5120:6144].rearrange("p (r d) -> p r d", r=2)
            conv_third = w_reg[0:TP, 0, 2048:2048 + NT * D // 2].bitcast(BF16).rearrange("p (t n) -> p t n", n=D)
            z_ready, parts = z_tiles(w_conv, [[t_xn, wc_in]] * NT, t_wo, conv_third, ctmp)
            y_ready, ct_free = [], [None, None]
            for i in range(NT):
                b = bank()
                t = neighbours(psum[0:TP, b, :], parts, i, z_ready, bank_free[b])
                t = bank_free[b] = DVE.do(lambda e, i=i, b=b: e.scalar_tensor_tensor(
                    ctmp[:, i % 2, :], psum[0:TP, b, :], inv_deg[:, i:i + 1], rows3[:, 0, :], ALU.mult, ALU.add), t,
                    t_ha, norms_in)
                t = DVE.do(lambda e, i=i: e.scalar_tensor_tensor(
                    ctmp[:, i % 2, :], ctmp[:, i % 2, :], 0.0, h_attn[:, min(i, 3), :], ALU.max, ALU.add), t)
                y_ready.append(DVE.do(lambda e, i=i: e.tensor_tensor(htok[:, i, :], htok[:, i, :], ctmp[:, i % 2, :],
                                                                     ALU.add), t))
            adj_over = (PE.sem, PE.count)

            def token_mean(src, ready):
                b = bank()
                t = None
                for i in range(NT):
                    t = PE.do(lambda e, i=i: e.matmul(psum[0:TP, b, :], mean_w, src(i), start=(i == 0),
                                                      stop=(i == NT - 1)), ready[i], bank_free[b])
                return b, t
            bm, t_mean = token_mean(lambda i: htok[:, i, :], y_ready)
            c_ready, s_ready = [], []
            squares = a_reg[0:TP, 0:NT * D].rearrange("p (t n) -> p t n", n=D)
            for i in range(NT):
                c_ready.append(DVE.do(lambda e, i=i: e.tensor_tensor(htok[:, i, :], htok[:, i, :], psum[0:TP, bm, :],
                                                                     ALU.subtract), t_mean))
                s_ready.append(SC.do(lambda e, i=i: e.square(squares[:, i, :], htok[:, i, :]), c_ready[i], adj_over))
            bank_free[bm] = c_ready[-1]
            bv, t_var = token_mean(lambda i: squares[:, i, :], s_ready)
            sc2 = ctmp[:, 0, :]
            t = bank_free[bv] = SC.do(lambda e: e.activation(sc2, psum[0:TP, bv, :], ACT.Sqrt, bias=eps[0:TP, :]),
                                      t_var, y_ready)
            t = DVE.do(lambda e: e.reciprocal(sc2, sc2), t)
            t_sc = DVE.do(lambda e: e.tensor_tensor(sc2, sc2, rows3[:, 1, :], ALU.mult), t)
            x_ready = []
            for i in range(NT):
                t = POOL.do(lambda e, i=i: e.tensor_tensor(x_res[:, i, :], x_res[:, i, :], rows3[:, 2, :], ALU.add),
                            t_sc)
                t2 = DVE.do(lambda e, i=i: e.tensor_tensor(htok[:, i, :], htok[:, i, :], sc2, ALU.mult), t_sc, s_ready)
                x_ready.append(DVE.do(lambda e, i=i: e.tensor_tensor(x_res[:, i, :], x_res[:, i, :], htok[:, i, :],
                                                                     ALU.add), t, t2))

        if upto >= 4:
            ld_d = landing("values")
            w_pv = w_conv.rearrange("p k n -> p (k n)").rearrange("p (k n) -> p k n", n=D_PV)
            t_zc = (PE.sem, PE.count)
            ld_d.dma(SP, w_conv.rearrange("p k n -> p (k n)"), a["w_values"], t_zc)
            w_oi_flat = z_reg[:, 2500:3012]
            w_oi_r = w_oi_flat.rearrange("p (k n) -> p k n", k=2)
            d_in = ld_d.dma(SP, w_oi_flat, a["w_oi"], t_var)
            w_pi = w_reg[:, 1, 2048:4096].rearrange("p (k n) -> p k n", k=2)
            w_ip = w_reg[:, 1, 4096:5120].rearrange("p (k n) -> p k n", k=KD)
            w_op = w_reg[:, 1, 5120:6144].rearrange("p (k n) -> p k n", k=2)
            actsT = z_reg[:, 0:2 * N_TOK].rearrange("p (k n) -> p k n", k=2)
            acts = a_reg[0:TP, 0:NT * N_PROC].rearrange("p (t n) -> p t n", n=N_PROC)
            wexp = a_reg[0:TP, 10240:12288].rearrange("p (r n) -> p r n", r=2)
            rest = htok.rearrange("p t n -> p (t n)")[:, 0:2048].rearrange("p (r n) -> p r n", r=2)
            junk = htok.rearrange("p t n -> p (t n)")[:, 2048:4096].rearrange("p (r n) -> p r n", r=2)
            hT_flat = hT.rearrange("p k n -> p (k n)")
            wT = hT_flat[:, 0:2000].rearrange("p (r k n) -> p r k n", r=2, k=8)
            agg = hT_flat[0:TP, 2000:2512].rearrange("p (r n) -> p r n", r=2)
            aggT = hT_flat[:, 2512:3012].rearrange("p (r k n) -> p r k n", r=2, k=2)
            outT = hT_flat[:, 3012:3512].rearrange("p (r k n) -> p r k n", r=2, k=2)
            ch = blk[0:TP, 0:400]
            act_sum = ch[:, 0:2 * NT].rearrange("p (t h) -> p t h", h=2)
            thr, step, cnt, left, cut, cut_cnt, x_max, neg_max, bad, w_sum, w_inv = (
                ch[:, (2 + n) * NT:(3 + n) * NT] for n in range(11))
            cand = ch[:, 150:150 + 17 * NT].rearrange("p (t n) -> p t n", n=17)
            iota17 = ch[:, 330:347]
            bad_i = blk[0:1, 400:400 + NT].bitcast(I32)
            ones_col = blk[0:TP, 420:421]
            top_s = blk[0:TP, 424:432]

            ln_ready = layer_norm(htok, x_res, x_ready)
            turned = to_features(htok, ln_ready)
            t_ia = []
            for c, (o, w) in enumerate(TOK_CHUNKS):
                for f in range(2):
                    b = bank()
                    t = PE.do(group(psum[:, b, 0:w], [(w_ip[:, k, f * 128:(f + 1) * 128], hT[:, k, o:o + w])
                                                      for k in range(KD)]), turned, wb_in, bank_free[b])
                    bank_free[b] = SC.do(lambda e, o=o, w=w, f=f, b=b: e.activation(
                        actsT[:, f, o:o + w], psum[:, b, 0:w], ACT.Gelu), t, t_var)
                    t_ia.append(bank_free[b])
            it = [{} for _ in range(NT)]
            t_blk3 = DVE.do(lambda e: e.memset(ones_col, 1.0), x_ready)
            t_17 = POOL.do(lambda e: e.iota(iota17, [[1, 17]], base=0, channel_multiplier=0,
                                            allow_small_or_imprecise_dtypes=True), x_ready)

            GUESS = 1.17 / (N_PROC * 0.39894)
            AIM = K_PROC - 8
            SLOPE = 1.17 * N_PROC * 0.2059

            def process(i):
                me = it[i]
                for h in range(2):
                    b = bank()
                    t = PE.do(group(psum[0:TP, b, :], [(actsT[:, k, i * TP:(i + 1) * TP],
                                                        w_pi[:, k, h * 512:(h + 1) * 512]) for k in range(2)]),
                              t_ia, bank_free[b])
                    bank_free[b] = me["acts"] = SC.do(lambda e, b=b, h=h: e.activation(
                        acts[:, i, h * 512:(h + 1) * 512], psum[0:TP, b, :], ACT.Gelu,
                        accum_out=act_sum[:, i, h:h + 1]), t, adj_over, t_blk3)
                me["max"] = DVE.do(lambda e: e.tensor_reduce(x_max[:, i:i + 1], acts[:, i, :], AX.X, ALU.max),
                                   me["acts"])
            for i in range(NT):
                process(i)

            BY_ACT = NT // 2

            def counts(ready):
                done = []
                for i in range(NT):
                    j = junk[:, 0, :] if i >= BY_ACT else junk[:, 1, :]
                    if i < BY_ACT:
                        done.append(SC.do(lambda e, i=i, j=j: e.activation(
                            j, acts[:, i, :], ACT.Sign, bias=thr[:, i:i + 1], scale=-1.0,
                            accum_out=cnt[:, i:i + 1]), ready, (SC.sem, SC.count)))
                for i in range(BY_ACT, NT):
                    done.append(DVE.do(lambda e, i=i, j=junk[:, 0, :]: e.tensor_scalar(
                        j, acts[:, i, :], thr[:, i:i + 1], None, ALU.is_ge, ALU.add,
                        accum_out=cnt[:, i:i + 1]), ready, it[i]["acts"], (DVE.sem, DVE.count)))
                return DVE.do(lambda e: e.tensor_scalar(cnt[:, 0:BY_ACT], cnt[:, 0:BY_ACT], -0.5, N_PROC / 2,
                                                        ALU.mult, ALU.add), done)
            last_acts = it[NT - 1]["acts"]
            t = DVE.do(lambda e: e.tensor_reduce(thr, act_sum, AX.X, ALU.add), last_acts)
            t = DVE.do(lambda e: e.tensor_scalar(thr, thr, GUESS, None, ALU.mult), t)
            t_step = DVE.do(lambda e: e.tensor_scalar(step, thr, 0.8 / SLOPE, None, ALU.mult), t)
            for n in range(2):
                t = counts(t)
                t = DVE.do(lambda e: e.scalar_tensor_tensor(cnt, cnt, -float(AIM), step, ALU.add, ALU.mult), t, t_step)
                t = DVE.do(lambda e: e.tensor_tensor(thr, thr, cnt, ALU.add), t)
            t = counts(t)
            DVE.do(lambda e: e.tensor_copy(cand[:, :, 0], thr), t)
            t_left = DVE.do(lambda e: e.tensor_scalar(left, cnt, -1.0, float(K_PROC), ALU.mult, ALU.add), t)
            t_nm = DVE.do(lambda e: e.tensor_scalar(neg_max, x_max, -1.0, None, ALU.mult), it[NT - 1]["max"])
            s_w, s_gen = sem("weights"), sem("general")

            def choose(i):
                me, q = it[i], i % 2
                me["exp"] = SC.do(lambda e: e.activation(wexp[:, q, :], acts[:, i, :], ACT.Exp,
                                                         bias=neg_max[:, i:i + 1]), t_nm,
                                  it[i - 2]["turned"] if i >= 2 else None)
                r = rest[:, q, :]
                t = DVE.do(lambda e: e.scalar_tensor_tensor(r, acts[:, i, :], thr[:, i:i + 1], acts[:, i, :],
                                                            ALU.is_lt, ALU.mult), t_left,
                           it[i - 2]["weights"] if i >= 2 else None)
                t = DVE.do(lambda e: e.max(cand[:, i, 1:9], r), t)
                t = DVE.do(lambda e: e.match_replace(r, cand[:, i, 1:9], r, REPLACED), t)
                t = DVE.do(lambda e: e.max(cand[:, i, 9:17], r), t)
                t = DVE.do(lambda e: e.scalar_tensor_tensor(junk[:, 1, 0:17], iota17, left[:, i:i + 1], cand[:, i, :],
                                                            ALU.is_equal, ALU.mult, accum_out=cut[:, i:i + 1]), t, t_17)
                t = DVE.do(lambda e: e.tensor_scalar(junk[:, 0, :], acts[:, i, :], cut[:, i:i + 1], None, ALU.is_ge,
                                                     ALU.add, accum_out=cut_cnt[:, i:i + 1]), t)
                t = DVE.do(lambda e: e.tensor_scalar(bad[:, i:i + 1], cut_cnt[:, i:i + 1], float(K_PROC), None,
                                                     ALU.not_equal), t)
                b = bank()
                t = PE.do(lambda e: e.matmul(psum[0:1, b, 0:1], ones_col, bad[:, i:i + 1], start=True, stop=True), t,
                          bank_free[b])
                bank_free[b] = me["bad"] = SC.do(lambda e: e.copy(bad_i[:, i:i + 1], psum[0:1, b, 0:1]), t)

            def weigh(i):
                me, q = it[i], i % 2
                r, w = rest[:, q, :], wexp[:, q, :]

                def fn(e):
                    failed = e.value_load(bad_i[0:1, i:i + 1], min_val=0, max_val=TP)
                    with e.If(failed > 0):
                        src = acts[:, i, :]
                        for n in range(K_PROC // 8):
                            e.max(top_s, src)
                            e.drain()
                            e.match_replace(r, top_s, src, REPLACED)
                            e.drain()
                            src = r
                        e.scalar_tensor_tensor(w, r, REPLACED, w, ALU.is_equal, ALU.mult,
                                               accum_out=w_sum[:, i:i + 1]).then_inc(s_w, 1)
                    with e.Else():
                        e.scalar_tensor_tensor(w, acts[:, i, :], cut[:, i:i + 1], w, ALU.is_ge, ALU.mult,
                                               accum_out=w_sum[:, i:i + 1]).then_inc(s_w, 1)
                DVE.raw(fn, me["bad"], me["exp"])
                me["weights"] = me["sum"] = DVE.do(lambda e: e.reciprocal(w_inv[:, i:i + 1], w_sum[:, i:i + 1]),
                                                   (s_w, i + 1))

            def values(i):
                me, q = it[i], i % 2
                for g in range(2):
                    b = bank()

                    def fn(e, g=g, b=b):
                        for k in range(4):
                            c = (4 * g + k) * 128
                            ins = e.transpose(psum[:, b, k * TP:(k + 1) * TP], wexp[:, q, c:c + 128], ident[0:TP, 0:TP])
                        return ins
                    me["turned"] = t = PE.do(fn, me["weights"], bank_free[b])
                    t_w = bank_free[b] = SC.do(lambda e, g=g, b=b: e.copy(
                        wT[:, q, 4 * g:4 * g + 4, :], psum[:, b, 0:4 * TP].rearrange("p (k n) -> p k n", k=4)), t,
                        it[i - 2]["aggp"] if i >= 2 else None)
                b = bank()
                me["aggp"] = PE.do(group(psum[0:TP, b, 0:D_PV], [(wT[:, q, k, :], w_pv[:, k, :]) for k in range(8)]),
                                   t_w, d_in, bank_free[b])
                me["agg"] = bank_free[b] = SC.do(lambda e, b=b: e.activation(
                    agg[:, q, :], psum[0:TP, b, 0:D_PV], ACT.Copy, scale=w_inv[:, i:i + 1]), me["aggp"], me["sum"])
                b = bank()

                def fn_t(e, b=b):
                    for k in range(2):
                        ins = e.transpose(psum[:, b, k * TP:(k + 1) * TP], agg[:, q, k * 128:(k + 1) * 128],
                                          ident[0:TP, 0:TP])
                    return ins
                t = PE.do(fn_t, me["agg"], bank_free[b])
                t = bank_free[b] = SC.do(lambda e, b=b: e.copy(
                    aggT[:, q], psum[:, b, 0:2 * TP].rearrange("p (k n) -> p k n", k=2)), t)
                b = bank()

                def fn_o(e, b=b):
                    for f in range(2):
                        for k in range(2):
                            ins = e.matmul(psum[:, b, f * TP:(f + 1) * TP], w_oi_r[:, k, f * 128:(f + 1) * 128],
                                           aggT[:, q, k, :], start=(k == 0), stop=(k == 1))
                    return ins
                t = PE.do(fn_o, t, bank_free[b])
                t = bank_free[b] = SC.do(lambda e, b=b: e.activation(
                    outT[:, q], psum[:, b, 0:2 * TP].rearrange("p (k n) -> p k n", k=2), ACT.Gelu), t)
                b = me["bank"] = bank()
                me["out"] = PE.do(group(psum[0:TP, b, :], [(outT[:, q, k, :], w_op[:, k, :]) for k in range(2)]), t,
                                  bank_free[b])
                bank_free[b] = me["out"]

            ld_out = landing("out")
            o_dram = a["out"].rearrange("(t p) d -> t p d", p=TP)

            def finish(i):
                b = it[i]["bank"]
                t = bank_free[b] = DVE.do(lambda e: e.tensor_tensor(x_res[:, i, :], x_res[:, i, :], psum[0:TP, b, :],
                                                                    ALU.add), it[i]["out"])
                ld_out.dma(SP, o_dram[i], x_res[:, i, :], t)
            pipeline(NT, choose, weigh, values, finish)
            SP.wait((ld_out.sem, ld_out.total))
        else:
            ld_out = landing("out")
            o_dram = a["out"].rearrange("(t p) d -> p t d", p=TP)
            SP.wait(x_ready)
            ld_out.dma(SP, o_dram[0:112], x_res[0:112])
            SP.wait(ld_out.dma(SP, o_dram[112:TP], x_res[112:TP]))

        block = ctx.enter_context(nc.Block())
        block.sync(SP.run)
        block.gpsimd(POOL.run)
        block.scalar(SC.run)
        block.vector(DVE.run)
        block.tensor(PE.run)


def by_blocks(w):
    import numpy as np
    k = w.shape[0] // 128
    return np.ascontiguousarray(w.reshape(k, 128, -1).transpose(1, 0, 2)).reshape(128, -1)


def host_arrays(inputs):
    import numpy as np
    g = {k: np.asarray(v) for k, v in inputs.items()}
    out = {"x": g["x"], "L0_gnn_bs": g["L0_gnn_bs"].reshape(1, N_GNN, D)}
    for n in ("src", "dst"):
        out[n] = np.ascontiguousarray(g[n].reshape(ECH, TP).T)
    out["w_gnn"] = np.concatenate([by_blocks(g[n][l]) for l in range(N_GNN)
                                   for n in ("L0_gnn_Ws_self", "L0_gnn_Ws_neigh")], axis=1)
    out["w_shared"] = np.concatenate([by_blocks(g["L0_ffn_shared_gate_up"].T), by_blocks(g["L0_ffn_shared_down"].T)],
                                     axis=1)
    out["w_expert"] = np.stack([np.concatenate([by_blocks(gu.T), by_blocks(dn.T)], axis=1)
                                for gu, dn in zip(g["L0_ffn_expert_gate_up"], g["L0_ffn_expert_down"])])
    out["L0_ffn_gate_w"] = by_blocks(g["L0_ffn_gate_w"].T)
    out["L0_ffn_expert_bias"] = g["L0_ffn_expert_bias"]
    out["w_qkv"] = np.concatenate([by_blocks(g[n]) for n in ("L1_gnn_Wq", "L1_gnn_Wk", "L1_gnn_Wv")], axis=1)
    out["w_last"] = np.concatenate([by_blocks(w) for w in (
        g["L1_gnn_Wo"], g["L1_ffn_process_input_weights"].T, g["L1_ffn_input_patterns"].T,
        g["L1_ffn_output_patterns"])], axis=1)
    out["w_values"] = by_blocks(g["L1_ffn_process_values"])
    out["w_oi"] = by_blocks(g["L1_ffn_output_input_weights"].T)
    out["projT"] = np.ascontiguousarray(g["L1_gnn_proj"].T)
    for n in ("L1_gnn_norm1_g", "L1_gnn_norm1_b"):
        out[n] = np.ascontiguousarray(g[n].reshape(KD, 128).T)
    for n in ("L1_gnn_b_conv", "L1_gnn_norm2_g", "L1_gnn_norm2_b"):
        out[n] = g[n]
    out["L1_gnn_W_conv"] = by_blocks(g["L1_gnn_W_conv"])
    return out


def kernel(**inputs):
    import numpy as np
    import concourse.bacc as bacc
    from concourse.bass_utils import run_bass_kernel_spmd

    nc = bacc.Bacc("TRN2", target_bir_lowering=False, num_devices=1)
    arrays = host_arrays(inputs)
    aps = {n: nc.dram_tensor(n, list(v.shape), mybir.dt.from_np(v.dtype), kind="ExternalInput").ap()
           for n, v in arrays.items()}
    aps["out"] = nc.dram_tensor("out", [N_TOK, D], F32, kind="ExternalOutput").ap()
    build(nc, aps)
    r = run_bass_kernel_spmd(nc, [arrays], core_ids=[0])
    return np.asarray(r.results[0]["out"])
```

```python
from contextlib import ExitStack

import concourse.bass as bass
import concourse.mybir as mybir

F32 = mybir.dt.float32
BF16 = mybir.dt.bfloat16
FP16 = mybir.dt.float16
I32 = mybir.dt.int32
U32 = mybir.dt.uint32
ALU = mybir.AluOpType
ACT = mybir.ActivationFunctionType
AX = mybir.AxisListType

N_TOK, D = 1250, 512
TP = 125
NT = N_TOK // TP
KD = D // 128
TOK_CHUNKS = [(0, 418), (418, 416), (834, 416)]
N_EDGES = 40000
ECH = N_EDGES // TP
RUN = 4
RUNS = ECH // RUN
assert RUNS * RUN == ECH
N_GNN = 3
NORM_EPS = 1e-5
N_EXP, TOP_K, D_FF = 16, 3, 512
SLOTS = 128
MIN_BLOCKS = -(-N_TOK * TOP_K // SLOTS)
MAX_BLOCKS = (N_TOK * TOP_K + N_EXP * SLOTS) // SLOTS
HEADS, DH, M_FEAT, N_DENSE = 8, 64, 256, 256
K_EPS = 1e-6
N_PROC, D_PV, K_PROC = 1024, 256, 128
REPLACED = -3.0e38


class Lane:

    def __init__(self, sem):
        self.sem, self.steps, self.count, self.seen = sem, [], 0, {}

    def wait(self, *tokens):
        for t in tokens:
            if t is None:
                continue
            if isinstance(t, list):
                self.wait(*t)
                continue
            sem, value = t
            if self.seen.get(id(sem), 0) < value:
                self.seen[id(sem)] = value
                self.steps.append(lambda e, sem=sem, value=value: e.wait_ge(sem, value))

    def do(self, fn, *tokens):
        self.wait(*tokens)
        self.count += 1
        self.steps.append(lambda e: fn(e).then_inc(self.sem, 1))
        return (self.sem, self.count)

    def raw(self, fn, *tokens):
        self.wait(*tokens)
        self.steps.append(fn)

    def split(self, fn, *tokens):
        self.wait(*tokens)
        self.count += 1
        self.steps.append(fn)
        return (self.sem, self.count)

    def run(self, eng):
        for s in self.steps:
            s(eng)


class Landing:

    def __init__(self, sem):
        self.sem, self.total = sem, 0

    def dma(self, lane, out, in_, *tokens):
        lane.wait(*tokens)
        self.total += 16
        lane.steps.append(lambda e: e.dma_start(out, in_).then_inc(self.sem, 16))
        return (self.sem, self.total)


def build(nc, a):
    ctx = ExitStack()
    with ctx:
        def sb(name, shape, dt=F32):
            return ctx.enter_context(nc.sbuf_tensor("sb_" + name, shape, dt))[:]

        def sem(name):
            return ctx.enter_context(nc.semaphore(name))

        PE, DVE, SC, POOL = (Lane(sem("done_" + n)) for n in ("pe", "dve", "act", "pool"))
        SP = Lane(sem("done_sp"))

        def landing(name):
            return Landing(sem("ld_" + name))

        x_res = sb("x_res", [TP, NT, D])
        PITCH = TP + TP % 2
        a_reg = sb("a_reg", [128, NT * NT * PITCH])
        half_a = NT * NT * PITCH // 2
        adj = [part.bitcast(BF16).rearrange("p (s t n) -> p s t n", s=NT, t=NT)
               for part in (a_reg[0:TP, 0:half_a], a_reg[0:TP, half_a:])]
        htok = sb("htok", [TP, NT, D])
        hT = sb("hT", [128, KD, N_TOK])
        z_reg = sb("z_reg", [128, NT * D])
        z_part = [part.rearrange("p (t n) -> p t n", n=D)
                  for part in (z_reg[0:TP, 0:NT * D // 2].bitcast(BF16), z_reg[0:TP, NT * D // 2:].bitcast(BF16))]
        w_reg = sb("w_reg", [128, 2, 6 * 1024])
        w_conv = sb("w_conv", [128, KD, D])
        blk = sb("blk", [128, 3584])
        ident = sb("ident", [128, 128])
        inv_deg = sb("inv_deg", [TP, NT])
        deg3 = sb("deg3", [TP, NT, 3])
        stats = sb("stats", [TP, NT, 6])
        mv = sb("mv", [TP, NT, 2])
        rstd = sb("rstd", [TP, NT])
        eps = sb("eps", [128, 1])
        bias_rows = blk[0:TP, 0:N_GNN * D].rearrange("p (l d) -> p l d", d=D)
        self_sum = blk[0:TP, 1536:2560].rearrange("p (l d) -> p l d", d=D)

        psum = ctx.enter_context(nc.psum_tensor("psum", [128, 8, 512], F32))
        bank_free = [None] * 8
        turn = [0]

        def bank(lo=0, hi=8):
            b = lo + turn[0] % (hi - lo)
            turn[0] += 1
            return b

        def group(out, pairs):
            def fn(e):
                for n, (l, r) in enumerate(pairs):
                    ins = e.matmul(out, l, r, start=(n == 0), stop=(n == len(pairs) - 1))
                return ins
            return fn

        def pipeline(n, *stages, first=0, after=None):
            for t in range(n - first + len(stages) - 1):
                for s in reversed(range(len(stages))):
                    if 0 <= t - s < n - first:
                        stages[s](first + t - s)
                if after:
                    after(t)

        src_i = z_reg[0:TP, 0:ECH].bitcast(I32)
        dst_i = z_reg[0:TP, ECH:2 * ECH].bitcast(I32)
        src_f = z_reg[0:TP, 2 * ECH:3 * ECH]
        dst_f = z_reg[0:TP, 3 * ECH:4 * ECH]
        o = 4 * ECH
        node_iota = z_reg[0:TP, o:o + N_TOK // 2].bitcast(FP16)
        o += N_TOK // 2
        hot_src = [z_reg[0:TP, o + j * 625:o + (j + 1) * 625].bitcast(BF16) for j in range(RUN)]
        o += RUN * 625
        hot_dst = [z_reg[0:TP, o + j * 63:o + (j + 1) * 63].bitcast(BF16)[:, 0:TP] for j in range(RUN)]
        o += RUN * 63
        assert o <= NT * D
        scratch = htok.rearrange("p t n -> p (t n)")
        w_row = NT * PITCH // 2
        *parts4, lo_junk = (
            scratch[:, j * w_row:(j + 1) * w_row].bitcast(BF16).rearrange("p (t n) -> p t n", n=PITCH)[:, :, 0:TP]
            for j in range(5))
        a_parts = [parts4[0:2], parts4[2:4]]
        a_row = scratch[:, 5 * w_row:5 * w_row + N_TOK]
        a_row_t = a_row.rearrange("p (t n) -> p t n", n=TP)
        ld_edges = landing("edges")
        ld_edges.dma(SP, src_i, a["src"])
        edges_in = ld_edges.dma(SP, dst_i, a["dst"])
        ld_x = landing("x")
        x_dram = a["x"].rearrange("(t p) d -> p t d", p=TP)
        ld_x.dma(SP, x_res[0:112], x_dram[0:112])
        x_in = ld_x.dma(SP, x_res[112:TP], x_dram[112:TP])

        ld_w0 = landing("w0")
        w_gnn = w_reg.rearrange("p s n -> p (s n)").rearrange("p (m k n) -> p m k n", m=6, k=KD)
        ld_w0.dma(SP, blk[0:TP, 0:N_GNN * D], a["L0_gnn_bs"].partition_broadcast(TP))
        w0_in = ld_w0.dma(SP, w_reg.rearrange("p s n -> p (s n)"), a["w_gnn"])

        sel = sb("sel", [TP, NT, NT], BF16)
        zeros = sb("zeros", [1, 512], BF16)
        ramps = blk[0:NT, 2560:2560 + 2 * RUNS].rearrange("p (a c) -> p a c", a=2)
        t_id0 = POOL.do(lambda e: e.memset(ident, 0.0))
        t_id = POOL.do(lambda e: e.affine_select(out=ident, in_=ident, compare_op=ALU.not_equal, fill=1.0,
                                                 base=0, pattern=[[-1, 128]], channel_multiplier=1), t_id0)
        POOL.do(lambda e: e.iota(node_iota, [[1, N_TOK]], base=0, channel_multiplier=0,
                                 allow_small_or_imprecise_dtypes=True))
        POOL.do(lambda e: e.iota(ramps[:, 0, :], [[1, RUNS]], base=1, channel_multiplier=0,
                                 allow_small_or_imprecise_dtypes=True))
        t_iota = POOL.do(lambda e: e.iota(ramps[:, 1, :], [[-1, RUNS]], base=RUNS, channel_multiplier=0,
                                          allow_small_or_imprecise_dtypes=True))
        ident_b = sb("ident_b", [TP, TP], BF16)
        lo_sum = sb("lo_sum", [TP, NT])
        lo_flag = sb("lo_flag", [1, 1], I32)
        ones_tp = sb("ones_tp", [TP, 1])
        DVE.do(lambda e: e.tensor_copy(ident_b, ident[0:TP, 0:TP]), t_id)
        DVE.do(lambda e: e.memset(ones_tp, 1.0))
        t_c0 = DVE.do(lambda e: e.memset(sel, 0.0))
        sel_flat = sel.rearrange("p a b -> p (a b)")
        DVE.do(lambda e: e.memset(sel_flat[:, 0:NT * NT:NT + 1], 1.0), t_c0)
        DVE.do(lambda e: e.memset(sel_flat[:, NT:NT * NT:NT + 1], -1.0))
        DVE.do(lambda e: e.memset(zeros, 0.0))
        t_const = DVE.do(lambda e: e.memset(eps, NORM_EPS))

        DVE.do(lambda e: e.tensor_copy(src_f, src_i), edges_in)
        t_dst = DVE.do(lambda e: e.tensor_copy(dst_f, dst_i))
        ge = htok[:, 0:4, :].rearrange("p a b -> p (a b)").bitcast(BF16)[:, 0:NT * ECH].rearrange(
            "p (b c) -> p b c", c=ECH)
        for b in range(NT):
            t_ge = DVE.do(lambda e, b=b: e.tensor_scalar(ge[:, b, :], dst_f, float(TP * b), None, ALU.is_ge), t_dst)
        t_cnt = PE.do(group(psum[0:NT, 6, 0:ECH], [(sel[:, b, :], ge[:, b, :]) for b in range(NT)]), t_ge, t_const)
        has = blk[0:NT, 2880:3200].rearrange("p (c a) -> p c a", a=RUN)
        span = blk[0:NT, 3200:3200 + 2 * RUNS].rearrange("p (a c) -> p a c", a=2)
        reach = sb("reach", [NT, 2])
        span_i = sb("span_i", [NT, 2], I32)
        t = DVE.do(lambda e: e.tensor_copy(has.rearrange("p c a -> p (c a)"), psum[0:NT, 6, 0:ECH]), t_cnt)
        bank_free[6] = t
        for j in range(1, RUN):
            t = DVE.do(lambda e, j=j: e.tensor_tensor(has[:, :, 0], has[:, :, 0], has[:, :, j], ALU.add), t)
        t = DVE.do(lambda e: e.tensor_scalar(has[:, :, 0], has[:, :, 0], 1.0, None, ALU.min), t)
        DVE.do(lambda e: e.tensor_tensor(span[:, 0, :], has[:, :, 0], ramps[:, 0, :], ALU.mult), t, t_iota)
        t = DVE.do(lambda e: e.tensor_tensor(span[:, 1, :], has[:, :, 0], ramps[:, 1, :], ALU.mult))
        t = DVE.do(lambda e: e.tensor_reduce(reach, span, AX.X, ALU.max), t)
        t = DVE.do(lambda e: e.tensor_scalar(span[:, 1, 0:1], reach[:, 1:2], -1.0, float(RUNS), ALU.mult, ALU.add), t)
        t = DVE.do(lambda e: e.tensor_scalar(span[:, 1, 0:1], span[:, 1, 0:1], float(RUNS - 1), None, ALU.min), t)
        DVE.do(lambda e: e.tensor_copy(span_i[:, 0:1], span[:, 1, 0:1]), t)
        t = DVE.do(lambda e: e.tensor_tensor(span[:, 0, 0:1], reach[:, 0:1], span[:, 1, 0:1], ALU.subtract), t)
        t_span = DVE.do(lambda e: e.tensor_scalar(span_i[:, 1:2], span[:, 0, 0:1], 1.0, None, ALU.max), t)

        def layer_norm(dst, src, ready, free=None):
            out = {}

            def moments(i):
                t = DVE.do(lambda e: e.bn_stats(stats[:, i, :], src[:, i, :]), ready[i])
                out[i] = DVE.do(lambda e: e.bn_aggr(mv[:, i, :], stats[:, i, :]), t)

            def scale(i):
                t = SC.do(lambda e: e.activation(rstd[:, i:i + 1], mv[:, i, 1:2], ACT.Sqrt, bias=eps[0:TP, :]), out[i],
                          t_const)
                out[i] = DVE.do(lambda e: e.reciprocal(rstd[:, i:i + 1], rstd[:, i:i + 1]), t)

            def apply(i):
                out[i] = DVE.do(lambda e: e.tensor_scalar(dst(i), src[:, i, :], mv[:, i, 0:1], rstd[:, i:i + 1],
                                                          ALU.subtract, ALU.mult), out[i], free(i) if free else None)
            return [moments, scale, apply], out

        def turn_tile(src, i, ready, free, relu, banks=(0, 8), row=None):
            b = bank(*banks)
            row = i if row is None else row

            def fn(e):
                for k in range(KD):
                    ins = e.transpose(psum[:, b, k * TP:(k + 1) * TP], src[:, row, k * 128:(k + 1) * 128],
                                      ident[0:TP, 0:TP])
                return ins
            t = PE.do(fn, ready, bank_free[b], t_id)
            view = psum[:, b, 0:KD * TP].rearrange("p (k n) -> p k n", k=KD)
            dst = hT[:, :, i * TP:(i + 1) * TP]
            if relu:
                t = SC.do(lambda e: e.activation(dst, view, ACT.Relu), t, free)
            else:
                t = SC.do(lambda e: e.copy(dst, view), t, free)
            bank_free[b] = t
            return t

        s_hot, s_used = sem("hot_ready"), sem("hot_used")

        def build_bucket_dve(e, b, state):
            first = e.value_load(span_i[b:b + 1, 0:1], min_val=0, max_val=RUNS - 1)
            number = e.value_load(span_i[b:b + 1, 1:2], min_val=1, max_val=RUNS)
            before = state.get("turns", 0)
            with e.Fori(0, number) as i:
                run = e.bass.s_assert_within(
                    first + i, 0, RUNS - 1,
                    skip_runtime_bounds_check_because="first + number <= RUNS by their computation")
                for j in range(RUN):
                    chunk = run * RUN + j
                    e.wait_ge(s_used, (before + i) * RUN + (j + 1))
                    e.tensor_scalar(hot_dst[j], node_iota[:, b * TP:(b + 1) * TP],
                                    dst_f[:, bass.ds(chunk, 1)], None, ALU.is_equal)
                    e.tensor_scalar(hot_src[j], node_iota, src_f[:, bass.ds(chunk, 1)], None,
                                    ALU.is_equal).then_inc(s_hot, 1)
            state["turns"] = e.snap(before + number)

        def build_bucket_pe(e, b, state, pb):
            number = e.value_load(span_i[b:b + 1, 1:2], min_val=1, max_val=RUNS)
            before = state.get("turns", 0)
            if b == 0:
                e.sem_inc(s_used, RUN)
            for n, (o, w) in enumerate(TOK_CHUNKS):
                e.matmul(psum[0:TP, pb + n, 0:w], zeros[0:1, 0:TP], zeros[0:1, 0:w], start=True, stop=False,
                         skip_group_check=True)
            with e.Fori(0, number) as i:
                for j in range(RUN):
                    e.wait_ge(s_hot, (before + i) * RUN + (j + 1))
                    for n, (o, w) in enumerate(TOK_CHUNKS):
                        ins = e.matmul(psum[0:TP, pb + n, 0:w], hot_dst[j], hot_src[j][:, o:o + w],
                                       start=False, stop=False, skip_group_check=True)
                    ins.then_inc(s_used, 1)
            state["turns"] = e.snap(before + number)
            for n, (o, w) in enumerate(TOK_CHUNKS):
                ins = e.matmul(psum[0:TP, pb + n, 0:w], zeros[0:1, 0:TP], zeros[0:1, 0:w], start=False, stop=True,
                               skip_group_check=True)
            return ins

        ln, ln_ready = layer_norm(lambda i: htok[:, i, :], x_res, [[x_in, t_cnt]] * NT)
        turned = {}

        def turn_normed(i):
            turned[i] = turn_tile(htok, i, ln_ready[i], None, False)
        pipeline(NT, *ln, turn_normed)
        turned = [turned[i] for i in range(NT)]
        dve_state, pe_state = {}, {}
        row_free, parts_free = [None], [None, None]
        adj_done = []

        def bucket_sum(b):
            pb = 3 * (b % 2)
            DVE.raw(lambda e: build_bucket_dve(e, b, dve_state), t_span, t_iota)
            t = PE.do(lambda e: build_bucket_pe(e, b, pe_state, pb), t_span, t_const,
                      [bank_free[pb + n] for n in range(3)])
            summed[b] = t

        def bucket_out(b):
            pb = 3 * (b % 2)
            t = summed[b]
            SC.wait(row_free[0], turned)
            for n, (o, w) in enumerate(TOK_CHUNKS):
                t2 = SC.do(lambda e, n=n, o=o, w=w: e.activation(a_row[:, o:o + w], psum[0:TP, pb + n, 0:w], ACT.Copy,
                                                                accum_out=deg3[:, b, n:n + 1]), t)
            for n in range(3):
                bank_free[pb + n] = t2
            t_hi = SC.do(lambda e: e.copy(a_parts[b % 2][0], a_row_t), t2, parts_free[b % 2])
            t_lo = row_free[0] = POOL.do(lambda e: e.tensor_tensor(a_parts[b % 2][1], a_row_t, a_parts[b % 2][0],
                                                                   ALU.subtract), t_hi)
            rows[b] = [t_hi, t_lo]
            SC.do(lambda e: e.activation(lo_junk, a_parts[b % 2][1], ACT.Square, accum_out=lo_sum[:, b:b + 1]), rows[b])

        rows, summed = {}, {}

        def bucket_turn(b):
            for part in range(2):
                for s0 in range(0, NT, 8):
                    ns = min(8, NT - s0)
                    q = 6 + turn[0] % 2
                    turn[0] += 1
                    out = psum[0:TP, q, :].bitcast(BF16)

                    def fn(e, part=part, s0=s0, ns=ns, out=out):
                        for s in range(ns):
                            ins = e.transpose(out[:, s * PITCH:s * PITCH + TP], a_parts[b % 2][part][:, s0 + s, :],
                                              ident_b)
                        return ins
                    t = PE.do(fn, rows[b], bank_free[q], t_const)
                    bank_free[q] = SC.do(lambda e, part=part, s0=s0, ns=ns, out=out: e.copy(
                        adj[part][:, s0:s0 + ns, b, 0:TP],
                        out[:, 0:ns * PITCH].rearrange("p (s n) -> p s n", n=PITCH)[:, :, 0:TP]), t)
            parts_free[b % 2] = t
            adj_done.append(bank_free[q])

        pipeline(NT, bucket_sum, bucket_out, bucket_turn)
        t = DVE.do(lambda e: e.tensor_reduce(inv_deg, deg3, AX.X, ALU.add), adj_done[-1])
        t = DVE.do(lambda e: e.tensor_scalar(inv_deg, inv_deg, 1.0, None, ALU.max), t)
        t_inv = DVE.do(lambda e: e.reciprocal(inv_deg, inv_deg), t)
        t = DVE.do(lambda e: e.tensor_reduce(lo_sum[:, 0:1], lo_sum, AX.X, ALU.add), adj_done[-1])
        t = PE.do(lambda e: e.matmul(psum[0:1, 6, 0:1], lo_sum[:, 0:1], ones_tp, start=True, stop=True), t,
                  bank_free[6])
        t_flag = bank_free[6] = DVE.do(lambda e: e.tensor_scalar(lo_flag, psum[0:1, 6, 0:1], 1.0, None, ALU.min), t)
        big = {}

        def load_flag(e):
            big["flag"] = e.value_load(lo_flag[0:1, 0:1], min_val=0, max_val=1)
        PE.raw(load_flag, t_flag)

        def z_tiles(w, ready, free, third, diff):
            out, diff_free = [], [None, None]
            parts = z_part + [third]

            def one(i):
                b = bank()
                t = PE.do(group(psum[0:TP, b, :], [(hT[:, k, i * TP:(i + 1) * TP], w[:, k, :]) for k in range(KD)]),
                          ready[i], bank_free[b])
                d = diff[:, i % 2, :]
                t = SC.do(lambda e: e.copy(parts[0][:, i, :], psum[0:TP, b, :]), t, free)
                t = bank_free[b] = DVE.do(lambda e: e.tensor_tensor(
                    d, psum[0:TP, b, :], parts[0][:, i, :], ALU.subtract), t, diff_free[i % 2])
                t = DVE.do(lambda e: e.tensor_copy(parts[1][:, i, :], d), t)
                t = diff_free[i % 2] = POOL.do(lambda e: e.tensor_tensor(
                    parts[2][:, i, :], d, parts[1][:, i, :], ALU.subtract), t)
                out.append(t)
            return one, out, parts

        def neighbours(out, parts, i, *tokens):
            def pairs(adj_parts):
                return [(a_part[:, s, i, 0:TP], z_[:, s, :])
                        for a_part in adj_parts for s in range(NT) for z_ in parts]

            def fn(e):
                with e.If(big["flag"] > 0):
                    group(out, pairs(adj))(e).then_inc(PE.sem, 1)
                with e.Else():
                    group(out, pairs(adj[:1]))(e).then_inc(PE.sem, 1)
            return PE.split(fn, *tokens)

        gate_w = sb("gate_w", [128, KD, N_EXP])
        bias16 = sb("bias16", [TP, N_EXP])
        ld_r = landing("router")
        ld_r.dma(SP, gate_w.rearrange("p k n -> p (k n)"), a["L0_ffn_gate_w"])
        router_in = ld_r.dma(SP, bias16, a["L0_ffn_expert_bias"].partition_broadcast(TP))
        ld_up = [landing("slot0_up"), landing("slot1_up")]
        ld_down = [landing("slot0_down"), landing("slot1_down")]
        W_UP = KD * 2 * D_FF
        rows_dram = nc.dram_tensor("rows", [N_TOK, D], F32).ap()
        ld_rows = [landing(f"rows{n}") for n in range(4)]
        normed = w_conv[0:TP].rearrange("p k n -> p (k n)").rearrange("p (r n) -> p r n", r=4)
        normed_stored = {}
        h_ready, z_free, self_free = turned, adj_done[-1], [None, None]
        PE.wait(w0_in)
        htok_third = htok[:, 5:NT, :].rearrange("p t n -> p (t n)").bitcast(BF16).rearrange("p (t n) -> p t n", n=D)
        for l in range(N_GNN):
            w_self, w_neigh = w_gnn[:, 2 * l], w_gnn[:, 2 * l + 1]
            z_tile, z_ready, parts = z_tiles(w_neigh, h_ready, z_free, htok_third, htok[:, 3:5, :])
            for i in range(NT):
                z_tile(i)
            last = l == N_GNN - 1
            new, self_done = {}, {}
            if last:
                shared_up_in = ld_up[0].dma(SP, w_reg[:, 0, 0:W_UP], a["w_shared"][:, 0:W_UP], z_ready)
                shared_down_in = ld_down[0].dma(SP, w_reg[:, 0, W_UP:], a["w_shared"][:, W_UP:])

            def sums(i):
                bs, bn = bank(), bank()
                t_s = PE.do(group(psum[0:TP, bs, :], [(hT[:, k, i * TP:(i + 1) * TP], w_self[:, k, :])
                                                      for k in range(KD)]),
                            bank_free[bs])
                self_done[i] = t_s[1]
                t_n = neighbours(psum[0:TP, bn, :], parts, i, z_ready, bank_free[bn])
                r = i % 3
                t = DVE.do(lambda e, l=l: e.tensor_tensor(self_sum[:, i % 2, :], psum[0:TP, bs, :],
                                                          bias_rows[:, l, :], ALU.add),
                           t_s, w0_in, self_free[i % 2])
                bank_free[bs] = t
                t = DVE.do(lambda e: e.scalar_tensor_tensor(htok[:, r, :], psum[0:TP, bn, :], inv_deg[:, i:i + 1],
                                                            self_sum[:, i % 2, :], ALU.mult, ALU.add), t, t_n, t_inv,
                           new.get(i - 3))
                bank_free[bn] = self_free[i % 2] = t
                if last:
                    t = DVE.do(lambda e: e.tensor_tensor(x_res[:, i, :], x_res[:, i, :], htok[:, r, :], ALU.add), t)
                new[i] = t

            def turns(i):
                if last:
                    return
                new[i] = turn_tile(htok, i, new[i], None, True, row=i % 3)

            if last:
                ln, ln_ready = layer_norm(lambda i: normed[:, i % 4, :], x_res, new,
                                          lambda i: [normed_stored.get(i - 4), turned.get(i - 4)])
                turned = {}

                def turn_normed(i):
                    turned[i] = turn_tile(normed, i, ln_ready[i], (PE.sem, self_done[i]), False, row=i % 4)
                    normed_stored[i] = ld_rows[i % 4].dma(SP, rows_dram[i * TP:(i + 1) * TP, :], normed[:, i % 4, :],
                                                   ln_ready[i])
                pipeline(NT, sums, *ln, turn_normed)
                turned = [turned[i] for i in range(NT)]
            else:
                pipeline(NT, sums, lambda i: None, turns)
            h_ready = [new[i] for i in range(NT)]
            z_free = (PE.sem, PE.count)
        x_ready = h_ready
        t_l0 = [(PE.sem, PE.count), (DVE.sem, DVE.count)]

        def expert_views(slot):
            w = w_reg[:, slot, :]
            return (w[:, 0:4096].rearrange("p (k n) -> p k n", k=KD),
                    w[:, 4096:6144].rearrange("p (k n) -> p k n", k=KD))
        ld_up[1].dma(SP, w_reg[:, 1, 0:W_UP], a["w_expert"][0][:, 0:W_UP], t_l0)
        ld_down[1].dma(SP, w_reg[:, 1, W_UP:], a["w_expert"][0][:, W_UP:])
        rows_out = [(ld.sem, ld.total) for ld in ld_rows]
        ld_wc = landing("wc")
        wc_in = ld_wc.dma(SP, w_conv.rearrange("p k n -> p (k n)"), a["L1_gnn_W_conv"], rows_out, turned)

        list_dram = nc.dram_tensor("slot_tokens", [MAX_BLOCKS * SLOTS, 1], I32).ap()
        outs_dram = nc.dram_tensor("slot_outs", [MAX_BLOCKS * SLOTS, D], F32).ap()
        rt = blk[0:TP, 16:16 + 2400]
        zero_list = blk[:, 2600:2600 + MAX_BLOCKS].bitcast(I32)
        t = DVE.do(lambda e: e.memset(zero_list, 0), t_l0)
        ld_list = landing("list")
        list_zero = ld_list.dma(SC, list_dram.rearrange("(p c) o -> p (c o)", p=128), zero_list, t)

        zero_rows = blk[:, 2660:3172]
        t = DVE.do(lambda e: e.memset(zero_rows, 0.0), t_l0)
        ld_fill = landing("fill")
        spare = MAX_BLOCKS - MIN_BLOCKS
        outs_filled = ld_fill.dma(SC, outs_dram[MIN_BLOCKS * SLOTS:, :].rearrange("(b p) d -> p b d", p=SLOTS),
                                  zero_rows.unsqueeze(1).to_broadcast([128, spare, D]), t)

        def small(n, w=N_EXP * NT):
            return rt[:, n * w:(n + 1) * w]

        def by_tile(v):
            return v.rearrange("p (t n) -> p t n", t=NT)
        aff, score, hot, prod = (by_tile(small(n)) for n in (0, 1, 2, 3))
        ones_hot = [by_tile(small(4 + k)) for k in range(TOP_K)]
        exp_iota, rank = by_tile(small(7)), by_tile(small(8))
        top8 = small(9)[:, 0:8 * NT].rearrange("p (t n) -> p t n", t=NT)
        top8_i = small(10)[:, 0:8 * NT].bitcast(U32).rearrange("p (t n) -> p t n", t=NT)
        top8_f = small(11)[:, 0:8 * NT].rearrange("p (t n) -> p t n", t=NT)
        sel_aff = small(12)[:, 0:TOP_K * NT].rearrange("p (t n) -> p t n", t=NT)
        gating = sb("gating", [TP, NT, TOP_K])
        slot_f = small(13)[:, 0:TOP_K * NT].rearrange("p (t n) -> p t n", t=NT)
        slot_i = sb("slot_i", [TP, TOP_K, NT], I32)
        list_i = sb("list_i", [TP, NT, TOP_K], I32)
        tok_id = sb("tok_id", [TP, NT], I32)
        picked = sb("picked", [TP, NT, N_EXP], BF16)
        before = sb("before", [TP, TP], BF16)
        ones_b = sb("ones_b", [TP, 128], BF16)
        n_blk_i = sb("n_blk_i", [128, N_EXP + 1], I32)
        n_blk_f = sb("n_blk_f", [128, N_EXP])
        base_f = sb("base_f", [128, N_EXP])
        one16 = sb("one16", [128, N_EXP])

        POOL.do(lambda e: e.iota(exp_iota, [[0, NT], [1, N_EXP]], base=0, channel_multiplier=0,
                                 allow_small_or_imprecise_dtypes=True), t_l0)
        t_tok = POOL.do(lambda e: e.iota(tok_id, [[TP, NT]], base=0, channel_multiplier=1))
        t = POOL.do(lambda e: e.memset(before, 1.0))
        t_lt = POOL.do(lambda e: e.affine_select(out=before, in_=before, compare_op=ALU.is_gt, fill=0.0, base=0,
                                                 pattern=[[1, TP]], channel_multiplier=-1), t)
        DVE.do(lambda e: e.memset(one16, 1.0))
        t_ones = DVE.do(lambda e: e.memset(ones_b, 1.0))

        logits_t = htok.rearrange("p t n -> p (t n)")[0:N_EXP, 0:N_TOK]
        for o, w in TOK_CHUNKS:
            b = bank()
            t = PE.do(group(psum[0:N_EXP, b, 0:w], [(gate_w[:, k, :], hT[:, k, o:o + w]) for k in range(KD)]),
                      turned, router_in, bank_free[b])
            t = bank_free[b] = SC.do(lambda e, o=o, w=w, b=b: e.copy(logits_t[:, o:o + w], psum[0:N_EXP, b, 0:w]), t,
                                     t_l0)
        lb = bank()

        def turn_logits(e):
            for i in range(NT):
                ins = e.transpose(psum[0:TP, lb, i * N_EXP:(i + 1) * N_EXP], logits_t[:, i * TP:(i + 1) * TP],
                                  ident[0:N_EXP, 0:N_EXP])
            return ins
        t = PE.do(turn_logits, t, bank_free[lb])
        t = SC.do(lambda e: e.activation(aff, psum[0:TP, lb, 0:NT * N_EXP].rearrange("p (t n) -> p t n", t=NT),
                                         ACT.Sigmoid), t, t_l0)
        bank_free[lb] = t
        t = DVE.do(lambda e: e.tensor_tensor(score, aff, bias16.unsqueeze(1).to_broadcast([TP, NT, N_EXP]),
                                             ALU.add), t, router_in)
        for i in range(NT):
            t2 = DVE.do(lambda e, i=i: e.max(top8[:, i, :], score[:, i, :]), t)
        for i in range(NT):
            t = DVE.do(lambda e, i=i: e.max_index(top8_i[:, i, :], top8[:, i, :], score[:, i, :]), t2)
        t_top = DVE.do(lambda e: e.tensor_copy(top8_f, top8_i), t)
        for k in range(TOP_K):
            t = DVE.do(lambda e, k=k: e.tensor_tensor(
                ones_hot[k], exp_iota, top8_f[:, :, k:k + 1].to_broadcast([TP, NT, N_EXP]), ALU.is_equal),
                t_top, t_tok)
            t2 = DVE.do(lambda e, k=k: e.tensor_tensor(prod, ones_hot[k], aff, ALU.mult), t)
            t2 = DVE.do(lambda e, k=k: e.tensor_reduce(sel_aff[:, :, k], prod, AX.X, ALU.add), t2)
        denom = small(12)[:, 40:40 + NT]
        t2 = DVE.do(lambda e: e.tensor_reduce(denom, sel_aff, AX.X, ALU.add), t2)
        t2 = DVE.do(lambda e: e.tensor_scalar(denom, denom, 1e-9, None, ALU.add), t2)
        t2 = DVE.do(lambda e: e.reciprocal(denom, denom), t2)
        t_gate = DVE.do(lambda e: e.tensor_tensor(
            gating, sel_aff, denom.unsqueeze(2).to_broadcast([TP, NT, TOP_K]), ALU.mult), t2)
        t = DVE.do(lambda e: e.tensor_tensor(hot, ones_hot[0], ones_hot[1], ALU.add), t)
        t = DVE.do(lambda e: e.tensor_tensor(picked, hot, ones_hot[2], ALU.add), t)

        t_picked = t

        w_gu, w_dn = expert_views(0)
        hid_s = z_reg[:, 0:KD * N_TOK].rearrange("p (k n) -> p k n", k=KD)
        sil = sb("sil", [128, 2, 418])
        sil_free = [None, None]
        hid_ready = []
        steps = [(c, f) for c in range(len(TOK_CHUNKS)) for f in range(KD)]

        def shared_up(n):
            c, f = steps[n]
            o, w = TOK_CHUNKS[c]
            bg, bu = bank(), bank()
            t_g = PE.do(group(psum[:, bg, 0:w], [(w_gu[:, k, f * 128:(f + 1) * 128], hT[:, k, o:o + w])
                                                 for k in range(KD)]), turned, shared_up_in, bank_free[bg])
            t_u = PE.do(group(psum[:, bu, 0:w], [(w_gu[:, k, D_FF + f * 128:D_FF + (f + 1) * 128],
                                                  hT[:, k, o:o + w]) for k in range(KD)]), bank_free[bu])
            t = SC.do(lambda e: e.activation(sil[:, n % 2, 0:w], psum[:, bg, 0:w], ACT.Silu), t_g, sil_free[n % 2])
            bank_free[bg] = t
            t = DVE.do(lambda e: e.tensor_tensor(hid_s[:, f, o:o + w], sil[:, n % 2, 0:w], psum[:, bu, 0:w],
                                                 ALU.mult), t, t_u)
            bank_free[bu] = sil_free[n % 2] = t
            hid_ready.append(t)
        for n in range(3):
            shared_up(n)

        rb = bank()

        def ranks(e):
            for i in range(NT):
                for j in range(i + 1):
                    e.matmul(psum[0:TP, rb, i * N_EXP:(i + 1) * N_EXP], before if j == i else ones_b[:, 0:TP],
                             picked[:, j, :], start=(j == 0), stop=(j == i))
            for j in range(NT):
                ins = e.matmul(psum[:, rb, 256:256 + N_EXP], ones_b, picked[:, j, :],
                               start=(j == 0), stop=(j == NT - 1))
            return ins
        t_rank = PE.do(ranks, t_picked, t_lt, t_ones, bank_free[rb])
        t = DVE.do(lambda e: e.tensor_scalar(n_blk_i[:, 0:N_EXP], psum[:, rb, 256:256 + N_EXP],
                                             float(SLOTS - 1), float(SLOTS), ALU.add, ALU.max), t_rank)
        t = DVE.do(lambda e: e.tensor_single_scalar(n_blk_i[:, 0:N_EXP], n_blk_i[:, 0:N_EXP],
                                                    SLOTS.bit_length() - 1, ALU.arith_shift_right), t)
        t = DVE.do(lambda e: e.tensor_copy(n_blk_f, n_blk_i[:, 0:N_EXP]), t)
        t = DVE.do(lambda e: e.tensor_tensor_scan(base_f, one16, n_blk_f, 0.0, ALU.mult, ALU.add), t)
        t_nblk = DVE.do(lambda e: e.tensor_copy(n_blk_i[:, N_EXP:N_EXP + 1], base_f[:, N_EXP - 1:N_EXP]), t)
        t = DVE.do(lambda e: e.tensor_tensor(base_f, base_f, n_blk_f, ALU.subtract), t_nblk)
        t = DVE.do(lambda e: e.tensor_scalar(base_f, base_f, float(SLOTS), None, ALU.mult), t)
        t = DVE.do(lambda e: e.tensor_tensor(
            rank, psum[0:TP, rb, 0:NT * N_EXP].rearrange("p (t n) -> p t n", t=NT),
            base_f[0:TP].unsqueeze(1).to_broadcast([TP, NT, N_EXP]), ALU.add), t)
        bank_free[rb] = t
        for k in range(TOP_K):
            t = DVE.do(lambda e, k=k: e.tensor_tensor(prod, ones_hot[k], rank, ALU.mult), t)
            t = DVE.do(lambda e, k=k: e.tensor_reduce(slot_f[:, :, k], prod, AX.X, ALU.add), t)
            t = DVE.do(lambda e, k=k: e.tensor_copy(slot_i[:, k, :], slot_f[:, :, k]), t)
        t_slot = t
        blk_i = small(14)[:, 0:TOP_K * NT].bitcast(I32).rearrange("p (t n) -> p t n", t=NT)
        blk_f = small(14)[:, 40:40 + TOP_K * NT].rearrange("p (t n) -> p t n", t=NT)
        t = DVE.do(lambda e: e.tensor_single_scalar(blk_i, slot_i.rearrange("p k t -> p t k"),
                                                    SLOTS.bit_length() - 1, ALU.arith_shift_right), t)
        t = DVE.do(lambda e: e.tensor_scalar(blk_f, blk_i, -float(SLOTS * MAX_BLOCKS - 1), None, ALU.mult), t)
        t_list = DVE.do(lambda e: e.scalar_tensor_tensor(list_i, slot_f, float(MAX_BLOCKS), blk_f, ALU.mult,
                                                         ALU.add), t)

        ld_scatter = landing("scatter")
        for i in range(NT):
            for k in range(TOP_K):
                POOL.wait(t_list, t_tok, list_zero)
                ld_scatter.total += 16
                POOL.steps.append(lambda e, i=i, k=k: e.indirect_dma_start(
                    list_dram, bass.IndirectOffsetOnAxis(ap=list_i[:, i, k:k + 1], axis=0),
                    tok_id[:, i:i + 1], None).then_inc(ld_scatter.sem, 16))
        list_out = (ld_scatter.sem, ld_scatter.total)

        for n in range(3, len(steps)):
            shared_up(n)
        x_ready = []
        for i in range(NT):
            b = bank()
            t = PE.do(group(psum[0:TP, b, :], [(hid_s[:, k, i * TP:(i + 1) * TP], w_dn[:, k, :])
                                               for k in range(KD)]), hid_ready[-1], shared_down_in, bank_free[b])
            bank_free[b] = DVE.do(lambda e, i=i, b=b: e.tensor_tensor(
                x_res[:, i, :], x_res[:, i, :], psum[0:TP, b, :], ALU.add), t)
            x_ready.append(bank_free[b])
        t_shared = (PE.sem, PE.count)

        xg = blk[:, 0:512]
        xgT = blk[:, 512:1024].rearrange("p (k n) -> p k n", k=KD)
        hid = blk[:, 1024:1536]
        hidT = blk[:, 1536:2048].rearrange("p (k n) -> p k n", k=KD)
        silg = blk[:, 2048:2560].rearrange("p (h n) -> p h n", h=2)
        y_blk = blk[:, 2560:3072]
        idx_all = blk[:, 3072:3072 + MAX_BLOCKS].bitcast(I32)
        idx = blk[:, 3172:3173].bitcast(I32)
        s_idx, s_col, s_row, s_out = (sem(n) for n in ("idx_in", "idx_column", "rows_in", "block_out"))
        s_xt, s_xe, s_gu, s_hid, s_ht, s_he, s_dn, s_y = (sem(n) for n in (
            "x_turned", "x_copied", "gate_up", "hidden", "hid_turned", "hid_copied", "down", "y_ready"))
        HF = D_FF // 2

        def block_of(e, g):
            return e.bass.s_assert_within(
                g, 0, MAX_BLOCKS - 1,
                skip_runtime_bounds_check_because="the experts' blocks are at most MAX_BLOCKS in all")

        def loops(e, body, before_expert=None):
            done = 0
            for x in range(N_EXP):
                if before_expert:
                    before_expert(e, x)
                number = e.value_load(n_blk_i[0:1, x:x + 1], min_val=1, max_val=10)
                with e.Fori(0, number) as i:
                    body(e, x, done + i)
                done = e.snap(done + number)
            return done

        s_pass = sem("gather_may_go")

        def pool_blocks(e):
            total = e.value_load(n_blk_i[0:1, N_EXP:N_EXP + 1], min_val=N_EXP, max_val=MAX_BLOCKS)
            e.dma_start(idx_all, list_dram.rearrange("(p c) o -> p (c o)", p=128)).then_inc(s_idx, 16)
            e.wait_ge(s_idx, 16)
            with e.Fori(0, total) as g:
                e.wait_ge(s_xt, g + 1)
                gather(e, g, idx_all[:, bass.ds(block_of(e, g), 1)])
            e.wait_ge(s_xt, total + 1)
            e.sem_inc(s_pass, 1)
            gather(e, total, idx_all[:, 0:1])

        def gather(e, g, column):
            e.tensor_copy(idx, column).then_inc(s_col, 1)
            e.wait_ge(s_col, g + 1)
            e.sem_inc(s_pass, 1)
            e.indirect_dma_start(xg, None, rows_dram,
                                 bass.IndirectOffsetOnAxis(ap=idx, axis=0)).then_inc(s_row, 16)
        POOL.raw(pool_blocks, t_nblk, list_out, rows_out, t_rank, t_slot, outs_filled, list_zero)

        def turn_rows(e, g):
            e.wait_ge(s_row, g * 16 + 16)
            for k in range(KD):
                ins = e.transpose(psum[:, 0, k * 128:(k + 1) * 128], xg[:, k * 128:(k + 1) * 128], ident)
            ins.then_inc(s_xt, 1)

        def turn_hidden(e, g, h):
            e.wait_ge(s_hid, g * 2 + h + 3)
            if h == 0:
                e.wait_ge(s_he, g * 2 + 2)
            for k in range(2):
                ins = e.transpose(psum[:, 3 + h, k * 128:(k + 1) * 128],
                                  hid[:, h * HF + k * 128:h * HF + (k + 1) * 128], ident)
            ins.then_inc(s_ht, 1)

        def pe_block(e, x, g):
            w_gu, w_dn = expert_views((x + 1) % 2)
            e.wait_ge(s_xe, g + 1)
            e.wait_ge(s_hid, g * 2 + 2)
            for h in range(2):
                for part in range(2):
                    if h == 1 and part == 1:
                        turn_hidden(e, g, 0)
                    for k in range(KD):
                        c = part * D_FF + h * HF
                        ins = e.matmul(psum[:, 1 + h, part * HF:(part + 1) * HF], xgT[:, k, :],
                                       w_gu[:, k, c:c + HF], start=(k == 0), stop=(k == KD - 1))
                ins.then_inc(s_gu, 1)
            e.wait_ge(ld_down[(x + 1) % 2].sem, slot_need[x])
            e.wait_ge(s_y, g + 1)
            for k in range(KD):
                if k == 2:
                    turn_hidden(e, g, 1)
                    turn_rows(e, g + 1)
                if k % 2 == 0:
                    e.wait_ge(s_he, g * 2 + k // 2 + 3)
                ins = e.matmul(psum[:, 5, :], hidT[:, k, :], w_dn[:, k, :], start=(k == 0), stop=(k == KD - 1))
            ins.then_inc(s_dn, 1)

        def copy_rows(e, g):
            e.wait_ge(s_xt, g + 2)
            e.copy(xgT.rearrange("p k n -> p (k n)"), psum[:, 0, :]).then_inc(s_xe, 1)

        def act_block(e, x, g):
            for h in range(2):
                e.wait_ge(s_gu, g * 2 + h + 1)
                e.activation(silg[:, h, :], psum[:, 1 + h, 0:HF], ACT.Silu).then_inc(s_sil, 1)
            copy_rows(e, g + 1)
            e.wait_ge(s_dn, g + 1)
            e.wait_ge(s_out, g * 16 + 16)
            e.copy(y_blk, psum[:, 5, :]).then_inc(s_y, 1)

        def act_all(e):
            copy_rows(e, 0)
            loops(e, act_block)
        s_sil = sem("silu")

        def dve_block(e, x, g):
            for h in range(2):
                e.wait_ge(s_sil, g * 2 + h + 1)
                e.tensor_tensor(hid[:, h * HF:(h + 1) * HF], silg[:, h, :], psum[:, 1 + h, HF:2 * HF],
                                ALU.mult).then_inc(s_hid, 1)
                e.wait_ge(s_ht, g * 2 + h + 1)
                e.tensor_copy(hidT[:, 2 * h:2 * h + 2, :].rearrange("p k n -> p (k n)"),
                              psum[:, 3 + h, 0:256]).then_inc(s_he, 1)

        def sp_block(e, x, g):
            e.wait_ge(s_y, g + 2)
            e.dma_start(outs_dram[bass.ds(block_of(e, g) * SLOTS, SLOTS), :], y_blk).then_inc(s_out, 16)

        PE.wait(bank_free, t_nblk)
        s_exp = sem("expert_done")
        ld_qkv = landing("qkv")
        ld_qkv.total = 16

        def weights_ready(e, x):
            e.wait_ge(ld_up[(x + 1) % 2].sem, slot_need[x])

        slot_need = {0: 16}
        for x in range(1, N_EXP):
            slot_need[x] = slot_need.get(x - 2, 16) + 16 if x > 1 else 32

        def load_next(e, x):
            if x + 1 < N_EXP:
                if x >= 1:
                    e.wait_ge(s_exp, x)
                e.dma_start(w_reg[:, x % 2, 0:W_UP], a["w_expert"][x + 1][:, 0:W_UP]).then_inc(ld_up[x % 2].sem, 16)
                e.dma_start(w_reg[:, x % 2, W_UP:], a["w_expert"][x + 1][:, W_UP:]).then_inc(ld_down[x % 2].sem, 16)
            else:
                e.wait_ge(s_exp, x)
                e.dma_start(w_reg[:, 1, :], a["w_qkv"]).then_inc(ld_qkv.sem, 16)

        def pe_all(e):
            done = 0
            turn_rows(e, 0)
            for x in range(N_EXP):
                weights_ready(e, x)
                number = e.value_load(n_blk_i[0:1, x:x + 1], min_val=1, max_val=10)
                with e.Fori(0, number) as i:
                    pe_block(e, x, done + i)
                done = e.snap(done + number)
                ins = e.matmul(psum[0:1, 6, 0:2], ident[:, 0:1], ident[:, 0:2], start=True, stop=True)
                ins.then_inc(s_exp, 1)
            return e.matmul(psum[0:1, 6, 0:2], ident[:, 0:1], ident[:, 0:2], start=True, stop=True)
        t_pe_moe = PE.do(pe_all)
        SC.raw(act_all, t_nblk, t_shared, bank_free, outs_filled)
        DVE.raw(lambda e: loops(e, dve_block), t_nblk, t_shared, bank_free)

        def sp_start(e):
            for s, n in ((s_xt, 1), (s_hid, 2), (s_he, 2), (s_y, 1), (s_out, 16)):
                e.sem_inc(s, n)
        SP.raw(sp_start, t_nblk, outs_filled)
        SP.wait(t_shared)

        def sp_all(e):
            g = loops(e, sp_block, load_next)
            e.wait_ge(s_out, g * 16 + 16)
            return e.sem_inc(stored, 1)
        stored = sem("blocks_stored")
        SP.raw(sp_all)
        for lds in (ld_up, ld_down):
            lds[1].total, lds[0].total = slot_need[N_EXP - 2], slot_need[N_EXP - 1]
        t_stored = (stored, 1)

        ring = z_reg[0:TP, :].rearrange("p (r n) -> p r n", n=D)
        RING = NT
        ld_take = [landing(f"take{r}") for r in range(RING)]
        ring_free = [t_shared] * RING
        bank_free[:] = [t_pe_moe] * 8

        def take(i):
            for k in range(TOP_K):
                r = (i * TOP_K + k) % RING
                POOL.wait(t_stored, ring_free[r])
                ld_take[r].total += 16
                POOL.steps.append(lambda e, i=i, k=k, r=r: e.indirect_dma_start(
                    ring[:, r, :], None, outs_dram,
                    bass.IndirectOffsetOnAxis(ap=slot_i[:, k, i:i + 1], axis=0)).then_inc(ld_take[r].sem, 16))
                x_ready[i] = ring_free[r] = DVE.do(lambda e, i=i, k=k, r=r: e.scalar_tensor_tensor(
                    x_res[:, i, :], ring[:, r, :], gating[:, i, k:k + 1], x_res[:, i, :], ALU.mult, ALU.add),
                    (ld_take[r].sem, ld_take[r].total), x_ready[i], t_gate)
        ln, ln_ready = layer_norm(lambda i: htok[:, i, :], x_res, x_ready)
        turned = {}

        turn_banks = [0, 8]

        def turn_taken(i):
            turned[i] = turn_tile(htok, i, ln_ready[i], None, False, turn_banks)
        DENSE_TILES = -(-N_DENSE // TP)
        pipeline(DENSE_TILES, take, *ln, turn_taken)

        ld_b, ld_c = landing("slot_b"), landing("norms")
        experts_over = t_pe_moe
        qkv_in = (ld_qkv.sem, ld_qkv.total)
        wb_in = ld_b.dma(SP, w_reg[:, 0, 0:KD * D], a["w_last"][:, 0:KD * D], x_ready[DENSE_TILES - 1])
        w_q, w_k, w_v = (w_reg[:, 1, n * 2048:(n + 1) * 2048].rearrange("p (k n) -> p k n", k=KD) for n in range(3))
        w_o = w_reg[:, 0, 0:2048].rearrange("p (k n) -> p k n", k=KD)
        rows3 = blk[0:TP, 0:1536].rearrange("p (m d) -> p m d", d=D)
        attn = blk[:, 1536:2560].rearrange("p (t d) -> p t d", d=D)
        projT = blk[:, 2560:2816]
        kv = blk[:, 2816:3076].rearrange("p (r m d) -> p r m d", r=2, m=2)
        mean_w = blk[0:TP, 3076:3201]
        half = blk[:, 3202:3204]
        s3 = blk[:, 3204:3584]
        blk_over = [x_ready[-1], t_stored, (POOL.sem, POOL.count), t_pe_moe]
        for n, name in enumerate(("L1_gnn_b_conv", "L1_gnn_norm2_g", "L1_gnn_norm2_b")):
            ld_c.dma(SP, rows3[:, n, :], a[name].partition_broadcast(TP), blk_over)
        n1 = sb("n1", [128, 2, KD])
        ld_c.dma(SP, n1[:, 0, :], a["L1_gnn_norm1_g"])
        ld_c.dma(SP, n1[:, 1, :], a["L1_gnn_norm1_b"])
        for h in range(2):
            norms_in = ld_c.dma(SP, projT[h * 64:h * 64 + 64, :], a["projT"])
        DVE.do(lambda e: e.memset(mean_w, 1.0 / N_TOK), blk_over)
        t_half = DVE.do(lambda e: e.memset(half, 0.0), blk_over)
        for odd in range(2):
            t_half2 = DVE.do(lambda e, odd=odd: e.memset(half[odd * DH:(odd + 1) * DH, odd:odd + 1], 0.5), t_half)

        qk = [w_reg[:, 0, 2048 + n * 1024:3072 + n * 1024].rearrange("p (f n) -> p f n", f=KD) for n in range(2)]
        qf = w_reg[:, 0, 4096:5120].rearrange("p (r t m) -> p r t m", r=2, t=2)
        kf = w_reg[:, 0, 5120:6144].rearrange("p (r t m) -> p r t m", r=2, t=2)
        qfT = w_reg[:, 1, 1040:1552].rearrange("p (m n) -> p m n", m=2)
        conv_sum = w_reg[0:TP, 1, 1552:2576].rearrange("p (r d) -> p r d", r=2)
        conv_third = w_reg[0:TP, 1, 2576:2576 + NT * D // 2].bitcast(BF16).rearrange("p (t n) -> p t n", n=D)
        v_ext = w_reg[:, 1, 0:1040].rearrange("p (t h d) -> p t h d", t=2, h=HEADS)
        attnT = w_reg[:, 0, 4096:6096].rearrange("p (k n) -> p k n", k=KD)
        sq = [w_reg[:, 1, 2576 + n * 1024:3600 + n * 1024].rearrange("p (f n) -> p f n", f=KD) for n in range(2)]
        h_attn = w_reg[0:TP, 0, 2048:4096].rearrange("p (t d) -> p t d", d=D)
        scale = DH ** -0.25
        t_qk, t_ve, leave = [], [], []

        def take_qk(n, f2, b, t):
            bank_free[b] = SC.do(lambda e: e.mul(
                qk[n][:, 2 * f2:2 * f2 + 2, :].rearrange("p f n -> p (f n)"), psum[:, b, :], scale), t, experts_over)
            t_qk.append(bank_free[b])

        def take_v(s, b, t):
            bank_free[b] = SC.do(lambda e: e.copy(
                v_ext[:, s, :, 0:DH], psum[:, b, :].rearrange("p (h d) -> p h d", h=HEADS)), t, t_qkv)
            t_ve.append(bank_free[b])

        b = 0
        for n, w in enumerate((w_q, w_k)):
            for f2 in range(2):
                def fn(e, w=w, f2=f2, b=b):
                    for f in range(2):
                        for k in range(KD):
                            c = (f2 * 2 + f) * 128
                            ins = e.matmul(psum[:, b, f * 256:(f + 1) * 256], w[:, k, c:c + 128], hT[:, k, 0:N_DENSE],
                                           start=(k == 0), stop=(k == KD - 1))
                    return ins
                t = PE.do(fn, turned[DENSE_TILES - 1], qkv_in, bank_free[b])
                leave.append(lambda n=n, f2=f2, b=b, t=t: take_qk(n, f2, b, t))
                b += 1
        for s in range(2):
            t = PE.do(group(psum[:, b, :], [(hT[:, k, s * 128:(s + 1) * 128], w_v[:, k, :]) for k in range(KD)]),
                      bank_free[b])
            leave.append(lambda s=s, b=b, t=t: take_v(s, b, t))
            b += 1
        t_qkv = t
        turn_banks[:] = [b, 8]
        pipeline(NT, take, *ln, turn_taken, first=DENSE_TILES, after=lambda t: leave and leave.pop(0)())
        assert not leave
        turned = [turned[i] for i in range(NT)]
        t_sq = [SC.do(lambda e, n=n: e.square(sq[n], qk[n]), t_qk, t_qkv) for n in range(2)]
        t_vx = DVE.do(lambda e: e.memset(v_ext[:, :, :, DH:DH + 1], 1.0), t_qkv)
        diag = s3[:, 0:32].rearrange("p (q t h) -> p q t h", q=2, t=2)
        db = bank()

        def diags(e):
            for n in range(2):
                for s in range(2):
                    for f in range(KD):
                        c = (n * 2 + s) * HEADS + 2 * f
                        ins = e.matmul(psum[:, db, c:c + 2], sq[n][:, f, s * 128:(s + 1) * 128], half, start=True,
                                       stop=True)
            return ins
        t_dg = PE.do(diags, t_sq, t_half2, bank_free[db])
        t_diag = bank_free[db] = DVE.do(lambda e: e.tensor_copy(
            diag.rearrange("p q t h -> p (q t h)"), psum[:, db, 0:4 * HEADS]), t_dg, blk_over)

        def features(n, h, b):
            rows = slice(64 * (h % 2), 64 * (h % 2) + 64)

            def fn(e):
                for s in range(2):
                    ins = e.matmul(psum[:, b, s * 256:(s + 1) * 256], qk[n][rows, h // 2, s * 128:(s + 1) * 128],
                                   projT[rows, :], start=True, stop=True)
                return ins
            return PE.do(fn, t_qk, norms_in, bank_free[b])

        bst = s3[:, 250:322].rearrange("p (k c s) -> p k c s", k=KD, c=3)
        bmv = s3[:, 322:330].rearrange("p (k s) -> p k s", k=KD)
        bsc, bsh = s3[:, 330:334], s3[:, 334:338]
        for k in range(KD):
            for c, (o, w) in enumerate(TOK_CHUNKS):
                t = DVE.do(lambda e, k=k, c=c, o=o, w=w: e.bn_stats(bst[:, k, c, :], hT[:, k, o:o + w]), turned,
                           blk_over)
        for k in range(KD):
            t2 = DVE.do(lambda e, k=k: e.bn_aggr(bmv[:, k, :], bst[:, k].rearrange("p c s -> p (c s)")), t)
        t = SC.do(lambda e: e.activation(bsc, bmv[:, :, 1], ACT.Sqrt, bias=eps), t2)
        t = DVE.do(lambda e: e.reciprocal(bsc, bsc), t)
        t = DVE.do(lambda e: e.tensor_tensor(bsc, bsc, n1[:, 0, :], ALU.mult), t, norms_in)
        t = DVE.do(lambda e: e.tensor_tensor(bsh, bmv[:, :, 0], bsc, ALU.mult), t)
        t = DVE.do(lambda e: e.tensor_tensor(bsh, n1[:, 1, :], bsh, ALU.subtract), t)
        for k in range(KD):
            t_xn = DVE.do(lambda e, k=k: e.tensor_scalar(hT[:, k, :], hT[:, k, :], bsc[:, k:k + 1],
                                                         bsh[:, k:k + 1], ALU.mult, ALU.add), t, t_qkv)

        k_max = s3[:, 32:40]
        for h in range(HEADS):
            b = bank()
            t = features(1, h, b)
            t_km = bank_free[b] = DVE.do(lambda e, h=h, b=b: e.reduce_max(k_max[:, h:h + 1], psum[:, b, :], AX.X),
                                         t, blk_over)
        b = bank()
        t = PE.do(lambda e, b=b: e.transpose(psum[0:HEADS, b, 0:128], k_max, ident), t_km, bank_free[b])
        k_max8, k_diag = s3[0:HEADS, 40:41], s3[0:HEADS, 41:49]
        t = bank_free[b] = DVE.do(lambda e, b=b: e.reduce_max(k_max8, psum[0:HEADS, b, 0:128], AX.X), t)
        t = DVE.do(lambda e: e.tensor_scalar(k_diag, ident[0:HEADS, 0:HEADS], k_max8, None, ALU.mult), t)
        ones8 = s3[0:HEADS, 49:177]
        t2 = DVE.do(lambda e: e.memset(ones8, 1.0), blk_over)
        b = bank()
        t = PE.do(lambda e, b=b: e.matmul(psum[:, b, 0:HEADS], ones8, k_diag, start=True, stop=True), t, t2,
                  bank_free[b])
        k_bias = s3[:, 180:196].rearrange("p (t h) -> p t h", t=2)
        for s in range(2):
            t_kb = DVE.do(lambda e, s=s, b=b: e.scalar_tensor_tensor(
                k_bias[:, s, :], diag[:, 1, s, :], -1.0, psum[:, b, 0:HEADS], ALU.mult, ALU.subtract), t, t_diag)
        bank_free[b] = t_kb
        q_max = s3[:, 196:212].rearrange("p (t h) -> p t h", t=2)
        q_bias = s3[:, 212:228].rearrange("p (t h) -> p t h", t=2)
        rden = s3[:, 228:244].rearrange("p (t h) -> p t h", t=2)
        inv_root_m = M_FEAT ** -0.5
        head = [{} for _ in range(HEADS)]
        attn_done = []

        def head_features(h):
            r, me = h % 2, head[h]
            bk, bq = bank(), bank()
            t_k, t_q = features(1, h, bk), features(0, h, bq)
            for s in range(2):
                t = SC.do(lambda e, s=s: e.activation(kf[:, r, s, :], psum[:, bk, s * 256:(s + 1) * 256], ACT.Exp,
                                                      bias=k_bias[:, s, h:h + 1]), t_k, t_kb,
                          head[h - 2].get("kv") if h >= 2 else None)
            bank_free[bk] = t
            me["kf"] = DVE.do(lambda e: e.tensor_scalar(kf[:, r], kf[:, r], inv_root_m, K_EPS, ALU.mult, ALU.add), t)
            t = DVE.do(lambda e: e.tensor_reduce(q_max[:, :, h], psum[:, bq, :].rearrange("p (t m) -> p t m", t=2),
                                                 AX.X, ALU.max), t_q)
            t = DVE.do(lambda e: e.scalar_tensor_tensor(q_bias[:, :, h], diag[:, 0, :, h], -1.0, q_max[:, :, h],
                                                        ALU.mult, ALU.subtract), t, t_diag)
            for s in range(2):
                t2 = SC.do(lambda e, s=s: e.activation(qf[:, r, s, :], psum[:, bq, s * 256:(s + 1) * 256], ACT.Exp,
                                                       bias=q_bias[:, s, h:h + 1]), t,
                           head[h - 2].get("turned") if h >= 2 else None)
            bank_free[bq] = t2
            me["qf"] = DVE.do(lambda e: e.tensor_scalar(qf[:, r], qf[:, r], inv_root_m, K_EPS, ALU.mult, ALU.add), t2)

        def head_products(h):
            r, me = h % 2, head[h]
            b = bank()

            def fn_kv(e):
                for m in range(2):
                    for s in range(2):
                        ins = e.matmul(psum[:, b, m * 65:(m + 1) * 65], kf[:, r, s, m * 128:(m + 1) * 128],
                                       v_ext[:, s, h, :], start=(s == 0), stop=(s == 1))
                return ins
            me["kv"] = PE.do(fn_kv, me["kf"], t_vx, t_ve, bank_free[b])
            t_kv = bank_free[b] = DVE.do(lambda e: e.tensor_copy(
                kv[:, r].rearrange("p m d -> p (m d)"), psum[:, b, 0:130]), me["kv"],
                head[h - 2].get("out") if h >= 2 else None)
            bt = bank()

            def fn_t(e):
                for m in range(2):
                    for s in range(2):
                        ins = e.transpose(psum[:, bt, m * 256 + s * 128:m * 256 + (s + 1) * 128],
                                          qf[:, r, s, m * 128:(m + 1) * 128], ident)
                return ins
            me["turned"] = PE.do(fn_t, me["qf"], bank_free[bt])
            t_q = bank_free[bt] = SC.do(lambda e: e.copy(qfT.rearrange("p m n -> p (m n)"), psum[:, bt, :]),
                                        me["turned"], head[h - 1].get("out") if h >= 1 else None)
            bo = bank()

            def fn_o(e):
                for s in range(2):
                    for m in range(2):
                        ins = e.matmul(psum[:, bo, s * 65:(s + 1) * 65], qfT[:, m, s * 128:(s + 1) * 128],
                                       kv[:, r, m, :], start=(m == 0), stop=(m == 1))
                return ins
            me["out"] = PE.do(fn_o, t_q, t_kv, bank_free[bo])
            out = psum[:, bo, 0:130].rearrange("p (t d) -> p t d", t=2)
            t = DVE.do(lambda e: e.tensor_scalar(rden[:, :, h], out[:, :, DH], K_EPS, None, ALU.add), me["out"])
            t = DVE.do(lambda e: e.reciprocal(rden[:, :, h], rden[:, :, h]), t)
            for s in range(2):
                t2 = DVE.do(lambda e, s=s: e.tensor_scalar(attn[:, s, h * DH:(h + 1) * DH], out[:, s, 0:DH],
                                                           rden[:, s, h:h + 1], None, ALU.mult), t)
            bank_free[bo] = t2
            attn_done.append(t2)
        y_ready = {}

        def convolve(i):
            b = bank()
            t = neighbours(psum[0:TP, b, :], parts, i, z_ready, bank_free[b])
            t = bank_free[b] = DVE.do(lambda e: e.scalar_tensor_tensor(
                conv_sum[:, i % 2, :], psum[0:TP, b, :], inv_deg[:, i:i + 1], rows3[:, 0, :], ALU.mult, ALU.add), t,
                norms_in)
            y_ready[i] = DVE.do(lambda e: e.scalar_tensor_tensor(
                htok[:, i, :], conv_sum[:, i % 2, :], 0.0, htok[:, i, :], ALU.max, ALU.add), t)

        z_tile, z_ready, parts = z_tiles(w_conv, [[t_xn, wc_in]] * NT, [t_dg, x_ready[-1]], conv_third, conv_sum)
        work = [lambda i=i: z_tile(i) for i in range(NT)] + [lambda i=i: convolve(i) for i in range(NT)]
        PER_TURN = [2, 3, 3, 2, 2, 2, 2, 2, 2]

        def between(t):
            for _ in range(PER_TURN[t]):
                work.pop(0)()
        pipeline(HEADS, head_features, head_products, after=between)

        for s in range(2):
            b = bank()

            def fn(e, s=s, b=b):
                for k in range(KD):
                    ins = e.transpose(psum[:, b, k * 128:(k + 1) * 128], attn[:, s, k * 128:(k + 1) * 128], ident)
                return ins
            t = PE.do(fn, attn_done[-1], bank_free[b])
            t = bank_free[b] = DVE.do(lambda e, s=s, b=b: e.tensor_copy(
                attnT[:, :, s * 128:(s + 1) * 128], psum[:, b, :].rearrange("p (k n) -> p k n", k=KD)), t, t_qkv)
        t_at = DVE.do(lambda e: e.tensor_copy(attnT[:, :, N_DENSE:4 * TP],
                                              attnT[:, :, N_DENSE - 1:N_DENSE].to_broadcast(
                                                  [128, KD, 4 * TP - N_DENSE])), t)
        t_ha = {}
        for i in range(4):
            b = bank()
            t = PE.do(group(psum[0:TP, b, :], [(attnT[:, k, i * TP:(i + 1) * TP], w_o[:, k, :]) for k in range(KD)]),
                      t_at, wb_in, bank_free[b])
            t_ha[i] = bank_free[b] = SC.do(lambda e, i=i, b=b: e.copy(h_attn[:, i, :], psum[0:TP, b, :]), t,
                                        head[HEADS - 1]["out"])

        shifted = [POOL.do(lambda e, i=i: e.tensor_tensor(x_res[:, i, :], x_res[:, i, :], rows3[:, 2, :], ALU.add),
                           ln_ready[i], norms_in) for i in range(NT)]

        for i in range(NT):
            y_ready[i] = DVE.do(lambda e, i=i: e.tensor_tensor(
                htok[:, i, :], htok[:, i, :], h_attn[:, min(i, DENSE_TILES), :], ALU.add), y_ready[i], t_ha[min(i, 3)])
        wl_in = ld_b.dma(SP, w_reg[:, 0, KD * D:], a["w_last"][:, KD * D:], y_ready[NT - 1])
        adj_over = (PE.sem, PE.count)

        def token_mean(src, ready):
            b = bank()
            t = None
            for i in range(NT):
                t = PE.do(lambda e, i=i: e.matmul(psum[0:TP, b, :], mean_w, src(i), start=(i == 0),
                                                  stop=(i == NT - 1)), ready[i], bank_free[b])
            return b, t
        bm, t_mean = token_mean(lambda i: htok[:, i, :], y_ready)
        c_ready, s_ready = [], []
        squares = a_reg[0:TP, 0:NT * D].rearrange("p (t n) -> p t n", n=D)
        for i in range(NT):
            c_ready.append(DVE.do(lambda e, i=i: e.tensor_tensor(htok[:, i, :], htok[:, i, :], psum[0:TP, bm, :],
                                                                 ALU.subtract), t_mean))
            s_ready.append(SC.do(lambda e, i=i: e.square(squares[:, i, :], htok[:, i, :]), c_ready[i], adj_over))
        bank_free[bm] = c_ready[-1]
        bv, t_var = token_mean(lambda i: squares[:, i, :], s_ready)
        sc2 = conv_sum[:, 0, :]
        t = bank_free[bv] = SC.do(lambda e: e.activation(sc2, psum[0:TP, bv, :], ACT.Sqrt, bias=eps[0:TP, :]),
                                  t_var, list(y_ready.values()))
        t = DVE.do(lambda e: e.reciprocal(sc2, sc2), t)
        t_sc = DVE.do(lambda e: e.tensor_tensor(sc2, sc2, rows3[:, 1, :], ALU.mult), t)
        x_ready = {}

        def residual(i):
            t2 = (POOL if i % 2 else DVE).do(lambda e: e.tensor_tensor(htok[:, i, :], htok[:, i, :], sc2, ALU.mult),
                                             t_sc, s_ready)
            x_ready[i] = DVE.do(lambda e: e.tensor_tensor(x_res[:, i, :], x_res[:, i, :], htok[:, i, :], ALU.add),
                                shifted[i], t2)
        ln, ln_ready = layer_norm(lambda i: htok[:, i, :], x_res, x_ready)
        turned = {}

        def turn_last(i):
            turned[i] = turn_tile(htok, i, ln_ready[i], None, False)
        pipeline(NT, residual, *ln, turn_last)
        turned = [turned[i] for i in range(NT)]
        x_ready = [x_ready[i] for i in range(NT)]

        ld_d = landing("values")
        w_pv = w_conv.rearrange("p k n -> p (k n)").rearrange("p (k n) -> p k n", n=D_PV)
        t_zc = (PE.sem, PE.count)
        ld_d.dma(SP, w_conv.rearrange("p k n -> p (k n)"), a["w_values"], t_zc)
        w_oi_flat = z_reg[:, 2500:3012]
        w_oi_r = w_oi_flat.rearrange("p (k n) -> p k n", k=2)
        d_in = ld_d.dma(SP, w_oi_flat, a["w_oi"], t_var)
        w_pi = w_reg[:, 0, 2048:4096].rearrange("p (k n) -> p k n", k=2)
        w_ip = w_reg[:, 0, 4096:5120].rearrange("p (k n) -> p k n", k=KD)
        w_op = w_reg[:, 0, 5120:6144].rearrange("p (k n) -> p k n", k=2)
        actsT = z_reg[:, 0:2 * N_TOK].rearrange("p (k n) -> p k n", k=2)
        acts = a_reg[0:TP, 0:NT * N_PROC].rearrange("p (t n) -> p t n", n=N_PROC)
        wexp = [a_reg[0:TP, 10240:11264], a_reg[0:TP, 11264:12288],
                htok.rearrange("p t n -> p (t n)")[:, 4096:5120]]
        rest = htok.rearrange("p t n -> p (t n)")[:, 0:2048].rearrange("p (r n) -> p r n", r=2)
        junk = htok.rearrange("p t n -> p (t n)")[:, 2048:4096].rearrange("p (r n) -> p r n", r=2)
        hT_flat = hT.rearrange("p k n -> p (k n)")
        wT = hT_flat[:, 0:2000].rearrange("p (r k n) -> p r k n", r=2, k=8)
        agg = hT_flat[0:TP, 2000:2512].rearrange("p (r n) -> p r n", r=2)
        aggT = hT_flat[:, 2512:3012].rearrange("p (r k n) -> p r k n", r=2, k=2)
        outT = hT_flat[:, 3012:3512].rearrange("p (r k n) -> p r k n", r=2, k=2)
        ch = blk[0:TP, 0:400]
        act_sum = ch[:, 0:2 * NT].rearrange("p (t h) -> p t h", h=2)
        thr, step, cnt, left, cut, cut_cnt, x_max, neg_max, bad, w_sum, w_inv = (
            ch[:, (2 + n) * NT:(3 + n) * NT] for n in range(11))
        cand = ch[:, 150:150 + 17 * NT].rearrange("p (t n) -> p t n", n=17)
        iota16 = ch[:, 330:346]
        cut_junk = ch[:, 350:366]
        bad_i = blk[0:1, 400:400 + NT].bitcast(I32)
        ones_col = blk[0:TP, 420:421]
        top_s = blk[0:TP, 424:432]

        t_ia = []
        for c, (o, w) in enumerate(TOK_CHUNKS):
            for f in range(2):
                b = bank()
                t = PE.do(group(psum[:, b, 0:w], [(w_ip[:, k, f * 128:(f + 1) * 128], hT[:, k, o:o + w])
                                                  for k in range(KD)]), turned, wl_in, bank_free[b])
                bank_free[b] = SC.do(lambda e, o=o, w=w, f=f, b=b: e.activation(
                    actsT[:, f, o:o + w], psum[:, b, 0:w], ACT.Gelu), t, t_var)
                t_ia.append(bank_free[b])
        it = [{} for _ in range(NT)]
        t_blk3 = DVE.do(lambda e: e.memset(ones_col, 1.0), x_ready)
        t_16 = POOL.do(lambda e: e.iota(iota16, [[1, 16]], base=0, channel_multiplier=0,
                                        allow_small_or_imprecise_dtypes=True), x_ready)

        GUESS = 1.17 / (N_PROC * 0.39894)
        AIM = K_PROC - 8
        SLOPE = 1.17 * N_PROC * 0.2059

        def process(i):
            me = it[i]
            for h in range(2):
                b = bank()
                t = PE.do(group(psum[0:TP, b, :], [(actsT[:, k, i * TP:(i + 1) * TP],
                                                    w_pi[:, k, h * 512:(h + 1) * 512]) for k in range(2)]),
                          t_ia, bank_free[b])
                bank_free[b] = me["acts"] = SC.do(lambda e, b=b, h=h: e.activation(
                    acts[:, i, h * 512:(h + 1) * 512], psum[0:TP, b, :], ACT.Gelu,
                    accum_out=act_sum[:, i, h:h + 1]), t, adj_over, t_blk3)
        def count(i):
            it[i]["cnt"] = SC.do(lambda e: e.activation(junk[:, 1, :], acts[:, i, :], ACT.Sign, bias=thr[:, i:i + 1],
                                                        scale=-1.0, accum_out=cnt[:, i:i + 1]),
                                 it[i]["thr"], (SC.sem, SC.count))

        def guess(i):
            me, c = it[i], slice(i, i + 1)
            me["thr"] = DVE.do(lambda e: e.tensor_scalar(thr[:, c], act_sum[:, i, 0:1], act_sum[:, i, 1:2], GUESS,
                                                         ALU.add, ALU.mult), me["acts"])
            me["step"] = DVE.do(lambda e: e.tensor_scalar(step[:, c], thr[:, c], 0.8 / SLOPE, None, ALU.mult),
                                me["thr"])
            count(i)
            t = DVE.do(lambda e: e.tensor_reduce(x_max[:, c], acts[:, i, :], AX.X, ALU.max))
            me["neg"] = DVE.do(lambda e: e.tensor_scalar(neg_max[:, c], x_max[:, c], -1.0, None, ALU.mult), t)

        def count_last(i):
            it[i]["cnt"] = DVE.do(lambda e: e.tensor_scalar(junk[:, 0, :], acts[:, i, :], thr[:, i:i + 1], None,
                                                            ALU.is_ge, ALU.add, accum_out=cnt[:, i:i + 1]),
                                  it[i]["thr"])

        def refine(i, count=count):
            me, c = it[i], slice(i, i + 1)
            t = DVE.do(lambda e: e.tensor_scalar(left[:, c], cnt[:, c], -0.5, N_PROC / 2.0 - AIM, ALU.mult, ALU.add),
                       me["cnt"])
            me["thr"] = DVE.do(lambda e: e.scalar_tensor_tensor(thr[:, c], left[:, c], step[:, c], thr[:, c],
                                                                ALU.mult, ALU.add), t, me["step"])
            count(i)
        def refine_again(i):
            refine(i, count_last)
        s_w = sem("weights")

        def choose(i):
            me, q = it[i], i % 2
            c = slice(i, i + 1)
            t_thr = DVE.do(lambda e: e.tensor_copy(cand[:, i, 0:1], thr[:, c]), me["thr"])
            me["left"] = DVE.do(lambda e: e.tensor_scalar(left[:, c], cnt[:, c], -1.0, float(K_PROC), ALU.mult, ALU.add),
                            me["cnt"])
            r = rest[:, q, :]
            me["rest"] = DVE.do(lambda e: e.scalar_tensor_tensor(
                r, acts[:, i, :], thr[:, i:i + 1], acts[:, i, :], ALU.is_lt, ALU.mult), it[i]["thr"],
                t_thr)
            t = me["rest"]
            DVE.wait(me["left"])
            t = DVE.do(lambda e: e.max(cand[:, i, 1:9], r), t)
            t = DVE.do(lambda e: e.match_replace(r, cand[:, i, 1:9], r, REPLACED), t)
            t = DVE.do(lambda e: e.max(cand[:, i, 9:17], r), t)
            t = DVE.do(lambda e: e.scalar_tensor_tensor(cut_junk, iota16, left[:, c], cand[:, i, 0:16], ALU.is_equal,
                                                        ALU.mult, accum_out=cut[:, c]), t, t_16)
            t2 = DVE.do(lambda e: e.tensor_scalar(cut_junk, cand[:, i, 1:17], cut[:, c], None, ALU.is_ge, ALU.add,
                                                  accum_out=cut_cnt[:, c]), t)
            t = DVE.do(lambda e: e.tensor_scalar(bad[:, c], cut[:, c], 0.0, None, ALU.is_le), t)
            t2 = DVE.do(lambda e: e.tensor_tensor(cut_cnt[:, c], cut_cnt[:, c], left[:, c], ALU.not_equal), t2)
            t = DVE.do(lambda e: e.tensor_tensor(bad[:, c], bad[:, c], cut_cnt[:, c], ALU.add), t, t2)
            me["bad"] = t

        def verdict(i):
            me, q = it[i], i % 2
            b = bank()
            t = PE.do(lambda e: e.matmul(psum[0:1, b, 0:1], ones_col, bad[:, i:i + 1], start=True, stop=True), me["bad"],
                      bank_free[b])
            bank_free[b] = me["bad"] = SC.do(lambda e: e.copy(bad_i[:, i:i + 1], psum[0:1, b, 0:1]), t)

        def exponential(i):
            me = it[i]
            me["exp"] = SC.do(lambda e: e.activation(wexp[i % 3], acts[:, i, :], ACT.Exp,
                                                     bias=neg_max[:, i:i + 1]), me["neg"],
                              it[i - 3]["turned"] if i >= 3 else None)

        def weigh(i):
            me, q = it[i], i % 2
            r, w = junk[:, 1, :], wexp[i % 3]

            def fn(e):
                failed = e.value_load(bad_i[0:1, i:i + 1], min_val=0, max_val=2 * TP)
                with e.If(failed > 0):
                    src = acts[:, i, :]
                    for n in range(K_PROC // 8):
                        e.max(top_s, src)
                        e.drain()
                        e.match_replace(r, top_s, src, REPLACED)
                        e.drain()
                        src = r
                    e.scalar_tensor_tensor(w, r, REPLACED, w, ALU.is_equal, ALU.mult,
                                           accum_out=w_sum[:, i:i + 1]).then_inc(s_w, 1)
                with e.Else():
                    e.scalar_tensor_tensor(w, acts[:, i, :], cut[:, i:i + 1], w, ALU.is_ge, ALU.mult,
                                           accum_out=w_sum[:, i:i + 1]).then_inc(s_w, 1)
            DVE.raw(fn, me["bad"], me["exp"])
            me["weights"] = me["sum"] = DVE.do(lambda e: e.reciprocal(w_inv[:, i:i + 1], w_sum[:, i:i + 1]),
                                               (s_w, i + 1))

        def values(i):
            me, q = it[i], i % 2
            for g in range(2):
                b = bank()

                def fn(e, g=g, b=b):
                    for k in range(4):
                        c = (4 * g + k) * 128
                        ins = e.transpose(psum[:, b, k * TP:(k + 1) * TP], wexp[i % 3][:, c:c + 128], ident[0:TP, 0:TP])
                    return ins
                me["turned"] = t = PE.do(fn, me["weights"], bank_free[b])
                t_w = bank_free[b] = SC.do(lambda e, g=g, b=b: e.copy(
                    wT[:, q, 4 * g:4 * g + 4, :], psum[:, b, 0:4 * TP].rearrange("p (k n) -> p k n", k=4)), t,
                    it[i - 2]["aggp"] if i >= 2 else None)
            b = me["agg_bank"] = bank()
            me["aggp"] = PE.do(group(psum[0:TP, b, 0:D_PV], [(wT[:, q, k, :], w_pv[:, k, :]) for k in range(8)]),
                               t_w, d_in, bank_free[b])

        def scale_values(i):
            me, q, b = it[i], i % 2, it[i]["agg_bank"]
            me["agg"] = bank_free[b] = SC.do(lambda e, b=b: e.activation(
                agg[:, q, :], psum[0:TP, b, 0:D_PV], ACT.Copy, scale=w_inv[:, i:i + 1]), me["aggp"], me["sum"])
            b = bank()

            def fn_t(e, b=b):
                for k in range(2):
                    ins = e.transpose(psum[:, b, k * TP:(k + 1) * TP], agg[:, q, k * 128:(k + 1) * 128],
                                      ident[0:TP, 0:TP])
                return ins
            t = PE.do(fn_t, me["agg"], bank_free[b])
            me["aggT"] = bank_free[b] = SC.do(lambda e, b=b: e.copy(
                aggT[:, q], psum[:, b, 0:2 * TP].rearrange("p (k n) -> p k n", k=2)), t)

        def patterns(i):
            me, q = it[i], i % 2
            b = bank()

            def fn_o(e, b=b):
                for f in range(2):
                    for k in range(2):
                        ins = e.matmul(psum[:, b, f * TP:(f + 1) * TP], w_oi_r[:, k, f * 128:(f + 1) * 128],
                                       aggT[:, q, k, :], start=(k == 0), stop=(k == 1))
                return ins
            t = PE.do(fn_o, me["aggT"], bank_free[b])
            t = bank_free[b] = SC.do(lambda e, b=b: e.activation(
                outT[:, q], psum[:, b, 0:2 * TP].rearrange("p (k n) -> p k n", k=2), ACT.Gelu), t)
            b = me["bank"] = bank()
            me["out"] = PE.do(group(psum[0:TP, b, :], [(outT[:, q, k, :], w_op[:, k, :]) for k in range(2)]), t,
                              bank_free[b])
            bank_free[b] = me["out"]

        ld_out = landing("out")
        o_dram = a["out"].rearrange("(t p) d -> t p d", p=TP)

        def finish(i):
            b = it[i]["bank"]
            t = bank_free[b] = DVE.do(lambda e: e.tensor_tensor(x_res[:, i, :], x_res[:, i, :], psum[0:TP, b, :],
                                                                ALU.add), it[i]["out"])
            ld_out.dma(SP, o_dram[i], x_res[:, i, :], t)
        pipeline(NT, process, guess, refine, refine_again)
        pipeline(NT, choose, lambda i: (exponential(i), verdict(i)), weigh, values, scale_values, patterns, finish)
        SP.wait((ld_out.sem, ld_out.total))

        block = ctx.enter_context(nc.Block())
        block.sync(SP.run)
        block.gpsimd(POOL.run)
        block.scalar(SC.run)
        block.vector(DVE.run)
        block.tensor(PE.run)


def by_blocks(w):
    import numpy as np
    k = w.shape[0] // 128
    return np.ascontiguousarray(w.reshape(k, 128, -1).transpose(1, 0, 2)).reshape(128, -1)


def host_arrays(inputs):
    import numpy as np
    g = {k: np.asarray(v) for k, v in inputs.items()}
    out = {"x": g["x"], "L0_gnn_bs": g["L0_gnn_bs"].reshape(-1)}
    for n in ("src", "dst"):
        out[n] = np.ascontiguousarray(g[n].reshape(ECH, TP).T)
    out["w_gnn"] = np.concatenate([by_blocks(g[n][l]) for l in range(N_GNN)
                                   for n in ("L0_gnn_Ws_self", "L0_gnn_Ws_neigh")], axis=1)
    out["w_shared"] = np.concatenate([by_blocks(g["L0_ffn_shared_gate_up"].T), by_blocks(g["L0_ffn_shared_down"].T)],
                                     axis=1)
    out["w_expert"] = np.stack([np.concatenate([by_blocks(gu.T), by_blocks(dn.T)], axis=1)
                                for gu, dn in zip(g["L0_ffn_expert_gate_up"], g["L0_ffn_expert_down"])])
    out["L0_ffn_gate_w"] = by_blocks(g["L0_ffn_gate_w"].T)
    out["L0_ffn_expert_bias"] = g["L0_ffn_expert_bias"]
    out["w_qkv"] = np.concatenate([by_blocks(g[n]) for n in ("L1_gnn_Wq", "L1_gnn_Wk", "L1_gnn_Wv")], axis=1)
    out["w_last"] = np.concatenate([by_blocks(w) for w in (
        g["L1_gnn_Wo"], g["L1_ffn_process_input_weights"].T, g["L1_ffn_input_patterns"].T,
        g["L1_ffn_output_patterns"])], axis=1)
    out["w_values"] = by_blocks(g["L1_ffn_process_values"])
    out["w_oi"] = by_blocks(g["L1_ffn_output_input_weights"].T)
    out["projT"] = np.ascontiguousarray(g["L1_gnn_proj"].T)
    for n in ("L1_gnn_norm1_g", "L1_gnn_norm1_b"):
        out[n] = np.ascontiguousarray(g[n].reshape(KD, 128).T)
    for n in ("L1_gnn_b_conv", "L1_gnn_norm2_g", "L1_gnn_norm2_b"):
        out[n] = g[n]
    out["L1_gnn_W_conv"] = by_blocks(g["L1_gnn_W_conv"])
    return out


def kernel(**inputs):
    import numpy as np
    import concourse.bacc as bacc
    from concourse.bass_utils import run_bass_kernel_spmd

    nc = bacc.Bacc("TRN2", target_bir_lowering=False, num_devices=1)
    arrays = host_arrays(inputs)
    aps = {n: nc.dram_tensor(n, list(v.shape), mybir.dt.from_np(v.dtype), kind="ExternalInput").ap()
           for n, v in arrays.items()}
    aps["out"] = nc.dram_tensor("out", [N_TOK, D], F32, kind="ExternalOutput").ap()
    build(nc, aps)
    r = run_bass_kernel_spmd(nc, [arrays], core_ids=[0])
    return np.asarray(r.results[0]["out"])
```
